# Optimizing a Trainium2 kernel written in Bass

```python
import numpy as np
import jax
import jax.numpy as jnp

def _softmax(x, axis=-1):
    return jax.nn.softmax(x, axis=axis)

def _gelu(x):
    return jax.nn.gelu(x, approximate=True)

def _silu(x):
    return jax.nn.silu(x)

def _sigmoid(x):
    return jax.nn.sigmoid(x)

def _layernorm(x, axis=-1, eps=1e-05):
    m = jnp.mean(x, axis=axis, keepdims=True)
    v = jnp.var(x, axis=axis, keepdims=True)
    return (x - m) / jnp.sqrt(v + eps)

def _scatter_add(tgt, idx, src, axis=0):
    return tgt.at[idx].add(src)

def _segment_sum(src, seg, n):
    return jax.ops.segment_sum(src, seg, n)
kernel_name = 'mk_decoder_preln_d1_seqx_r8_030039'

def setup_inputs(seed: int=0):
    np.random.seed(seed)
    _w = jnp.asarray

    def _rec_inputs():
        import jax
        import jax.numpy as jnp
        _rk = jax.random.key(seed)
        x = -0.0002928 + 1 * jax.random.normal(jax.random.fold_in(_rk, 1), (4, 512, 128), jnp.float32)
        _lenS = 512 - jax.random.randint(jax.random.fold_in(_rk, 7), (4,), 0, max(1, 512 // 4) + 1, jnp.int32)
        _lenS2 = 154 - jax.random.randint(jax.random.fold_in(_rk, 8), (4,), 0, max(1, 154 // 4) + 1, jnp.int32)
        _ctx_1024P = jax.random.normal(jax.random.fold_in(_rk, 11), (4, 16, 128), jnp.float32)
        _ctx_1024c = jax.random.dirichlet(jax.random.fold_in(_rk, 511), 0.3 * jnp.ones((16,), jnp.float32), (4, 154))
        _ctx_1024t = jnp.einsum('bsk,bkd->bsd', _ctx_1024c, _ctx_1024P)
        _ctx_1024t = _ctx_1024t * jax.lax.rsqrt(jnp.mean(jnp.square(_ctx_1024t)) + 1e-12) * 0.953939
        ctx_1024 = -1.39393e-06 + 0.999914 * (_ctx_1024t + 0.3 * jax.random.normal(jax.random.fold_in(_rk, 611), (4, 154, 128), jnp.float32))
        _validS = jnp.arange(512)[None, :] < _lenS[:, None]
        _validS2 = jnp.arange(154)[None, :] < _lenS2[:, None]
        _causal = jnp.tril(jnp.ones((512, 512), dtype=bool))
        mask_Bx1xSxS2_ik1 = jnp.where(jnp.broadcast_to(_validS2[:, None, None, :], (4, 1, 512, 154)), 1, 0).astype(jnp.int32)
        return (x, ctx_1024, mask_Bx1xSxS2_ik1)
    x, ctx_1024, mask_Bx1xSxS2_ik1 = _rec_inputs()

    def _L0_attn_setup():
        import jax, jax.numpy as jnp
        import numpy as np
        D = 128
        key = jax.random.key(seed)
        k0, k1, k2, k3 = jax.random.split(key, 4)
        x = jax.random.normal(k0, (4, 256, D), dtype=jnp.float32)
        Wk = jax.random.normal(k1, (D, D), dtype=jnp.float32) * 0.02
        Wq = jax.random.normal(k2, (D, D), dtype=jnp.float32) * 0.02
        Wv = jax.random.normal(k3, (D, D), dtype=jnp.float32) * 0.02
        return {'x': x, 'Wk': Wk, 'Wq': Wq, 'Wv': Wv}
    _L0_attn_all = _L0_attn_setup()
    _L0_attn_in = {k: v for k, v in _L0_attn_all.items() if k in ('Wk', 'Wq', 'Wv')}
    del _L0_attn_all

    def _L0_xattn_setup():
        import jax, jax.numpy as jnp
        import numpy as np
        D_MODEL = 128
        NUM_HEAD = 16
        D_K = D_MODEL // NUM_HEAD

        def _split_heads(x):
            b, s, _ = x.shape
            return x.reshape(b, s, NUM_HEAD, D_K).transpose(0, 2, 1, 3)
        key = jax.random.key(seed)
        ks = jax.random.split(key, 13)
        B, S = (2, 256)
        s = 1.0 / np.sqrt(D_MODEL)
        return {'q': jax.random.normal(ks[0], (B, S, D_MODEL), jnp.float32), 'k': jax.random.normal(ks[1], (B, S, D_MODEL), jnp.float32), 'v': jax.random.normal(ks[2], (B, S, D_MODEL), jnp.float32), 'mask': jax.random.randint(ks[3], (B, 1, S, S), 0, 2, jnp.int32), 'wq': jax.random.normal(ks[4], (D_MODEL, D_MODEL), jnp.float32) * s, 'bq': jax.random.normal(ks[5], (D_MODEL,), jnp.float32) * 0.02, 'wk': jax.random.normal(ks[6], (D_MODEL, D_MODEL), jnp.float32) * s, 'bk': jax.random.normal(ks[7], (D_MODEL,), jnp.float32) * 0.02, 'wv': jax.random.normal(ks[8], (D_MODEL, D_MODEL), jnp.float32) * s, 'bv': jax.random.normal(ks[9], (D_MODEL,), jnp.float32) * 0.02, 'wo': jax.random.normal(ks[10], (D_MODEL, D_MODEL), jnp.float32) * s, 'bo': jax.random.normal(ks[11], (D_MODEL,), jnp.float32) * 0.02}
    _L0_xattn_all = _L0_xattn_setup()
    _L0_xattn_in = {k: v for k, v in _L0_xattn_all.items() if k in ('wq', 'bq', 'wk', 'bk', 'wv', 'bv', 'wo', 'bo')}
    del _L0_xattn_all

    def _L0_ffn_setup():
        import jax, jax.numpy as jnp
        import numpy as np
        from math import sqrt
        B, S, D, H, E, K, FF = (2, 128, 128, 16, 8, 2, 512)
        HD = D // H
        EPS = 1e-05

        def _rope_cache(seq_len, hd):
            inv_freq = 1.0 / 10000.0 ** (jnp.arange(0, hd, 2, dtype=jnp.float32) / hd)
            t = jnp.arange(seq_len, dtype=jnp.float32)
            freqs = t[:, None] * inv_freq[None, :]
            emb = jnp.concatenate([freqs, freqs], axis=-1)
            return (jnp.cos(emb), jnp.sin(emb))

        def _rotate_half(x):
            x1, x2 = jnp.split(x, 2, axis=-1)
            return jnp.concatenate([-x2, x1], axis=-1)

        def _layernorm(x, g, b):
            m = jnp.mean(x, axis=-1, keepdims=True)
            v = jnp.var(x, axis=-1, keepdims=True)
            return (x - m) * jax.lax.rsqrt(v + EPS) * g + b

        def _forward(x, Wq, bq, Wk, bk, Wv, bv, Wo, bo, Wg, bg, W1, b1, W2, b2, g1, be1, g2, be2):
            bsz, seq, d = x.shape
            q = (x @ Wq + bq).reshape(bsz, seq, H, HD).transpose(0, 2, 1, 3)
            k = (x @ Wk + bk).reshape(bsz, seq, H, HD).transpose(0, 2, 1, 3)
            v = (x @ Wv + bv).reshape(bsz, seq, H, HD).transpose(0, 2, 1, 3)
            cos, sin = _rope_cache(seq, HD)
            cos = cos[None, None]
            sin = sin[None, None]
            q = q * cos + _rotate_half(q) * sin
            k = k * cos + _rotate_half(k) * sin
            scores = jnp.einsum('bhqd,bhkd->bhqk', q, k) / sqrt(HD)
            attn = jax.nn.softmax(scores, axis=-1)
            ao = jnp.einsum('bhqk,bhkd->bhqd', attn, v)
            ao = ao.transpose(0, 2, 1, 3).reshape(bsz, seq, d)
            attn_out = ao @ Wo + bo
            x1 = _layernorm(x + attn_out, g1, be1)
            gate_logits = x1 @ Wg + bg
            gate_probs = jax.nn.softmax(gate_logits, axis=-1)
            topk_p, topk_i = jax.lax.top_k(gate_probs, K)
            topk_p = topk_p / jnp.sum(topk_p, axis=-1, keepdims=True)
            comb = jnp.sum(jax.nn.one_hot(topk_i, E, dtype=x.dtype) * topk_p[..., None], axis=-2)
            h = jax.nn.gelu(jnp.einsum('bsd,edf->bsef', x1, W1) + b1, approximate=False)
            y = jnp.einsum('bsef,efd->bsed', h, W2) + b2
            moe_out = jnp.einsum('bse,bsed->bsd', comb, y)
            return _layernorm(x1 + moe_out, g2, be2)
        key = jax.random.key(seed)
        ks = jax.random.split(key, 20)
        std = 0.02
        p = lambda k, sh: jax.random.normal(k, sh, dtype=jnp.float32) * std
        return {'x': jax.random.normal(ks[0], (B, S, D), dtype=jnp.float32), 'Wq': p(ks[1], (D, D)), 'bq': jnp.zeros((D,), jnp.float32), 'Wk': p(ks[2], (D, D)), 'bk': jnp.zeros((D,), jnp.float32), 'Wv': p(ks[3], (D, D)), 'bv': jnp.zeros((D,), jnp.float32), 'Wo': p(ks[4], (D, D)), 'bo': jnp.zeros((D,), jnp.float32), 'Wg': p(ks[5], (D, E)), 'bg': jnp.zeros((E,), jnp.float32), 'W1': p(ks[6], (E, D, FF)), 'b1': jnp.zeros((E, FF), jnp.float32), 'W2': p(ks[7], (E, FF, D)), 'b2': jnp.zeros((E, D), jnp.float32), 'g1': jnp.ones((D,), jnp.float32), 'be1': jnp.zeros((D,), jnp.float32), 'g2': jnp.ones((D,), jnp.float32), 'be2': jnp.zeros((D,), jnp.float32)}
    _L0_ffn_all = _L0_ffn_setup()
    _L0_ffn_in = {k: v for k, v in _L0_ffn_all.items() if k in ('Wq', 'bq', 'Wk', 'bk', 'Wv', 'bv', 'Wo', 'bo', 'Wg', 'bg', 'W1', 'b1', 'W2', 'b2', 'g1', 'be1', 'g2', 'be2')}
    del _L0_ffn_all
    return {'x': x, 'ctx_1024': ctx_1024, 'mask_Bx1xSxS2_ik1': mask_Bx1xSxS2_ik1, 'L0_attn_Wk': _L0_attn_in['Wk'], 'L0_attn_Wq': _L0_attn_in['Wq'], 'L0_attn_Wv': _L0_attn_in['Wv'], 'L0_xattn_wq': _L0_xattn_in['wq'], 'L0_xattn_bq': _L0_xattn_in['bq'], 'L0_xattn_wk': _L0_xattn_in['wk'], 'L0_xattn_bk': _L0_xattn_in['bk'], 'L0_xattn_wv': _L0_xattn_in['wv'], 'L0_xattn_bv': _L0_xattn_in['bv'], 'L0_xattn_wo': _L0_xattn_in['wo'], 'L0_xattn_bo': _L0_xattn_in['bo'], 'L0_ffn_Wq': _L0_ffn_in['Wq'], 'L0_ffn_bq': _L0_ffn_in['bq'], 'L0_ffn_Wk': _L0_ffn_in['Wk'], 'L0_ffn_bk': _L0_ffn_in['bk'], 'L0_ffn_Wv': _L0_ffn_in['Wv'], 'L0_ffn_bv': _L0_ffn_in['bv'], 'L0_ffn_Wo': _L0_ffn_in['Wo'], 'L0_ffn_bo': _L0_ffn_in['bo'], 'L0_ffn_Wg': _L0_ffn_in['Wg'], 'L0_ffn_bg': _L0_ffn_in['bg'], 'L0_ffn_W1': _L0_ffn_in['W1'], 'L0_ffn_b1': _L0_ffn_in['b1'], 'L0_ffn_W2': _L0_ffn_in['W2'], 'L0_ffn_b2': _L0_ffn_in['b2'], 'L0_ffn_g1': _L0_ffn_in['g1'], 'L0_ffn_be1': _L0_ffn_in['be1'], 'L0_ffn_g2': _L0_ffn_in['g2'], 'L0_ffn_be2': _L0_ffn_in['be2']}

def reference(x, ctx_1024, mask_Bx1xSxS2_ik1, L0_attn_Wk, L0_attn_Wq, L0_attn_Wv, L0_xattn_wq, L0_xattn_bq, L0_xattn_wk, L0_xattn_bk, L0_xattn_wv, L0_xattn_bv, L0_xattn_wo, L0_xattn_bo, L0_ffn_Wq, L0_ffn_bq, L0_ffn_Wk, L0_ffn_bk, L0_ffn_Wv, L0_ffn_bv, L0_ffn_Wo, L0_ffn_bo, L0_ffn_Wg, L0_ffn_bg, L0_ffn_W1, L0_ffn_b1, L0_ffn_W2, L0_ffn_b2, L0_ffn_g1, L0_ffn_be1, L0_ffn_g2, L0_ffn_be2):
    import jax
    import jax.numpy as jnp

    def _L0_attn_ref(x, Wk, Wq, Wv):
        import jax, jax.numpy as jnp
        import numpy as np
        D = 128
        K = x @ Wk
        Q = x @ Wq
        V = x @ Wv
        N = Q.shape[-2]
        d = K.shape[-1]
        scores = jnp.einsum('bnd,bmd->bnm', Q, K) / jnp.sqrt(jnp.float32(d))
        causal = jnp.tril(jnp.ones((N, N), dtype=bool))
        scores = jnp.where(causal[None, :, :], scores, -jnp.inf)
        attn = jax.nn.softmax(scores, axis=-1)
        return attn @ V

    def _L0_xattn_ref(q, k, v, mask, wq, bq, wk, bk, wv, bv, wo, bo):
        import jax, jax.numpy as jnp
        import numpy as np
        D_MODEL = 128
        NUM_HEAD = 16
        D_K = D_MODEL // NUM_HEAD

        def _split_heads(x):
            b, s, _ = x.shape
            return x.reshape(b, s, NUM_HEAD, D_K).transpose(0, 2, 1, 3)
        query = _split_heads(q @ wq + bq)
        key = _split_heads(k @ wk + bk)
        value = _split_heads(v @ wv + bv)
        scale = 1.0 / np.sqrt(D_K).astype(np.float32)
        scores = jnp.einsum('bhqd,bhkd->bhqk', query, key) * scale
        scores = jnp.where(mask == 0, -jnp.inf, scores)
        attn = jax.nn.softmax(scores, axis=-1)
        out = jnp.einsum('bhqk,bhkd->bhqd', attn, value)
        b, h, s, d = out.shape
        out = out.transpose(0, 2, 1, 3).reshape(b, s, h * d)
        return out @ wo + bo

    def _L0_ffn_ref(x, Wq, bq, Wk, bk, Wv, bv, Wo, bo, Wg, bg, W1, b1, W2, b2, g1, be1, g2, be2):
        import jax, jax.numpy as jnp
        import numpy as np
        from math import sqrt
        B, S, D, H, E, K, FF = (2, 128, 128, 16, 8, 2, 512)
        HD = D // H
        EPS = 1e-05

        def _rope_cache(seq_len, hd):
            inv_freq = 1.0 / 10000.0 ** (jnp.arange(0, hd, 2, dtype=jnp.float32) / hd)
            t = jnp.arange(seq_len, dtype=jnp.float32)
            freqs = t[:, None] * inv_freq[None, :]
            emb = jnp.concatenate([freqs, freqs], axis=-1)
            return (jnp.cos(emb), jnp.sin(emb))

        def _rotate_half(x):
            x1, x2 = jnp.split(x, 2, axis=-1)
            return jnp.concatenate([-x2, x1], axis=-1)

        def _layernorm(x, g, b):
            m = jnp.mean(x, axis=-1, keepdims=True)
            v = jnp.var(x, axis=-1, keepdims=True)
            return (x - m) * jax.lax.rsqrt(v + EPS) * g + b

        def _forward(x, Wq, bq, Wk, bk, Wv, bv, Wo, bo, Wg, bg, W1, b1, W2, b2, g1, be1, g2, be2):
            bsz, seq, d = x.shape
            q = (x @ Wq + bq).reshape(bsz, seq, H, HD).transpose(0, 2, 1, 3)
            k = (x @ Wk + bk).reshape(bsz, seq, H, HD).transpose(0, 2, 1, 3)
            v = (x @ Wv + bv).reshape(bsz, seq, H, HD).transpose(0, 2, 1, 3)
            cos, sin = _rope_cache(seq, HD)
            cos = cos[None, None]
            sin = sin[None, None]
            q = q * cos + _rotate_half(q) * sin
            k = k * cos + _rotate_half(k) * sin
            scores = jnp.einsum('bhqd,bhkd->bhqk', q, k) / sqrt(HD)
            attn = jax.nn.softmax(scores, axis=-1)
            ao = jnp.einsum('bhqk,bhkd->bhqd', attn, v)
            ao = ao.transpose(0, 2, 1, 3).reshape(bsz, seq, d)
            attn_out = ao @ Wo + bo
            x1 = _layernorm(x + attn_out, g1, be1)
            gate_logits = x1 @ Wg + bg
            gate_probs = jax.nn.softmax(gate_logits, axis=-1)
            topk_p, topk_i = jax.lax.top_k(gate_probs, K)
            topk_p = topk_p / jnp.sum(topk_p, axis=-1, keepdims=True)
            comb = jnp.sum(jax.nn.one_hot(topk_i, E, dtype=x.dtype) * topk_p[..., None], axis=-2)
            h = jax.nn.gelu(jnp.einsum('bsd,edf->bsef', x1, W1) + b1, approximate=False)
            y = jnp.einsum('bsef,efd->bsed', h, W2) + b2
            moe_out = jnp.einsum('bse,bsed->bsd', comb, y)
            return _layernorm(x1 + moe_out, g2, be2)
        return _forward(x, Wq, bq, Wk, bk, Wv, bv, Wo, bo, Wg, bg, W1, b1, W2, b2, g1, be1, g2, be2)
    x = x + _L0_attn_ref(_layernorm(x, axis=-1), L0_attn_Wk, L0_attn_Wq, L0_attn_Wv)
    x = x + _L0_xattn_ref(_layernorm(x, axis=-1), ctx_1024, ctx_1024, mask_Bx1xSxS2_ik1, L0_xattn_wq, L0_xattn_bq, L0_xattn_wk, L0_xattn_bk, L0_xattn_wv, L0_xattn_bv, L0_xattn_wo, L0_xattn_bo)
    x = x + _L0_ffn_ref(_layernorm(x, axis=-1), L0_ffn_Wq, L0_ffn_bq, L0_ffn_Wk, L0_ffn_bk, L0_ffn_Wv, L0_ffn_bv, L0_ffn_Wo, L0_ffn_bo, L0_ffn_Wg, L0_ffn_bg, L0_ffn_W1, L0_ffn_b1, L0_ffn_W2, L0_ffn_b2, L0_ffn_g1, L0_ffn_be1, L0_ffn_g2, L0_ffn_be2)
    return x

_drawn_inputs = setup_inputs


def setup_inputs(seed=0):
    import zlib

    import numpy as np

    out = dict(_drawn_inputs(seed))
    spreads = {'L0_ffn_bq': (0.0, 0.8),
     'L0_ffn_bk': (0.0, 0.8),
     'L0_ffn_bv': (0.0, 0.646),
     'L0_ffn_bo': (0.0, 0.1),
     'L0_ffn_bg': (0.0, 0.379),
     'L0_ffn_b1': (0.0, 0.8),
     'L0_ffn_b2': (0.0, 0.1),
     'L0_ffn_g1': (1.0, 0.2),
     'L0_ffn_be1': (0.0, 0.1),
     'L0_ffn_g2': (1.0, 0.2),
     'L0_ffn_be2': (0.0, 0.1)}
    factors = {'L0_attn_Wk': 8.0,
     'L0_attn_Wq': 8.0,
     'L0_xattn_bq': 8.0,
     'L0_xattn_bk': 8.0,
     'L0_xattn_bo': 2.897,
     'L0_ffn_Wq': 8.0,
     'L0_ffn_Wk': 8.0,
     'L0_ffn_Wv': 5.103,
     'L0_ffn_Wo': 3.568,
     'L0_ffn_W1': 3.093,
     'L0_ffn_W2': 2.756}
    for name, (base, spread) in spreads.items():
        noise = np.random.default_rng([zlib.crc32(name.encode()), seed]).standard_normal(out[name].shape)
        drawn = base * np.exp(spread * noise) if base else spread * noise
        out[name] = jnp.asarray(drawn.astype(out[name].dtype))
    for name, factor in factors.items():
        out[name] = (out[name] * factor).astype(out[name].dtype)
    return out
```

```python
from contextlib import ExitStack

import numpy as np

import concourse.bass as bass
from concourse import mybir

F32 = mybir.dt.float32
F32R = mybir.dt.float32r
BF16 = mybir.dt.bfloat16
I32 = mybir.dt.int32
ALU = mybir.AluOpType
ACT = mybir.ActivationFunctionType
AX = mybir.AxisListType

P = 128
B = 4
S = 512
T = S // P
D = 128
H = 16
DH = D // H
HG = 4
G = H // HG
BLK = P // HG
KC = 154
KT0 = KC - P
NE = 8
FF = 512
FC = FF // P
NJ = NE * FC
EPS = 1e-5
NEG = -1e30
SCALE_A = float(1.0 / np.sqrt(np.float32(D)))
SCALE_H = float(1.0 / np.sqrt(np.float32(DH)))

ROW_B1 = 0
ROW_XBQ, ROW_XBK, ROW_FBQ, ROW_FBK, ROW_G1, ROW_BE1 = range(NJ, NJ + 6)
NROWS = NJ + 6
COL_FBQR, COL_FBKR = NROWS, NROWS + 1
VEC_XBV, VEC_XBO, VEC_FBV, VEC_FBO, VEC_G2, VEC_BE2 = range(6)


def shape_constants():
    eye = np.eye(P, dtype=np.float32)
    tri = np.where(np.arange(P)[None, :] > np.arange(P)[:, None], np.float32(NEG), np.float32(0))
    sel = np.zeros((4, P, G, P), np.float32)
    for which, slots in enumerate(((1, 2), (3,), (1, 3), (2,))):
        for g in range(G):
            for hh in range(HG):
                for j in slots:
                    for d in range(DH):
                        sel[which, (HG * g + hh) * DH + d, g, BLK * hh + DH * j + d] = 1
    rep = np.zeros((P, P), np.float32)
    for hh in range(HG):
        for k in range(KT0):
            rep[k, BLK * hh + k] = 1
    rot = np.zeros((P, P), np.float32)
    half = DH // 2
    for h in range(H):
        for d in range(half):
            rot[h * DH + half + d, h * DH + d] = -1
            rot[h * DH + d, h * DH + half + d] = 1
    inv = (1.0 / np.power(np.float32(10000.0), np.arange(0, DH, 2, dtype=np.float32) / np.float32(DH))).astype(np.float32)
    freqs = np.arange(S, dtype=np.float32)[:, None] * inv[None, :]
    emb = np.concatenate([freqs, freqs], axis=-1).astype(np.float32)
    cos = np.tile(np.cos(emb).T, (H, 1)).astype(np.float32)
    sin = np.tile(np.sin(emb).T, (H, 1)).astype(np.float32)
    misc = np.zeros((P, 64), np.float32)
    misc[:, 0:T] = -0.5
    misc[::BLK, 4] = 1.0
    misc[:, 8:8 + T * NE] = np.tile(NE - np.arange(NE), T)[None, :]
    return dict(eye=eye, tri=tri, sel=sel, rep=rep, rot=rot, cos=cos, sin=sin, misc=misc)


class Own:

    def __init__(self, eng, sem, per):
        self.eng, self.sem, self.per, self.base, self.n = eng, sem, per, 0, 0

    def start(self, b):
        assert self.n in (0, self.per), (self.n, self.per)
        self.base, self.n = b * self.per, 0

    def inc(self, ins):
        self.n += 1
        return ins.then_inc(self.sem, 1)

    def wait(self):
        if self.n:
            self.eng.wait_ge(self.sem, self.base + self.n)


def build(nc, x, ctx_in, mask, w, consts, comb_dram, out):
    stack = ExitStack()
    with stack:
        def sb(name, shape, dt=F32):
            return stack.enter_context(nc.sbuf_tensor(name, shape, dt))

        def sem(name):
            return stack.enter_context(nc.semaphore(name))

        eye = sb("eye", [P, P])
        eye_r = sb("eye_r", [P, P], F32R)
        eye_b = sb("eye_b", [P, P], BF16)
        tri = sb("tri", [P, P])
        tri_b = sb("tri_b", [P, P], BF16)
        sel_r = sb("sel_r", [P, 4, G, P], F32R)
        rep = sb("rep", [P, P])
        rep_b = sb("rep_b", [P, P], BF16)
        rot = sb("rot", [P, P])
        cos = sb("cos", [P, S])
        sin = sb("sin", [P, S])
        misc = sb("misc", [P, 64])
        exponent = misc[:, 0:T]
        ones_row = misc[:, 4:5]
        rank = misc[:, 8:8 + T * NE].rearrange("p (t e) -> p t e", t=T)
        wa = sb("wa", [P, 3, D])
        wx = sb("wx", [P, 4, D])
        wf = sb("wf", [P, 4, D])
        wfr = sb("wfr", [P, 2, D])
        wg = sb("wg", [P, NE])
        w1 = sb("w1", [P, NE, FF])
        w2 = sb("w2", [P, NJ, D])
        b2 = sb("b2", [NE, D])
        rows = sb("rows", [NROWS, P])
        cols = sb("cols", [P, NROWS + 2])
        vecs = sb("vecs", [P, 6, D])
        bg = sb("bg", [P, NE])

        xin = sb("xin", [P, T, D])
        ctx = sb("ctx", [P, 2, D])
        msk = sb("msk", [P, T, KC], I32)
        stats = sb("stats", [P, T, 6])
        lnw = sb("lnw", [P, 5, T])
        mean = sb("mean", [P, T])
        ve = sb("ve", [P, T])
        rstd = sb("rstd", [P, T])
        hat = sb("hat", [P, T, D])
        hat3 = sb("hat3", [P, T, D])
        hatT = sb("hatT", [P, S])
        kTa = sb("kTa", [P, S])
        qTa = sb("qTa", [P, S])
        va = sb("va", [P, T, D])
        nma = sb("nma", [P, T])
        nmas = sb("nmas", [P, T])
        rsa = sb("rsa", [P, T])
        ria = sb("ria", [P, T])
        xa = sb("xa", [P, T, D])
        xab = sb("xab", [P, T, D])
        ctxT = sb("ctxT", [P, KC])
        mb = sb("mb", [P, T, KC], BF16)
        mT = sb("mT", [P, S], BF16)
        mTt = sb("mTt", [BLK, S], BF16)
        khi = sb("khi", [P, S], F32R)
        klo = sb("klo", [P, S], F32R)
        qhi = sb("qhi", [P, S], F32R)
        qlo = sb("qlo", [P, S], F32R)
        kst = sb("kst", [P, G, S], F32R)
        ktail = sb("ktail", [P, G, P], F32R)
        qst = sb("qst", [P, G, S], F32R)
        q2st = sb("q2st", [P, G, S], F32R)
        nm = sb("nm", [P, T, G, P], F32R)
        vx = sb("vx", [P, H, BLK])
        vxt = sb("vxt", [P, G, P])
        px = sb("px", [P, 2, HG, S])
        pxt = sb("pxt", [P, 2, S])
        pa, pTa = px[:, 0], px[:, 1]
        rope_t, rope_f = px[:, 0], px[:, 1, 0:2]
        combB = px[:].rearrange("p a b s -> p (a b) s")
        ot = sb("ot", [P, G, S])
        sel = ot[:].rearrange("p w (g q) -> p w g q", g=G)
        rs = sb("rs", [P, T, H])
        on = sb("on", [P, T, D])
        onT = sb("onT", [P, S])
        x2 = sb("x2", [P, T, D])
        x2b = sb("x2b", [P, T, D])
        hat3b = sb("hat3b", [P, T, D])
        vf = sb("vf", [P, T, H, BLK])
        r1 = sb("r1", [P, T, D])
        x1T = sb("x1T", [P, S])
        gt = sb("gt", [P, 10, T, NE])
        gs = sb("gs", [P, 8, T])
        comb = sb("comb", [P, T, NE])
        combT = sb("combT", [NE, S])
        hT = sb("hT", [P, 2, S])
        hc = sb("hc", [P, 2, S])
        rT = sb("rT", [P, S])
        outb = sb("outb", [P, T, D])

        bank = [stack.enter_context(nc.psum_tensor(f"bank{i}", [P, 512], F32)) for i in range(8)]

        k = {name: sem(name) for name in (
            "loaded", "casts", "zeroed", "rows_turned", "bias_cols", "rot_cols", "setup_done",
            "x_loaded", "ctx_loaded", "mask_loaded", 
            "ln_var", "ln_rstd", "ln_hat", "ln_turned", "ln_T",
            "a_proj", "a_k", "a_q", "a_v", "a_scores", "a_max", "a_probs", "a_turned", "a_probsT",
            "a_out", "a_done",
            "c_turned", "ctxT_ready", "mb_ready", "m_turned", "mT_ready", "x_proj", "x_khi", "x_klo",
            "x_v", "x_kst_mm", "x_kst", "x_ktail", "x_qproj", "x_qhi", "x_qlo", "x_qst_mm", "x_qst",
            "x_s1", "x_max", "x_q2_mm", "x_q2", "x_s2", "x_exp", "x_st", "x_expt", "x_av",
            "ot_ready", "o_turned", "on_ready", "on_turned", "onT_ready", "o_proj", "xab_ready",
            "b_done",
            "f_proj", "f_rope", "f_full", "f_hi", "f_lo", "f_v", "f_st_mm", "f_st", "f_s1", "f_max",
            "f_q2_mm", "f_q2", "f_s2", "f_exp", "f_av", "f_ot", "hat3b_ready", "r1_ready",
            "g_logits", "g_shift", "g_exp", "g_comb", "g_turned", "combT_ready", "comb_stored", "comb_loaded",
            "h_ready", "h_act", "h_scaled", "y_part", "rT_ready", "r_turned", "x2b_ready",
            "out_ready", "out_stored",
            "pe_own", "act_own", "dve_own",
        )}

        block = stack.enter_context(nc.Block())

        LN = 5

        @block.sync
        def _(sp):
            loads = [
                (eye[:], consts["eye"]), (tri[:], consts["tri"]),
                (sel, consts["sel"].rearrange("w p g q -> p w g q")),
                (rep[:], consts["rep"]), (rot[:], consts["rot"]),
                (cos[:], consts["cos"]), (sin[:], consts["sin"]), (misc[:], consts["misc"]),
                (wa[:, 0, :], w["L0_attn_Wk"]), (wa[:, 1, :], w["L0_attn_Wq"]), (wa[:, 2, :], w["L0_attn_Wv"]),
                (wx[:, 0, :], w["L0_xattn_wq"]), (wx[:, 1, :], w["L0_xattn_wk"]),
                (wx[:, 2, :], w["L0_xattn_wv"]), (wx[:, 3, :], w["L0_xattn_wo"]),
                (wf[:, 0, :], w["L0_ffn_Wq"]), (wf[:, 1, :], w["L0_ffn_Wk"]),
                (wf[:, 2, :], w["L0_ffn_Wv"]), (wf[:, 3, :], w["L0_ffn_Wo"]),
                (wg[:], w["L0_ffn_Wg"]), (b2[:], w["L0_ffn_b2"]),
                (rows[ROW_B1:NJ, :], w["L0_ffn_b1"].rearrange("e (c p) -> (e c) p", p=P)),
            ]
            for r, n in ((ROW_XBQ, "L0_xattn_bq"), (ROW_XBK, "L0_xattn_bk"), (ROW_FBQ, "L0_ffn_bq"),
                         (ROW_FBK, "L0_ffn_bk"), (ROW_G1, "L0_ffn_g1"), (ROW_BE1, "L0_ffn_be1")):
                loads.append((rows[r:r + 1, :], w[n].rearrange("(a d) -> a d", a=1)))
            for v, n in ((VEC_XBV, "L0_xattn_bv"), (VEC_XBO, "L0_xattn_bo"), (VEC_FBV, "L0_ffn_bv"),
                         (VEC_FBO, "L0_ffn_bo"), (VEC_G2, "L0_ffn_g2"), (VEC_BE2, "L0_ffn_be2")):
                loads.append((vecs[:, v, :], w[n].partition_broadcast(P)))
            loads.append((bg[:], w["L0_ffn_bg"].partition_broadcast(P)))
            loads += [
                (w1[:], w["L0_ffn_W1"].rearrange("e d f -> d e f")),
                (w2[:], w["L0_ffn_W2"].rearrange("e (c p) d -> p (e c) d", p=P)),
            ]
            assert len(loads) == N_LOADS

            def load_x(b):
                sp.dma_start(xin[:], x[bass.ds(b, 1)].rearrange("b (t p) d -> p (b t) d", p=P)).then_inc(k["x_loaded"], 16)

            def load_ctx(b):
                sp.dma_start(ctx[:, 0, :], ctx_in[bass.ds(b, 1), 0:P, :].rearrange("b k d -> (b k) d")).then_inc(k["ctx_loaded"], 16)
                sp.dma_start(ctx[0:KT0, 1, :], ctx_in[bass.ds(b, 1), P:KC, :].rearrange("b k d -> (b k) d")).then_inc(k["ctx_loaded"], 16)

            def load_mask(b):
                sp.dma_start(msk[:], mask[bass.ds(b, 1)].rearrange("b o (t p) k -> p (b o t) k", p=P)).then_inc(k["mask_loaded"], 16)

            load_x(0)
            load_ctx(0)
            load_mask(0)
            for dst, src in loads:
                sp.dma_start(dst, src).then_inc(k["loaded"], 16)

            def results(b):
                sp.wait_ge(k["combT_ready"], b + 1)
                sp.dma_start(comb_dram, combT[:]).then_inc(k["comb_stored"], 16)
                sp.wait_ge(k["comb_stored"], b * 16 + 16)
                sp.dma_start(combB.rearrange("p e s -> p (e s)"),
                             comb_dram.rearrange("e s -> (e s)").partition_broadcast(P)).then_inc(k["comb_loaded"], 16)
                sp.wait_ge(k["out_ready"], b + 1)
                sp.dma_start(out[bass.ds(b, 1)].rearrange("b (t p) d -> p (b t) d", p=P), outb[:]).then_inc(k["out_stored"], 16)

            with sp.Fori(0, B - 1) as b:
                sp.wait_ge(k["a_done"], b + 1)
                load_x(b + 1)
                sp.wait_ge(k["c_turned"], b + 1)
                load_ctx(b + 1)
                sp.wait_ge(k["mb_ready"], b + 1)
                load_mask(b + 1)
                results(b)
            results(B - 1)
            sp.wait_ge(k["out_stored"], 16 * B)

        @block.gpsimd
        def _(pool):
            for tile in (ktail, nm):
                pool.memset(tile[:].bitcast(F32), 0.0).then_inc(k["zeroed"], 1)
            for tile in (vx, vxt, vf):
                pool.memset(tile[:], 0.0).then_inc(k["zeroed"], 1)
            pool.memset(mTt[:], 0.0).then_inc(k["zeroed"], 1)
            pool.wait_ge(k["zeroed"], 6)
            pool.memset(vx[:, :, DH:DH + 1], 1.0).then_inc(k["zeroed"], 1)
            pool.memset(vf[:, :, :, DH:DH + 1], 1.0).then_inc(k["zeroed"], 1)
            pool.wait_ge(k["loaded"], 16 * N_LOADS)

            def rstd_of(b, n):
                pool.wait_ge(k["ln_var"], b * LN + n + 1)
                pool.tensor_tensor(rstd[:], ve[:], exponent, ALU.pow).then_inc(k["ln_rstd"], 1)

            with pool.Fori(0, B) as b:
                rstd_of(b, 0)
                pool.wait_ge(k["a_done"], b + 1)
                pool.tensor_tensor(xab[:], xa[:], vecs[:, VEC_XBO, :].unsqueeze(1).to_broadcast([P, T, D]), ALU.add).then_inc(k["xab_ready"], 1)
                rstd_of(b, 1)
                rstd_of(b, 2)
                pool.tensor_tensor(x2b[:], x2[:], vecs[:, VEC_BE2, :].unsqueeze(1).to_broadcast([P, T, D]), ALU.add).then_inc(k["x2b_ready"], 1)
                pool.wait_ge(k["ln_hat"], b * LN + 3)
                pool.tensor_tensor(hat3b[:], hat3[:], vecs[:, VEC_FBO, :].unsqueeze(1).to_broadcast([P, T, D]), ALU.add).then_inc(k["hat3b_ready"], 1)
                for i, lo in ((0, qlo), (1, klo)):
                    pool.wait_ge(k["f_rope"], 2 * (2 * b + i + 1))
                    pool.tensor_tensor(rope_f[:, i, :], rope_t[:, 2 * i, :], rope_t[:, 2 * i + 1, :], ALU.add).then_inc(k["f_full"], 1)
                    pool.wait_ge(k["f_hi"], 2 * b + i + 1)
                    pool.tensor_tensor(lo[:], rope_f[:, i, :], (qhi, khi)[i][:], ALU.subtract).then_inc(k["f_lo"], 1)
                rstd_of(b, 3)
                pool.wait_ge(k["comb_loaded"], b * 16 + 16)
                for j in range(NJ):
                    pool.wait_ge(k["h_act"], b * NJ + j + 1)
                    if j >= 2:
                        pool.wait_ge(k["y_part"], b * NJ + j - 1)
                    pool.tensor_tensor(hc[:, j % 2, :], hT[:, j % 2, :], combB[:, j // FC, :], ALU.mult).then_inc(k["h_scaled"], 1)
                rstd_of(b, 4)

        @block.scalar
        def _(act):
            own = Own(act, k["act_own"], ACT_STEPS)
            act.wait_ge(k["setup_done"], 1)

            def ln_evac(b, n):
                act.wait_ge(k["ln_turned"], b * (LN - 1) + n + 1)
                if n == 3:
                    act.activation(x1T[:], bank[0][:], ACT.Identity, bias=cols[:, ROW_BE1:ROW_BE1 + 1],
                                   scale=cols[:, ROW_G1:ROW_G1 + 1]).then_inc(k["ln_T"], 1)
                else:
                    act.activation(hatT[:], bank[0][:], ACT.Copy).then_inc(k["ln_T"], 1)

            def attention_out(b, n):
                act.wait_ge(k["on_turned"], 2 * b + n + 1)
                act.activation(onT[:], bank[0][:], ACT.Copy).then_inc(k["onT_ready"], 1)

            with act.Fori(0, B) as b:
                own.start(b)
                ln_evac(b, 0)
                act.wait_ge(k["a_proj"], 3 * b + 1)
                act.activation(kTa[:], bank[1][:], ACT.Copy).then_inc(k["a_k"], 1)
                act.wait_ge(k["a_proj"], 3 * b + 3)
                act.activation(va[:].rearrange("p t d -> p (t d)"), bank[3][:], ACT.Copy).then_inc(k["a_v"], 1)
                for t in range(T):
                    act.wait_ge(k["a_max"], T * b + t + 1)
                    n = (t + 1) * P
                    act.activation(pa[:, t, 0:n], bank[4 + t][:, 0:n], ACT.Exp, bias=nmas[:, t:t + 1],
                                   scale=SCALE_A, accum_out=rsa[:, t:t + 1]).then_inc(k["a_probs"], 1)
                for t in range(T):
                    act.wait_ge(k["a_turned"], T * b + t + 1)
                    n = (t + 1) * P
                    act.activation(pTa[:, t, 0:n], bank[t][:, 0:n], ACT.Copy).then_inc(k["a_probsT"], 1)
                act.wait_ge(k["c_turned"], b + 1)
                act.activation(ctxT[:], bank[5][:, 0:KC], ACT.Copy).then_inc(k["ctxT_ready"], 1)
                act.wait_ge(k["m_turned"], b + 1)
                own.inc(act.activation(mT[:], bank[6][:].bitcast(BF16)[:, 0:S], ACT.Copy))
                act.activation(mTt[0:KT0, :], bank[7][0:KT0, :].bitcast(BF16)[:, 0:S], ACT.Copy).then_inc(k["mT_ready"], 1)
                act.wait_ge(k["x_proj"], 3 * b + 1)
                act.activation(khi[:, 0:KC], bank[1][:, 0:KC], ACT.Identity,
                               bias=cols[:, ROW_XBK:ROW_XBK + 1]).then_inc(k["x_khi"], 1)
                for i in range(2):
                    act.wait_ge(k["x_kst_mm"], 2 * b + i + 1)
                    act.activation(kst[:, 2 * i:2 * i + 2, 0:KC],
                                   bank[5 + i][:, 0:2 * KC].rearrange("p (g k) -> p g k", g=2),
                                   ACT.Identity, bias=ones_row).then_inc(k["x_kst"], 1)
                ln_evac(b, 1)
                act.wait_ge(k["x_qproj"], b + 1)
                act.activation(qhi[:], bank[4][:], ACT.Identity, bias=cols[:, ROW_XBQ:ROW_XBQ + 1]).then_inc(k["x_qhi"], 1)
                for i, g in enumerate((0, 2)):
                    act.wait_ge(k["x_qst_mm"], G * b + g + 1)
                    act.activation(qst[:, g, :], bank[g][:], ACT.Copy).then_inc(k["x_qst"], 1)
                for g in range(G):
                    act.wait_ge(k["x_q2_mm"], G * b + g + 1)
                    act.activation(q2st[:, g, :], bank[g][:], ACT.Copy).then_inc(k["x_q2"], 1)
                for g in range(G):
                    if g >= 2:
                        act.wait_ge(k["x_av"], G * b + g - 1)
                    for i in range(HG):
                        act.wait_ge(k["x_s2"], H * b + HG * g + i + 1)
                        act.activation(px[:, g % 2, i, :], bank[4 + i][:], ACT.Exp, scale=SCALE_H).then_inc(k["x_exp"], 1)
                    act.wait_ge(k["x_st"], G * b + g + 1)
                    act.activation(pxt[:, g % 2, :], bank[2 * (g % 2)][:], ACT.Exp, scale=SCALE_H).then_inc(k["x_expt"], 1)
                attention_out(b, 0)
                ln_evac(b, 2)
                for i, hi in ((0, qhi), (1, khi)):
                    act.wait_ge(k["f_full"], 2 * b + i + 1)
                    act.activation(hi[:], rope_f[:, i, :], ACT.Copy).then_inc(k["f_hi"], 1)
                for i in range(G):
                    act.wait_ge(k["f_st_mm"], 2 * G * b + 2 * i + 2)
                    act.activation(kst[:, i, :], bank[4 + i][:], ACT.Identity, bias=ones_row).then_inc(k["f_st"], 1)
                act.wait_ge(k["f_q2_mm"], G * b + 1)
                act.activation(q2st[:, 0, :], bank[slot_q2(0)][:], ACT.Copy).then_inc(k["f_q2"], 1)
                for g in range(G):
                    for c in range(T):
                        for i in range(2):
                            n = (g * T + c) * 2 + i
                            act.wait_ge(k["f_s2"], 2 * T * G * b + n + 1)
                            if g * T + c >= 2:
                                act.wait_ge(k["f_av"], T * G * b + g * T + c - 1)
                            for q in range(2):
                                ins = act.activation(px[:, c % 2, 2 * i + q, :], bank[4 + 2 * i + q][:],
                                                     ACT.Exp, scale=SCALE_H)
                                ins.then_inc(k["f_exp"], 1)
                    act.wait_ge(k["f_av"], T * G * b + (g + 1) * T)
                    act.activation(ot[:, g, :], bank[3][:], ACT.Copy).then_inc(k["f_ot"], 1)
                    if g + 1 < G:
                        act.wait_ge(k["f_q2_mm"], G * b + g + 2)
                        act.activation(q2st[:, g + 1, :], bank[slot_q2(g + 1)][:], ACT.Copy).then_inc(k["f_q2"], 1)
                attention_out(b, 1)
                ln_evac(b, 3)
                act.wait_ge(k["g_shift"], b + 1)
                act.activation(gt[:, 1].rearrange("p t e -> p (t e)"), gt[:, 0].rearrange("p t e -> p (t e)"),
                               ACT.Exp).then_inc(k["g_exp"], 1)
                for j in range(NJ):
                    act.wait_ge(k["h_ready"], NJ * b + j + 1)
                    if j >= 2:
                        act.wait_ge(k["h_scaled"], NJ * b + j - 1)
                    act.activation(hT[:, j % 2, :], bank[4 + j % 2][:], ACT.Gelu,
                                   bias=cols[:, ROW_B1 + j:ROW_B1 + j + 1]).then_inc(k["h_act"], 1)
                assert own.n == ACT_STEPS

        @block.vector
        def _(dve):
            own = Own(dve, k["dve_own"], DVE_STEPS)
            dve.wait_ge(k["loaded"], 16 * N_LOADS)
            for dst, src in ((eye_r, eye[:]), (eye_b, eye[:]), (tri_b, tri[:]), (sel_r, sel), (rep_b, rep[:])):
                dve.tensor_copy(dst[:], src).then_inc(k["casts"], 1)
            half = DH // 2
            for i in range(2):
                src = wf[:, i, :].rearrange("p (h d) -> p h d", d=DH)
                dst = wfr[:, i, :].rearrange("p (h d) -> p h d", d=DH)
                dve.tensor_scalar(dst[:, :, 0:half], src[:, :, half:DH], -1.0, None, ALU.mult).then_inc(k["casts"], 1)
                dve.tensor_copy(dst[:, :, half:DH], src[:, :, 0:half]).then_inc(k["casts"], 1)
            dve.wait_ge(k["rows_turned"], 1)
            dve.tensor_copy(cols[:, 0:NROWS], bank[0][:, 0:NROWS]).then_inc(k["bias_cols"], 1)
            dve.wait_ge(k["rot_cols"], 1)
            dve.wait_ge(k["zeroed"], 8)
            for hh in range(HG):
                p0 = BLK * hh
                dve.memset(vxt[p0:p0 + KT0, :, p0 + DH:p0 + DH + 1], 1.0).then_inc(k["casts"], 1)
            dve.wait_ge(k["casts"], 13)
            dve.tensor_copy(cols[:, COL_FBQR:COL_FBKR + 1], bank[1][:, 0:2]).then_inc(k["setup_done"], 1)
            dve.wait_ge(k["setup_done"], 1)

            def layer_norm(b, n, src, dst):
                for t in range(T):
                    own.inc(dve.bn_stats(stats[:, t, :], src[:, t, :]))
                own.wait()
                own.inc(dve.tensor_tensor(lnw[:, 0, :], stats[:, :, 1], stats[:, :, 4], ALU.add))
                own.inc(dve.tensor_tensor(lnw[:, 1, :], stats[:, :, 1], stats[:, :, 4], ALU.subtract))
                own.inc(dve.tensor_tensor(lnw[:, 2, :], stats[:, :, 2], stats[:, :, 5], ALU.add))
                own.wait()
                own.inc(dve.tensor_tensor(lnw[:, 3, :], lnw[:, 1, :], lnw[:, 1, :], ALU.mult))
                own.inc(dve.tensor_scalar(lnw[:, 4, :], lnw[:, 2, :], 1.0 / D, EPS, ALU.mult, ALU.add))
                own.inc(dve.tensor_scalar(mean[:], lnw[:, 0, :], 0.5, None, ALU.mult))
                own.wait()
                dve.scalar_tensor_tensor(ve[:], lnw[:, 3, :], 0.25, lnw[:, 4, :], ALU.mult, ALU.add).then_inc(k["ln_var"], 1)
                dve.wait_ge(k["ln_rstd"], b * LN + n + 1)
                for t in range(T):
                    ins = dve.tensor_scalar(dst[:, t, :], src[:, t, :], mean[:, t:t + 1], rstd[:, t:t + 1],
                                            ALU.subtract, ALU.mult)
                ins.then_inc(k["ln_hat"], 1)

            def bc(v):
                return vecs[:, v, :].unsqueeze(1).to_broadcast([P, T, D])

            def normalise_heads(b, n):
                for t in range(T):
                    dve.wait_ge(k["o_turned"], T * (2 * b + n) + t + 1)
                    heads = bank[4 + t][:].rearrange("p (h c) -> p h c", c=BLK)
                    own.inc(dve.reciprocal(rs[:, t, :].unsqueeze(2), heads[:, :, DH:DH + 1]))
                    own.wait()
                    dve.tensor_tensor(on[:, t, :].rearrange("p (h d) -> p h d", d=DH), heads[:, :, 0:DH],
                                      rs[:, t, :].unsqueeze(2).to_broadcast([P, H, DH]), ALU.mult).then_inc(k["on_ready"], 1)

            with dve.Fori(0, B) as b:
                own.start(b)
                dve.wait_ge(k["x_loaded"], 16 * b + 16)
                layer_norm(b, 0, xin, hat)
                dve.wait_ge(k["a_proj"], 3 * b + 2)
                dve.tensor_copy(qTa[:], bank[2][:]).then_inc(k["a_q"], 1)
                for t in range(T):
                    dve.wait_ge(k["a_scores"], T * b + t + 1)
                    own.inc(dve.tensor_reduce(nma[:, t:t + 1], bank[4 + t][:, 0:(t + 1) * P], AX.X, ALU.max, negate=True))
                    own.wait()
                    dve.tensor_scalar(nmas[:, t:t + 1], nma[:, t:t + 1], SCALE_A, None, ALU.mult).then_inc(k["a_max"], 1)
                dve.wait_ge(k["mask_loaded"], 16 * b + 16)
                dve.tensor_scalar(mb[:], msk[:], 0.0, NEG, ALU.is_equal, ALU.mult).then_inc(k["mb_ready"], 1)
                dve.wait_ge(k["a_probs"], T * b + T)
                own.inc(dve.reciprocal(ria[:], rsa[:]))
                own.wait()
                dve.wait_ge(k["a_out"], b + 1)
                for t in range(T):
                    ins = dve.scalar_tensor_tensor(xa[:, t, :], bank[4][:, t * D:(t + 1) * D], ria[:, t:t + 1],
                                                   xin[:, t, :], ALU.mult, ALU.add)
                ins.then_inc(k["a_done"], 1)
                dve.wait_ge(k["x_khi"], b + 1)
                dve.scalar_tensor_tensor(klo[:, 0:KC], bank[1][:, 0:KC], cols[:, ROW_XBK:ROW_XBK + 1],
                                         khi[:, 0:KC], ALU.add, ALU.subtract).then_inc(k["x_klo"], 1)
                dve.wait_ge(k["x_proj"], 3 * b + 3)
                dve.tensor_tensor(vx[:, :, 0:DH], bank[2][:, 0:D].rearrange("p (h d) -> p h d", d=DH),
                                  vecs[:, VEC_XBV, :].rearrange("p (h d) -> p h d", d=DH), ALU.add).then_inc(k["x_v"], 1)
                for hh in range(HG):
                    p0 = BLK * hh
                    dve.tensor_tensor(
                        vxt[p0:p0 + KT0, :, p0:p0 + DH],
                        bank[3][p0:p0 + KT0, 0:G * DH].rearrange("p (g d) -> p g d", d=DH),
                        vecs[p0:p0 + KT0, VEC_XBV, :].rearrange("p (g c) -> p g c", g=G)[:, :, hh * DH:(hh + 1) * DH],
                        ALU.add).then_inc(k["x_v"], 1)
                dve.wait_ge(k["x_kst"], 2 * b + 2)
                for hh in range(HG):
                    p0 = BLK * hh
                    dve.tensor_copy(ktail[p0:p0 + BLK, :, p0:p0 + KT0], kst[p0:p0 + BLK, :, P:KC]).then_inc(k["x_ktail"], 1)
                dve.wait_ge(k["a_done"], b + 1)
                layer_norm(b, 1, xa, hat)
                dve.wait_ge(k["x_qhi"], b + 1)
                dve.scalar_tensor_tensor(qlo[:], bank[4][:], cols[:, ROW_XBQ:ROW_XBQ + 1], qhi[:],
                                         ALU.add, ALU.subtract).then_inc(k["x_qlo"], 1)
                for g in (1, 3):
                    dve.wait_ge(k["x_qst_mm"], G * b + g + 1)
                    dve.tensor_copy(qst[:, g, :], bank[g if g < 3 else 7][:]).then_inc(k["x_qst"], 1)
                for t in range(T):
                    for hh in range(HG):
                        dve.wait_ge(k["x_s1"], H * b + HG * t + hh + 1)
                        for i in range(2):
                            ins = dve.tensor_reduce(
                                nm[:, t, 2 * i:2 * i + 2, BLK * hh],
                                bank[2 * hh + i][:, 0:2 * KC].rearrange("p (g k) -> p g k", g=2),
                                AX.X, ALU.max, negate=True)
                        ins.then_inc(k["x_max"], 1)
                for g in range(G):
                    dve.wait_ge(k["x_av"], G * b + g + 1)
                    dve.tensor_copy(ot[:, g, :], bank[1 + 2 * (g % 2)][:]).then_inc(k["ot_ready"], 1)
                normalise_heads(b, 0)
                dve.wait_ge(k["xab_ready"], b + 1)
                dve.wait_ge(k["o_proj"], 2 * b + 1)
                own.inc(dve.tensor_tensor(x2[:].rearrange("p t d -> p (t d)"), bank[1][:],
                                          xab[:].rearrange("p t d -> p (t d)"), ALU.add))
                own.wait()
                layer_norm(b, 2, x2, hat3)
                for i in range(2):
                    dve.wait_ge(k["f_proj"], 5 * b + 2 * i + 2)
                    dve.scalar_tensor_tensor(rope_t[:, 2 * i, :], bank[2 + 2 * i][:], cols[:, ROW_FBQ + i:ROW_FBQ + i + 1],
                                             cos[:], ALU.add, ALU.mult).then_inc(k["f_rope"], 1)
                    dve.scalar_tensor_tensor(rope_t[:, 2 * i + 1, :], bank[3 + 2 * i][:], cols[:, COL_FBQR + i:COL_FBQR + i + 1],
                                             sin[:], ALU.add, ALU.mult).then_inc(k["f_rope"], 1)
                dve.wait_ge(k["f_proj"], 5 * b + 5)
                dve.tensor_tensor(vf[:].rearrange("p t h c -> p (t h) c")[:, :, 0:DH],
                                  bank[6][:].rearrange("p (n d) -> p n d", d=DH),
                                  vecs[:, VEC_FBV, :].unsqueeze(1).to_broadcast([P, T, D]).rearrange("p t (h d) -> p t h d", d=DH),
                                  ALU.add).then_inc(k["f_v"], 1)
                for g in range(G):
                    dve.wait_ge(k["f_st_mm"], 2 * G * b + 2 * g + 1)
                    dve.tensor_copy(qst[:, g, :], bank[g][:]).then_inc(k["f_st"], 1)
                for g in range(G):
                    for t in range(T):
                        for hh in range(HG):
                            dve.wait_ge(k["f_s1"], H * T * b + (g * T + t) * HG + hh + 1)
                            dve.tensor_reduce(nm[:, t, g, BLK * hh:BLK * hh + 1], bank[slot_s1(g, t, hh)][:],
                                              AX.X, ALU.max, negate=True).then_inc(k["f_max"], 1)
                normalise_heads(b, 1)
                dve.wait_ge(k["hat3b_ready"], b + 1)
                dve.wait_ge(k["o_proj"], 2 * b + 2)
                own.inc(dve.tensor_tensor(r1[:].rearrange("p t d -> p (t d)"), bank[1][:],
                                          hat3b[:].rearrange("p t d -> p (t d)"), ALU.add))
                own.wait()
                layer_norm(b, 3, r1, hat)
                flat = lambda i: gt[:, i]
                per_token = lambda i: gs[:, i, :].unsqueeze(2).to_broadcast([P, T, NE])
                dve.wait_ge(k["g_logits"], b + 1)
                own.inc(dve.tensor_tensor(flat(2), bank[3][:, 0:T * NE].rearrange("p (t e) -> p t e", e=NE),
                                          bg[:].unsqueeze(1).to_broadcast([P, T, NE]), ALU.add))
                own.wait()
                own.inc(dve.reduce_max(gs[:, 0, :], flat(2), AX.X))
                own.wait()
                dve.tensor_tensor(flat(0), flat(2), per_token(0), ALU.subtract).then_inc(k["g_shift"], 1)
                dve.wait_ge(k["g_exp"], b + 1)
                left = 1
                for i in range(2):
                    m, r, eq, hit = 1 + 2 * i, 2 + 2 * i, 3 + 3 * i, 4 + 3 * i
                    own.inc(dve.reduce_max(gs[:, m, :], flat(left), AX.X))
                    own.wait()
                    own.inc(dve.tensor_tensor(flat(eq), flat(left), per_token(m), ALU.is_equal))
                    own.wait()
                    own.inc(dve.tensor_tensor(flat(5 + i * 4), flat(eq), rank, ALU.mult))
                    own.wait()
                    own.inc(dve.reduce_max(gs[:, r, :], flat(5 + i * 4), AX.X))
                    own.wait()
                    own.inc(dve.tensor_tensor(flat(hit), flat(5 + i * 4), per_token(r), ALU.is_equal))
                    own.wait()
                    if i == 0:
                        own.inc(dve.scalar_tensor_tensor(flat(8), flat(hit), -4.0, flat(1), ALU.mult, ALU.add))
                        own.wait()
                        left = 8
                own.inc(dve.tensor_tensor(flat(2), flat(4), flat(7), ALU.add))
                own.inc(dve.tensor_tensor(gs[:, 5, :], gs[:, 1, :], gs[:, 3, :], ALU.add))
                own.wait()
                own.inc(dve.tensor_tensor(flat(3), flat(2), flat(1), ALU.mult))
                own.inc(dve.reciprocal(gs[:, 6, :], gs[:, 5, :]))
                own.wait()
                dve.tensor_tensor(comb[:], flat(3), per_token(6), ALU.mult).then_inc(k["g_comb"], 1)
                dve.wait_ge(k["g_turned"], b + 1)
                dve.tensor_copy(combT[:], bank[1][0:NE, :]).then_inc(k["combT_ready"], 1)
                dve.wait_ge(k["y_part"], NJ * b + NJ)
                dve.tensor_tensor(rT[:], bank[6][:], x1T[:], ALU.add).then_inc(k["rT_ready"], 1)
                dve.wait_ge(k["r_turned"], b + 1)
                layer_norm(b, 4, bank[7][:].rearrange("p (t d) -> p t d", t=T), r1)
                dve.wait_ge(k["ln_hat"], b * LN + 5)
                own.inc(dve.tensor_tensor(hat[:], r1[:], bc(VEC_G2), ALU.mult))
                own.wait()
                dve.wait_ge(k["x2b_ready"], b + 1)
                dve.tensor_tensor(outb[:], hat[:], x2b[:], ALU.add).then_inc(k["out_ready"], 1)
                assert own.n == DVE_STEPS, own.n

        @block.tensor
        def _(pe):
            pe.wait_ge(k["loaded"], 16 * N_LOADS)
            pe.transpose(bank[0][:, 0:NROWS], rows[:], eye[0:NROWS, 0:NROWS]).then_inc(k["rows_turned"], 1)
            pe.wait_ge(k["bias_cols"], 1)
            for i in range(2):
                ins = pe.matmul(bank[1][:, i:i + 1], rot[:], cols[:, ROW_FBQ + i:ROW_FBQ + i + 1], start=True, stop=True)
            ins.then_inc(k["rot_cols"], 1)
            pe.wait_ge(k["setup_done"], 1)

            def turn_rows(b, n, src):
                pe.wait_ge(k["ln_hat"], b * LN + n + 1)
                for t in range(T):
                    ins = pe.transpose(bank[0][:, t * P:(t + 1) * P], src[:, t, :], eye[:])
                ins.then_inc(k["ln_turned"], 1)
                pe.wait_ge(k["ln_T"], b * (LN - 1) + n + 1)

            def attention_out(b, n, wo):
                for t in range(T):
                    for g in range(G):
                        ins = pe.transpose(bank[4 + t][:, g * P:(g + 1) * P], ot[:, g, t * P:(t + 1) * P], eye[:])
                    ins.then_inc(k["o_turned"], 1)
                for t in range(T):
                    pe.wait_ge(k["on_ready"], T * (2 * b + n) + t + 1)
                    ins = pe.transpose(bank[0][:, t * P:(t + 1) * P], on[:, t, :], eye[:])
                ins.then_inc(k["on_turned"], 1)
                pe.wait_ge(k["onT_ready"], 2 * b + n + 1)
                for t in range(T):
                    ins = pe.matmul(bank[1][:, t * D:(t + 1) * D], onT[:, t * P:(t + 1) * P], wo, start=True, stop=True)
                ins.then_inc(k["o_proj"], 1)

            def blk(hh):
                return slice(BLK * hh, BLK * (hh + 1))

            with pe.Fori(0, B) as b:
                turn_rows(b, 0, hat)
                pe.matmul(bank[1][:], wa[:, 0, :], hatT[:], start=True, stop=True).then_inc(k["a_proj"], 1)
                pe.matmul(bank[2][:], wa[:, 1, :], hatT[:], start=True, stop=True).then_inc(k["a_proj"], 1)
                for t in range(T):
                    ins = pe.matmul(bank[3][:, t * D:(t + 1) * D], hatT[:, t * P:(t + 1) * P], wa[:, 2, :], start=True, stop=True)
                ins.then_inc(k["a_proj"], 1)
                pe.wait_ge(k["a_k"], b + 1)
                pe.wait_ge(k["a_q"], b + 1)
                for t in range(T):
                    n = (t + 1) * P
                    pe.matmul(bank[4 + t][:, 0:n], qTa[:, t * P:(t + 1) * P], kTa[:, 0:n], start=True, stop=True)
                    pe.matmul(bank[4 + t][:, t * P:n], eye_b[:], tri_b[:], start=False, stop=True,
                              skip_group_check=True).then_inc(k["a_scores"], 1)
                pe.wait_ge(k["a_v"], b + 1)
                for t in range(T):
                    pe.wait_ge(k["a_probs"], T * b + t + 1)
                    for c in range(t + 1):
                        ins = pe.transpose(bank[t][:, c * P:(c + 1) * P], pa[:, t, c * P:(c + 1) * P], eye[:])
                    ins.then_inc(k["a_turned"], 1)
                for t in range(T):
                    pe.wait_ge(k["a_probsT"], T * b + t + 1)
                    for c in range(t + 1):
                        ins = pe.matmul(bank[4][:, t * D:(t + 1) * D], pTa[:, t, c * P:(c + 1) * P], va[:, c, :],
                                        start=(c == 0), stop=(c == t))
                ins.then_inc(k["a_out"], 1)

                pe.wait_ge(k["ctx_loaded"], 32 * b + 32)
                pe.transpose(bank[5][:, 0:P], ctx[:, 0, :], eye[:])
                pe.transpose(bank[5][:, P:KC], ctx[0:KT0, 1, :], eye[0:KT0, 0:KT0]).then_inc(k["c_turned"], 1)
                pe.wait_ge(k["mb_ready"], b + 1)
                for t in range(T):
                    pe.transpose(bank[6][:].bitcast(BF16)[:, t * P:(t + 1) * P], mb[:, t, 0:P], eye_b[:])
                    ins = pe.transpose(bank[7][0:KT0, :].bitcast(BF16)[:, t * P:(t + 1) * P], mb[:, t, P:KC], eye_b[:])
                ins.then_inc(k["m_turned"], 1)
                pe.wait_ge(k["ctxT_ready"], b + 1)
                pe.matmul(bank[1][:, 0:KC], wx[:, 1, :], ctxT[:], start=True, stop=True).then_inc(k["x_proj"], 1)
                pe.matmul(bank[2][:, 0:D], ctxT[:, 0:P], wx[:, 2, :], start=True, stop=True).then_inc(k["x_proj"], 1)
                for hh in range(HG):
                    ins = pe.matmul(bank[3][BLK * hh:BLK * hh + KT0, 0:G * DH], ctxT[:, P:KC],
                                    wx[:, 2, :].rearrange("p (g c) -> p g c", g=G)[:, :, hh * DH:(hh + 1) * DH],
                                    start=True, stop=True)
                ins.then_inc(k["x_proj"], 1)
                pe.wait_ge(k["x_klo"], b + 1)
                pe.wait_ge(k["mT_ready"], b + 1)
                for g in range(G):
                    dst = bank[5 + g // 2][:, (g % 2) * KC:(g % 2 + 1) * KC]
                    pe.matmul(dst, sel_r[:, 2, g, :], khi[:, 0:KC], start=True, stop=False)
                    ins = pe.matmul(dst, sel_r[:, 3, g, :], klo[:, 0:KC], start=False, stop=True)
                    if g % 2:
                        ins.then_inc(k["x_kst_mm"], 1)
                turn_rows(b, 1, hat)
                pe.matmul(bank[4][:], wx[:, 0, :], hatT[:], start=True, stop=True).then_inc(k["x_qproj"], 1)
                pe.wait_ge(k["x_qlo"], b + 1)
                for g in range(G):
                    dst = bank[g if g < 3 else 7][:]
                    pe.matmul(dst, sel_r[:, 0, g, :], qhi[:], start=True, stop=False)
                    pe.matmul(dst, sel_r[:, 1, g, :], qlo[:], start=False, stop=True).then_inc(k["x_qst_mm"], 1)
                pe.wait_ge(k["x_qst"], G * b + G)
                pe.wait_ge(k["x_ktail"], HG * b + HG)
                for t in range(T):
                    for hh in range(HG):
                        if t:
                            pe.wait_ge(k["x_max"], H * b + HG * (t - 1) + hh + 1)
                        for i in range(2):
                            pe.matmul(bank[2 * hh + i][:, 0:2 * KC], eye_b[:],
                                      mb[:, t, :].unsqueeze(1).to_broadcast([P, 2, KC]), start=True, stop=True,
                                      skip_group_check=True)
                        for g in range(G):
                            ins = pe.matmul(bank[2 * hh + g // 2][:, (g % 2) * KC:(g % 2 + 1) * KC],
                                            qst[blk(hh), g, t * P:(t + 1) * P], kst[blk(hh), g, 0:KC],
                                            start=False, stop=True, skip_group_check=True)
                        ins.then_inc(k["x_s1"], 1)
                pe.wait_ge(k["x_max"], H * b + H)
                for g in range(G):
                    pe.matmul(bank[g][:], sel_r[:, 0, g, :], qhi[:], start=True, stop=False, skip_group_check=True)
                    pe.matmul(bank[g][:], sel_r[:, 1, g, :], qlo[:], start=False, stop=False, skip_group_check=True)
                    for t in range(T):
                        ins = pe.matmul(bank[g][:, t * P:(t + 1) * P], nm[:, t, g, :], eye_r[:], start=False,
                                        stop=(t == T - 1), skip_group_check=True)
                    ins.then_inc(k["x_q2_mm"], 1)

                def x_sums(g):
                    acc = bank[1 + 2 * (g % 2)]
                    pe.wait_ge(k["x_exp"], H * b + HG * (g + 1))
                    pe.wait_ge(k["x_expt"], G * b + g + 1)
                    if g >= 2:
                        pe.wait_ge(k["ot_ready"], G * b + g - 1)
                    for hh in range(HG):
                        pe.matmul(acc[blk(hh), :], vx[:, HG * g + hh, :], px[:, g % 2, hh, :], start=True,
                                  stop=False, skip_group_check=True)
                    pe.matmul(acc[:], vxt[:, g, :], pxt[:, g % 2, :], start=False, stop=True,
                              skip_group_check=True).then_inc(k["x_av"], 1)

                for g in range(G):
                    if g == 0:
                        pe.wait_ge(k["x_q2"], G * b + G)
                    for hh in range(HG):
                        if g:
                            pe.wait_ge(k["x_exp"], H * b + HG * (g - 1) + hh + 1)
                        pe.matmul(bank[4 + hh][:], eye_b[:], mT[:], start=True, stop=False, skip_group_check=True)
                        pe.matmul(bank[4 + hh][:], kst[blk(hh), g, 0:P], q2st[blk(hh), g, :], start=False,
                                  stop=True, skip_group_check=True).then_inc(k["x_s2"], 1)
                    if g >= 2:
                        pe.wait_ge(k["x_expt"], G * b + g - 1)
                    tail = bank[2 * (g % 2)]
                    pe.matmul(tail[:], rep_b[0:BLK, :], mTt[:], start=True, stop=False, skip_group_check=True)
                    pe.matmul(tail[:], ktail[:, g, :], q2st[:, g, :], start=False, stop=True,
                              skip_group_check=True).then_inc(k["x_st"], 1)
                    if g:
                        x_sums(g - 1)
                x_sums(G - 1)
                pe.wait_ge(k["ot_ready"], G * b + G)
                attention_out(b, 0, wx[:, 3, :])

                turn_rows(b, 2, hat3)
                for i in range(2):
                    pe.matmul(bank[2 + 2 * i][:], wf[:, i, :], hatT[:], start=True, stop=True).then_inc(k["f_proj"], 1)
                    pe.matmul(bank[3 + 2 * i][:], wfr[:, i, :], hatT[:], start=True, stop=True).then_inc(k["f_proj"], 1)
                for t in range(T):
                    ins = pe.matmul(bank[6][:, t * D:(t + 1) * D], hatT[:, t * P:(t + 1) * P], wf[:, 2, :], start=True, stop=True)
                ins.then_inc(k["f_proj"], 1)
                pe.wait_ge(k["f_v"], b + 1)
                pe.wait_ge(k["f_lo"], 2 * b + 2)
                for g in range(G):
                    pe.matmul(bank[g][:], sel_r[:, 0, g, :], qhi[:], start=True, stop=False)
                    pe.matmul(bank[g][:], sel_r[:, 1, g, :], qlo[:], start=False, stop=True).then_inc(k["f_st_mm"], 1)
                    pe.matmul(bank[4 + g][:], sel_r[:, 2, g, :], khi[:], start=True, stop=False)
                    pe.matmul(bank[4 + g][:], sel_r[:, 3, g, :], klo[:], start=False, stop=True).then_inc(k["f_st_mm"], 1)
                pe.wait_ge(k["f_st"], 2 * G * b + 2 * G)

                def wait_slot(c):
                    c -= RING
                    if c < 0:
                        return
                    g, i = divmod(c, H + 1)
                    if i == H:
                        pe.wait_ge(k["f_q2"], G * b + g + 1)
                    else:
                        pe.wait_ge(k["f_max"], H * T * b + g * H + i + 1)

                def s1(g, t, hh):
                    wait_slot(g * (H + 1) + t * HG + hh)
                    pe.matmul(bank[slot_s1(g, t, hh)][:], qst[blk(hh), g, t * P:(t + 1) * P], kst[blk(hh), g, :],
                              start=True, stop=True).then_inc(k["f_s1"], 1)

                def q2(g):
                    wait_slot(g * (H + 1) + H)
                    pe.wait_ge(k["f_max"], H * T * b + (g + 1) * H)
                    dst = bank[slot_q2(g)]
                    pe.matmul(dst[:], sel_r[:, 0, g, :], qhi[:], start=True, stop=False, skip_group_check=True)
                    pe.matmul(dst[:], sel_r[:, 1, g, :], qlo[:], start=False, stop=False, skip_group_check=True)
                    for t in range(T):
                        ins = pe.matmul(dst[:, t * P:(t + 1) * P], nm[:, t, g, :], eye_r[:], start=False,
                                        stop=(t == T - 1), skip_group_check=True)
                    ins.then_inc(k["f_q2_mm"], 1)

                def s2(g, c, i):
                    n = (g * T + c) * 2 + i
                    if n >= 2:
                        pe.wait_ge(k["f_exp"], H * T * b + 2 * (n - 1))
                    for q in range(2):
                        hh = 2 * i + q
                        ins = pe.matmul(bank[4 + hh][:], kst[blk(hh), g, c * P:(c + 1) * P], q2st[blk(hh), g, :],
                                        start=True, stop=True)
                    ins.then_inc(k["f_s2"], 1)

                def sums_of(g, c):
                    pe.wait_ge(k["f_exp"], H * T * b + (g * T + c + 1) * HG)
                    if c == 0 and g:
                        pe.wait_ge(k["f_ot"], G * b + g)
                    for hh in range(HG):
                        ins = pe.matmul(bank[3][blk(hh), :], vf[:, c, HG * g + hh, :], px[:, c % 2, hh, :],
                                        start=(c == 0), stop=(c == T - 1), skip_group_check=True)
                    ins.then_inc(k["f_av"], 1)

                for t in range(T):
                    for hh in range(HG):
                        s1(0, t, hh)
                q2(0)
                for g in range(G):
                    pe.wait_ge(k["f_q2"], G * b + g + 1)
                    for c in range(T):
                        for i in range(2):
                            s2(g, c, i)
                            if g + 1 < G:
                                s1(g + 1, c, 2 * i)
                                s1(g + 1, c, 2 * i + 1)
                        if c:
                            sums_of(g, c - 1)
                    sums_of(g, T - 1)
                    if g + 1 < G:
                        q2(g + 1)
                pe.wait_ge(k["f_ot"], G * b + G)
                attention_out(b, 1, wf[:, 3, :])

                turn_rows(b, 3, hat)
                for t in range(T):
                    ins = pe.matmul(bank[3][:, t * NE:(t + 1) * NE], x1T[:, t * P:(t + 1) * P], wg[:], start=True, stop=True)
                ins.then_inc(k["g_logits"], 1)
                pe.wait_ge(k["g_comb"], b + 1)
                for t in range(T):
                    ins = pe.transpose(bank[1][0:NE, t * P:(t + 1) * P], comb[:, t, :], eye[:])
                ins.then_inc(k["g_turned"], 1)

                def up(j):
                    if j >= 2:
                        pe.wait_ge(k["h_act"], NJ * b + j - 1)
                    e, c = divmod(j, FC)
                    pe.matmul(bank[4 + j % 2][:], w1[:, e, c * P:(c + 1) * P], x1T[:], start=True, stop=True).then_inc(k["h_ready"], 1)

                def down(j):
                    pe.wait_ge(k["h_scaled"], NJ * b + j + 1)
                    pe.matmul(bank[6][:], w2[:, j, :], hc[:, j % 2, :], start=False, stop=(j == NJ - 1),
                              skip_group_check=True).then_inc(k["y_part"], 1)

                up(0)
                up(1)
                pe.wait_ge(k["combT_ready"], b + 1)
                pe.matmul(bank[6][:], b2[:], combT[:], start=True, stop=False, skip_group_check=True)
                for j in range(2, NJ):
                    up(j)
                    down(j - 2)
                down(NJ - 2)
                pe.wait_ge(k["h_scaled"], NJ * b + NJ)
                j = NJ - 1
                pe.matmul(bank[6][:], w2[:, j, :], hc[:, j % 2, :], start=False, stop=True,
                          skip_group_check=True).then_inc(k["y_part"], 1)
                pe.wait_ge(k["rT_ready"], b + 1)
                for t in range(T):
                    ins = pe.transpose(bank[7][:, t * P:(t + 1) * P], rT[:, t * P:(t + 1) * P], eye[:])
                ins.then_inc(k["r_turned"], 1)


RING = 3
N_LOADS = 22 + 6 + 7 + 2
ACT_STEPS = 1
DVE_STEPS = 83


def slot_s1(g, t, hh):
    return (g * (H + 1) + t * HG + hh) % RING


def slot_q2(g):
    return (g * (H + 1) + H) % RING


_WEIGHTS = [
    "L0_attn_Wk", "L0_attn_Wq", "L0_attn_Wv", "L0_xattn_wq", "L0_xattn_bq", "L0_xattn_wk", "L0_xattn_bk",
    "L0_xattn_wv", "L0_xattn_bv", "L0_xattn_wo", "L0_xattn_bo", "L0_ffn_Wq", "L0_ffn_bq", "L0_ffn_Wk",
    "L0_ffn_bk", "L0_ffn_Wv", "L0_ffn_bv", "L0_ffn_Wo", "L0_ffn_bo", "L0_ffn_Wg", "L0_ffn_bg", "L0_ffn_W1",
    "L0_ffn_b1", "L0_ffn_W2", "L0_ffn_b2", "L0_ffn_g1", "L0_ffn_be1", "L0_ffn_g2", "L0_ffn_be2",
]


def kernel(**inputs):
    import concourse.bacc as _bacc
    from concourse import mybir as _mybir
    from concourse.bass_utils import run_bass_kernel_spmd as _run

    nc = _bacc.Bacc("TRN2", target_bir_lowering=False, num_devices=1)
    arrays = {}

    def given(name, a):
        a = np.ascontiguousarray(a)
        arrays[f"in_{name}"] = a
        return nc.dram_tensor(f"in_{name}", a.shape, _mybir.dt.from_np(a.dtype), kind="ExternalInput").ap()

    x = given("x", inputs["x"])
    ctx = given("ctx_1024", inputs["ctx_1024"])
    mask = given("mask", inputs["mask_Bx1xSxS2_ik1"])
    w = {n: given(n, inputs[n]) for n in _WEIGHTS}
    consts = {n: given(f"const_{n}", a) for n, a in shape_constants().items()}
    comb = nc.dram_tensor("gate_weights", (NE, S), F32, kind="Internal").ap()
    out = nc.dram_tensor("out_0", (B, S, D), F32, kind="ExternalOutput").ap()
    build(nc, x, ctx, mask, w, consts, comb, out)
    r = _run(nc, [arrays], core_ids=[0])
    return r.results[0]["out_0"]
```

```python
from contextlib import ExitStack

import numpy as np

import concourse.bass as bass
from concourse import mybir

F32 = mybir.dt.float32
F32R = mybir.dt.float32r
BF16 = mybir.dt.bfloat16
I32 = mybir.dt.int32
ALU = mybir.AluOpType
ACT = mybir.ActivationFunctionType
AX = mybir.AxisListType

P = 128
B = 4
S = 512
T = S // P
D = 128
H = 16
DH = D // H
HG = 4
G = H // HG
BLK = P // HG
KC = 154
KT0 = KC - P
NE = 8
FF = 512
FC = FF // P
NJ = NE * FC
Y_BANKS = (6, 7, 2, 3, 1, 0)
EPS = 1e-5
NEG = -1e30
SCALE_A = float(1.0 / np.sqrt(np.float32(D)))
SCALE_H = float(1.0 / np.sqrt(np.float32(DH)))

ROW_B1 = 0
ROW_XBQ, ROW_XBK, ROW_FBQ, ROW_FBK, ROW_G1, ROW_BE1 = range(NJ, NJ + 6)
NROWS = NJ + 6
COL_FBQR, COL_FBKR = NROWS, NROWS + 1
VEC_XBV, VEC_XBO, VEC_FBV, VEC_FBO, VEC_G2, VEC_BE2 = range(6)


def shape_constants():
    eye = np.eye(P, dtype=np.float32)
    tri = np.where(np.arange(P)[None, :] > np.arange(P)[:, None], np.float32(NEG), np.float32(0))
    sel = np.zeros((4, P, G, P), np.float32)
    for which, slots in enumerate(((1, 2), (3,), (1, 3), (2,))):
        for g in range(G):
            for hh in range(HG):
                for j in slots:
                    for d in range(DH):
                        sel[which, (HG * g + hh) * DH + d, g, BLK * hh + DH * j + d] = 1
    rep = np.zeros((P, P), np.float32)
    for hh in range(HG):
        for k in range(KT0):
            rep[k, BLK * hh + k] = 1
    rot = np.zeros((P, P), np.float32)
    half = DH // 2
    for h in range(H):
        for d in range(half):
            rot[h * DH + half + d, h * DH + d] = -1
            rot[h * DH + d, h * DH + half + d] = 1
    inv = (1.0 / np.power(np.float32(10000.0), np.arange(0, DH, 2, dtype=np.float32) / np.float32(DH))).astype(np.float32)
    freqs = np.arange(S, dtype=np.float32)[:, None] * inv[None, :]
    emb = np.concatenate([freqs, freqs], axis=-1).astype(np.float32)
    cos = np.tile(np.cos(emb).T, (H, 1)).astype(np.float32)
    sin = np.tile(np.sin(emb).T, (H, 1)).astype(np.float32)
    misc = np.zeros((P, 64), np.float32)
    misc[:, 0:T] = -0.5
    misc[::BLK, 4] = 1.0
    misc[:, 8:8 + T * NE] = np.tile(NE - np.arange(NE), T)[None, :]
    return dict(eye=eye, tri=tri, sel=sel, rep=rep, rot=rot, cos=cos, sin=sin, misc=misc)


class Own:

    def __init__(self, eng, sem, per):
        self.eng, self.sem, self.per, self.base, self.n = eng, sem, per, 0, 0

    def start(self, b):
        assert self.n in (0, self.per), (self.n, self.per)
        self.base, self.n = b * self.per, 0

    def inc(self, ins):
        self.n += 1
        return ins.then_inc(self.sem, 1)

    def wait(self):
        if self.n:
            self.eng.wait_ge(self.sem, self.base + self.n)


def build(nc, x, ctx_in, mask, w, consts, comb_dram, out):
    stack = ExitStack()
    with stack:
        def sb(name, shape, dt=F32):
            return stack.enter_context(nc.sbuf_tensor(name, shape, dt))

        def sem(name):
            return stack.enter_context(nc.semaphore(name))

        eye = sb("eye", [P, P])
        eye_r = sb("eye_r", [P, P], F32R)
        eye_b = sb("eye_b", [P, P], BF16)
        tri = sb("tri", [P, P])
        tri_b = sb("tri_b", [P, P], BF16)
        sel_r = sb("sel_r", [P, 4, G, P], F32R)
        rep = sb("rep", [P, P])
        rep_b = sb("rep_b", [P, P], BF16)
        rot = sb("rot", [P, P])
        cos = sb("cos", [P, S])
        sin = sb("sin", [P, S])
        misc = sb("misc", [P, 64])
        exponent = misc[:, 0:T]
        ones_row = misc[:, 4:5]
        rank = misc[:, 8:8 + T * NE].rearrange("p (t e) -> p t e", t=T)
        wa = sb("wa", [P, 3, D])
        wx = sb("wx", [P, 4, D])
        wf = sb("wf", [P, 4, D])
        wfr = sb("wfr", [P, 2, D])
        wg = sb("wg", [P, NE])
        w1 = sb("w1", [P, NE, FF])
        w2 = sb("w2", [P, NJ, D])
        b2 = sb("b2", [NE, D])
        rows = sb("rows", [NROWS, P])
        cols = sb("cols", [P, NROWS + 2])
        vecs = sb("vecs", [P, 6, D])
        bg = sb("bg", [P, NE])

        xin = sb("xin", [P, T, D])
        ctx = sb("ctx", [P, 2, D])
        msk = sb("msk", [P, T, KC], I32)
        stats = sb("stats", [P, T, 6])
        lnw = sb("lnw", [P, 5, T])
        mean = sb("mean", [P, T])
        ve = sb("ve", [P, T])
        rstd = sb("rstd", [P, T])
        hat = sb("hat", [P, T, D])
        hat3 = sb("hat3", [P, T, D])
        hatT = sb("hatT", [P, S])
        kTa = sb("kTa", [P, S])
        qTa = sb("qTa", [P, S])
        va = sb("va", [P, T, D])
        nma = sb("nma", [P, T])
        nmas = sb("nmas", [P, T])
        rsa = sb("rsa", [P, T])
        ria = sb("ria", [P, T])
        xa = sb("xa", [P, T, D])
        xab = sb("xab", [P, T, D])
        ctxT = sb("ctxT", [P, KC])
        mb = sb("mb", [P, T, KC], BF16)
        mT = sb("mT", [P, S], BF16)
        mTt = sb("mTt", [BLK, S], BF16)
        khi = sb("khi", [P, S], F32R)
        klo = sb("klo", [P, S], F32R)
        qhi = sb("qhi", [P, S], F32R)
        qlo = sb("qlo", [P, S], F32R)
        kst = sb("kst", [P, G, S], F32R)
        ktail = sb("ktail", [P, G, P], F32R)
        qst = sb("qst", [P, G, S], F32R)
        q2st = sb("q2st", [P, G, S], F32R)
        nm = sb("nm", [P, T, G, P], F32R)
        vx = sb("vx", [P, H, BLK])
        vxt = sb("vxt", [P, G, P])
        px = sb("px", [P, 2, HG, S])
        pxt = sb("pxt", [P, 2, S])
        pa, pTa = px[:, 0], px[:, 1]
        rope_t, rope_f = px[:, 0], px[:, 1, 0:2]
        combB = px[:].rearrange("p a b s -> p (a b) s")
        ot = sb("ot", [P, G, S])
        sel = ot[:].rearrange("p w (g q) -> p w g q", g=G)
        rs = sb("rs", [P, T, H])
        on = sb("on", [P, T, D])
        onT = sb("onT", [P, S])
        x2 = sb("x2", [P, T, D])
        x2b = sb("x2b", [P, T, D])
        hat3b = sb("hat3b", [P, T, D])
        vf = sb("vf", [P, T, H, BLK])
        r1 = sb("r1", [P, T, D])
        x1T = sb("x1T", [P, S])
        gt = sb("gt", [P, 10, T, NE])
        gs = sb("gs", [P, 8, T])
        comb = sb("comb", [P, T, NE])
        combT = sb("combT", [NE, S])
        hT = sb("hT", [P, 2, S])
        hhi = sb("hhi", [P, 2, S], F32R)
        rT = sb("rT", [P, S])
        wsp = [t[:].rearrange("p (m r) s -> p m r s", r=2) for t in (qst, q2st)]
        x1hi, x1lo = qhi, qlo
        hlo = [khi, klo]
        ys = [onT, hatT]
        outb = sb("outb", [P, T, D])

        bank = [stack.enter_context(nc.psum_tensor(f"bank{i}", [P, 512], F32)) for i in range(8)]

        k = {name: sem(name) for name in (
            "loaded", "casts", "zeroed", "rows_turned", "bias_cols", "rot_cols", "setup_done",
            "x_loaded", "ctx_loaded", "mask_loaded", 
            "ln_var", "ln_rstd", "ln_hat", "ln_turned", "ln_T",
            "a_proj", "a_k", "a_q", "a_v", "a_scores", "a_max", "a_probs", "a_turned", "a_probsT",
            "a_out", "a_done",
            "c_turned", "ctxT_ready", "mb_ready", "m_turned", "mT_ready", "x_proj", "x_khi", "x_klo",
            "x_v", "x_kst_mm", "x_kst", "x_ktail", "x_qproj", "x_qhi", "x_qlo", "x_qst_mm", "x_qst",
            "x_s1", "x_max", "x_q2_mm", "x_q2", "x_s2", "x_exp", "x_st", "x_expt", "x_av",
            "ot_ready", "o_turned", "on_ready", "on_turned", "onT_ready", "o_proj", "xab_ready",
            "b_done",
            "f_proj", "f_rope", "f_full", "f_hi", "f_lo", "f_v", "f_st_mm", "f_qst0", "f_st", "f_s1", "f_max",
            "f_q2_mm", "f_q2", "f_s2", "f_exp", "f_av", "f_ot", "hat3b_ready", "r1_ready",
            "g_logits", "g_shift", "g_exp", "g_comb", "g_turned", "combT_ready", "comb_stored", "comb_loaded",
            "x1_split", "w_hi", "w_lo", "h_ready", "h_act", "h_hi", "h_lo", "y_part", "y_scaled", "b2_mm",
            "rT_begun", "rT_added", "r_turned", "x2b_ready",
            "out_ready", "out_stored",
            "pe_own", "act_own", "dve_own",
        )}

        def w_of(e, i):
            return w2[:, FC * e:FC * (e + 1), :].rearrange("p c d -> p (c d)") if i else w1[:, e, :]

        block = stack.enter_context(nc.Block())

        LN = 5

        @block.sync
        def _(sp):
            loads = [
                (eye[:], consts["eye"]), (tri[:], consts["tri"]),
                (sel, consts["sel"].rearrange("w p g q -> p w g q")),
                (rep[:], consts["rep"]), (rot[:], consts["rot"]),
                (cos[:], consts["cos"]), (sin[:], consts["sin"]), (misc[:], consts["misc"]),
                (wa[:, 0, :], w["L0_attn_Wk"]), (wa[:, 1, :], w["L0_attn_Wq"]), (wa[:, 2, :], w["L0_attn_Wv"]),
                (wx[:, 0, :], w["L0_xattn_wq"]), (wx[:, 1, :], w["L0_xattn_wk"]),
                (wx[:, 2, :], w["L0_xattn_wv"]), (wx[:, 3, :], w["L0_xattn_wo"]),
                (wf[:, 0, :], w["L0_ffn_Wq"]), (wf[:, 1, :], w["L0_ffn_Wk"]),
                (wf[:, 2, :], w["L0_ffn_Wv"]), (wf[:, 3, :], w["L0_ffn_Wo"]),
                (wg[:], w["L0_ffn_Wg"]), (b2[:], w["L0_ffn_b2"]),
                (rows[ROW_B1:NJ, :], w["L0_ffn_b1"].rearrange("e (c p) -> (e c) p", p=P)),
            ]
            for r, n in ((ROW_XBQ, "L0_xattn_bq"), (ROW_XBK, "L0_xattn_bk"), (ROW_FBQ, "L0_ffn_bq"),
                         (ROW_FBK, "L0_ffn_bk"), (ROW_G1, "L0_ffn_g1"), (ROW_BE1, "L0_ffn_be1")):
                loads.append((rows[r:r + 1, :], w[n].rearrange("(a d) -> a d", a=1)))
            for v, n in ((VEC_XBV, "L0_xattn_bv"), (VEC_XBO, "L0_xattn_bo"), (VEC_FBV, "L0_ffn_bv"),
                         (VEC_FBO, "L0_ffn_bo"), (VEC_G2, "L0_ffn_g2"), (VEC_BE2, "L0_ffn_be2")):
                loads.append((vecs[:, v, :], w[n].partition_broadcast(P)))
            loads.append((bg[:], w["L0_ffn_bg"].partition_broadcast(P)))
            loads += [
                (w1[:], w["L0_ffn_W1"].rearrange("e d f -> d e f")),
                (w2[:], w["L0_ffn_W2"].rearrange("e (c p) d -> p (e c) d", p=P)),
            ]
            assert len(loads) == N_LOADS

            def load_x(b):
                sp.dma_start(xin[:], x[bass.ds(b, 1)].rearrange("b (t p) d -> p (b t) d", p=P)).then_inc(k["x_loaded"], 16)

            def load_ctx(b):
                sp.dma_start(ctx[:, 0, :], ctx_in[bass.ds(b, 1), 0:P, :].rearrange("b k d -> (b k) d")).then_inc(k["ctx_loaded"], 16)
                sp.dma_start(ctx[0:KT0, 1, :], ctx_in[bass.ds(b, 1), P:KC, :].rearrange("b k d -> (b k) d")).then_inc(k["ctx_loaded"], 16)

            def load_mask(b):
                sp.dma_start(msk[:], mask[bass.ds(b, 1)].rearrange("b o (t p) k -> p (b o t) k", p=P)).then_inc(k["mask_loaded"], 16)

            load_x(0)
            load_ctx(0)
            load_mask(0)
            for dst, src in loads:
                sp.dma_start(dst, src).then_inc(k["loaded"], 16)

            def results(b):
                sp.wait_ge(k["combT_ready"], b + 1)
                sp.dma_start(comb_dram, combT[:]).then_inc(k["comb_stored"], 16)
                sp.wait_ge(k["comb_stored"], b * 16 + 16)
                sp.dma_start(combB.rearrange("p e s -> p (e s)"),
                             comb_dram.rearrange("e s -> (e s)").partition_broadcast(P)).then_inc(k["comb_loaded"], 16)
                sp.wait_ge(k["out_ready"], b + 1)
                sp.dma_start(out[bass.ds(b, 1)].rearrange("b (t p) d -> p (b t) d", p=P), outb[:]).then_inc(k["out_stored"], 16)

            with sp.Fori(0, B - 1) as b:
                sp.wait_ge(k["a_done"], b + 1)
                load_x(b + 1)
                sp.wait_ge(k["c_turned"], b + 1)
                load_ctx(b + 1)
                sp.wait_ge(k["mb_ready"], b + 1)
                load_mask(b + 1)
                results(b)
            results(B - 1)
            sp.wait_ge(k["out_stored"], 16 * B)

        @block.gpsimd
        def _(pool):
            for tile in (ktail, nm):
                pool.memset(tile[:].bitcast(F32), 0.0).then_inc(k["zeroed"], 1)
            for tile in (vx, vxt, vf):
                pool.memset(tile[:], 0.0).then_inc(k["zeroed"], 1)
            pool.memset(mTt[:], 0.0).then_inc(k["zeroed"], 1)
            pool.wait_ge(k["zeroed"], 6)
            pool.memset(vx[:, :, DH:DH + 1], 1.0).then_inc(k["zeroed"], 1)
            pool.memset(vf[:, :, :, DH:DH + 1], 1.0).then_inc(k["zeroed"], 1)
            pool.wait_ge(k["loaded"], 16 * N_LOADS)

            def rstd_of(b, n):
                pool.wait_ge(k["ln_var"], b * LN + n + 1)
                pool.tensor_tensor(rstd[:], ve[:], exponent, ALU.pow).then_inc(k["ln_rstd"], 1)

            with pool.Fori(0, B) as b:
                rstd_of(b, 0)
                pool.wait_ge(k["a_done"], b + 1)
                pool.tensor_tensor(xab[:], xa[:], vecs[:, VEC_XBO, :].unsqueeze(1).to_broadcast([P, T, D]), ALU.add).then_inc(k["xab_ready"], 1)
                rstd_of(b, 1)
                rstd_of(b, 2)
                pool.tensor_tensor(x2b[:], x2[:], vecs[:, VEC_BE2, :].unsqueeze(1).to_broadcast([P, T, D]), ALU.add).then_inc(k["x2b_ready"], 1)
                pool.wait_ge(k["ln_hat"], T * (b * LN + 3))
                pool.tensor_tensor(hat3b[:], hat3[:], vecs[:, VEC_FBO, :].unsqueeze(1).to_broadcast([P, T, D]), ALU.add).then_inc(k["hat3b_ready"], 1)
                def w_low(e):
                    for i in range(2):
                        pool.wait_ge(k["w_hi"], 2 * (NE * b + e) + i + 1)
                        pool.tensor_tensor(wsp[i][:, 1, e % 2, :], w_of(e, i), wsp[i][:, 0, e % 2, :],
                                           ALU.subtract).then_inc(k["w_lo"], 1)

                def add_expert(e):
                    pool.wait_ge(k["y_scaled"], NE * b + e + 1)
                    if e:
                        pool.wait_ge(k["rT_added"], NE * b + e)
                    else:
                        pool.wait_ge(k["rT_begun"], b + 1)
                    pool.tensor_tensor(rT[:], rT[:], ys[e % 2][:], ALU.add).then_inc(k["rT_added"], 1)

                w_low(0)
                w_low(1)
                rstd_of(b, 3)
                w_low(2)
                w_low(3)
                w_low(4)
                w_low(5)
                add_expert(0)
                add_expert(1)
                w_low(6)
                add_expert(2)
                add_expert(3)
                add_expert(4)
                w_low(7)
                for e in range(5, NE):
                    add_expert(e)
                rstd_of(b, 4)

        @block.scalar
        def _(act):
            own = Own(act, k["act_own"], ACT_STEPS)
            act.wait_ge(k["setup_done"], 1)

            def ln_evac(b, n):
                act.wait_ge(k["ln_turned"], b * (LN - 1) + n + 1)
                if n == 3:
                    for dst in (x1hi, x1T):
                        ins = act.activation(dst[:], bank[0][:], ACT.Identity, bias=cols[:, ROW_BE1:ROW_BE1 + 1],
                                             scale=cols[:, ROW_G1:ROW_G1 + 1])
                    ins.then_inc(k["ln_T"], 1)
                else:
                    act.activation(hatT[:], bank[0][:], ACT.Copy).then_inc(k["ln_T"], 1)

            def attention_out(b, n):
                act.wait_ge(k["on_turned"], 2 * b + n + 1)
                act.activation(onT[:], bank[0][:], ACT.Copy).then_inc(k["onT_ready"], 1)

            with act.Fori(0, B) as b:
                own.start(b)
                ln_evac(b, 0)
                act.wait_ge(k["a_proj"], 3 * b + 1)
                act.activation(kTa[:], bank[1][:], ACT.Copy).then_inc(k["a_k"], 1)
                act.wait_ge(k["a_proj"], 3 * b + 3)
                act.activation(va[:].rearrange("p t d -> p (t d)"), bank[3][:], ACT.Copy).then_inc(k["a_v"], 1)
                for t in range(T):
                    act.wait_ge(k["a_max"], T * b + t + 1)
                    n = (t + 1) * P
                    act.activation(pa[:, t, 0:n], bank[4 + t][:, 0:n], ACT.Exp, bias=nmas[:, t:t + 1],
                                   scale=SCALE_A, accum_out=rsa[:, t:t + 1]).then_inc(k["a_probs"], 1)
                for t in range(T):
                    act.wait_ge(k["a_turned"], T * b + t + 1)
                    n = (t + 1) * P
                    act.activation(pTa[:, t, 0:n], bank[t][:, 0:n], ACT.Copy).then_inc(k["a_probsT"], 1)
                act.wait_ge(k["c_turned"], b + 1)
                act.activation(ctxT[:], bank[5][:, 0:KC], ACT.Copy).then_inc(k["ctxT_ready"], 1)
                act.wait_ge(k["m_turned"], b + 1)
                own.inc(act.activation(mT[:], bank[6][:].bitcast(BF16)[:, 0:S], ACT.Copy))
                act.activation(mTt[0:KT0, :], bank[7][0:KT0, :].bitcast(BF16)[:, 0:S], ACT.Copy).then_inc(k["mT_ready"], 1)
                act.wait_ge(k["x_proj"], 3 * b + 1)
                act.activation(khi[:, 0:KC], bank[1][:, 0:KC], ACT.Identity,
                               bias=cols[:, ROW_XBK:ROW_XBK + 1]).then_inc(k["x_khi"], 1)
                for i in range(2):
                    act.wait_ge(k["x_kst_mm"], 2 * b + i + 1)
                    act.activation(kst[:, 2 * i:2 * i + 2, 0:KC],
                                   bank[5 + i][:, 0:2 * KC].rearrange("p (g k) -> p g k", g=2),
                                   ACT.Identity, bias=ones_row).then_inc(k["x_kst"], 1)
                ln_evac(b, 1)
                act.wait_ge(k["x_qproj"], b + 1)
                act.activation(qhi[:], bank[4][:], ACT.Identity, bias=cols[:, ROW_XBQ:ROW_XBQ + 1]).then_inc(k["x_qhi"], 1)
                for i, g in enumerate((0, 2)):
                    act.wait_ge(k["x_qst_mm"], G * b + g + 1)
                    act.activation(qst[:, g, :], bank[g][:], ACT.Copy).then_inc(k["x_qst"], 1)
                def copy_xq2(g):
                    act.wait_ge(k["x_q2_mm"], G * b + g + 1)
                    act.activation(q2st[:, g, :], bank[g][:], ACT.Copy).then_inc(k["x_q2"], 1)

                copy_xq2(0)
                copy_xq2(1)
                for g in range(G):
                    if g >= 2:
                        act.wait_ge(k["x_av"], G * b + g - 1)
                    for i in range(HG):
                        act.wait_ge(k["x_s2"], H * b + HG * g + i + 1)
                        act.activation(px[:, g % 2, i, :], bank[4 + i][:], ACT.Exp, scale=SCALE_H).then_inc(k["x_exp"], 1)
                    act.wait_ge(k["x_st"], G * b + g + 1)
                    act.activation(pxt[:, g % 2, :], bank[2 * (g % 2)][:], ACT.Exp, scale=SCALE_H).then_inc(k["x_expt"], 1)
                    if g + 2 < G:
                        copy_xq2(g + 2)
                attention_out(b, 0)
                ln_evac(b, 2)
                for i, hi in ((0, qhi), (1, khi)):
                    act.wait_ge(k["f_full"], 2 * b + i + 1)
                    act.activation(hi[:], rope_f[:, i, :], ACT.Copy).then_inc(k["f_hi"], 1)
                act.wait_ge(k["f_st_mm"], 2 * G * b + 2)
                act.activation(kst[:, 0, :], bank[ST_BANKS[1]][:], ACT.Identity, bias=ones_row).then_inc(k["f_st"], 1)

                def copy_stacks(g):
                    act.wait_ge(k["f_st_mm"], 2 * (G * b + g) + 1)
                    act.activation(qst[:, g, :], bank[ST_BANKS[2 * g]][:], ACT.Copy).then_inc(k["f_st"], 1)
                    act.wait_ge(k["f_st_mm"], 2 * (G * b + g) + 2)
                    act.activation(kst[:, g, :], bank[ST_BANKS[2 * g + 1]][:], ACT.Identity, bias=ones_row).then_inc(k["f_st"], 1)

                def copy_q2(g):
                    act.wait_ge(k["f_q2_mm"], G * b + g + 1)
                    act.activation(q2st[:, g, :], bank[q2_bank(g)][:], ACT.Copy).then_inc(k["f_q2"], 1)

                copy_stacks(1)
                copy_stacks(2)
                copy_q2(0)
                copy_stacks(3)
                for g in range(G):
                    for c in range(T):
                        for i in range(2):
                            n = (g * T + c) * 2 + i
                            act.wait_ge(k["f_s2"], 2 * T * G * b + n + 1)
                            if g * T + c >= 2:
                                act.wait_ge(k["f_av"], T * G * b + g * T + c - 1)
                            for q in range(2):
                                act.activation(px[:, c % 2, 2 * i + q, :], bank[4 + 2 * i + q][:],
                                               ACT.Exp, scale=SCALE_H).then_inc(k["f_exp"], 1)
                            if c == T - 1 and i == 0 and g + 1 < G:
                                copy_q2(g + 1)
                        if g and c == 0:
                            act.wait_ge(k["f_av"], T * G * b + g * T)
                            act.activation(ot[:, g - 1, :], bank[3][:], ACT.Copy).then_inc(k["f_ot"], 1)
                act.wait_ge(k["f_av"], T * G * (b + 1))
                act.activation(ot[:, G - 1, :], bank[3][:], ACT.Copy).then_inc(k["f_ot"], 1)

                def w_high(e, i):
                    if e >= 2 and i:
                        act.wait_ge(k["y_part"], NJ * b + FC * (e - 1))
                    act.activation(wsp[i][:, 0, e % 2, :], w_of(e, i), ACT.Copy).then_inc(k["w_hi"], 1)

                for e in range(2):
                    w_high(e, 0)
                    w_high(e, 1)
                attention_out(b, 1)
                ln_evac(b, 3)
                act.wait_ge(k["g_shift"], b + 1)
                act.activation(gt[:, 1].rearrange("p t e -> p (t e)"), gt[:, 0].rearrange("p t e -> p (t e)"),
                               ACT.Exp).then_inc(k["g_exp"], 1)
                for j in range(NJ):
                    act.wait_ge(k["h_ready"], NJ * b + j + 1)
                    if j >= 2:
                        act.wait_ge(k["h_lo"], NJ * b + j - 1)
                    act.activation(hT[:, j % 2, :], bank[4 + j % 2][:], ACT.Gelu,
                                   bias=cols[:, ROW_B1 + j:ROW_B1 + j + 1]).then_inc(k["h_act"], 1)
                    if j == COMB_AT:
                        act.wait_ge(k["g_turned"], b + 1)
                        act.activation(combT[:], bank[0][0:NE, :], ACT.Copy).then_inc(k["combT_ready"], 1)
                    e, c = divmod(j - 1 - FC, FC)
                    if e >= 0 and e + 2 < NE and c < 2:
                        w_high(e + 2, c)
                assert own.n == ACT_STEPS

        @block.vector
        def _(dve):
            own = Own(dve, k["dve_own"], DVE_STEPS)
            dve.wait_ge(k["loaded"], 16 * N_LOADS)
            for dst, src in ((eye_r, eye[:]), (eye_b, eye[:]), (tri_b, tri[:]), (sel_r, sel), (rep_b, rep[:])):
                dve.tensor_copy(dst[:], src).then_inc(k["casts"], 1)
            half = DH // 2
            for i in range(2):
                src = wf[:, i, :].rearrange("p (h d) -> p h d", d=DH)
                dst = wfr[:, i, :].rearrange("p (h d) -> p h d", d=DH)
                dve.tensor_scalar(dst[:, :, 0:half], src[:, :, half:DH], -1.0, None, ALU.mult).then_inc(k["casts"], 1)
                dve.tensor_copy(dst[:, :, half:DH], src[:, :, 0:half]).then_inc(k["casts"], 1)
            dve.wait_ge(k["rows_turned"], 1)
            dve.tensor_copy(cols[:, 0:NROWS], bank[0][:, 0:NROWS]).then_inc(k["bias_cols"], 1)
            dve.wait_ge(k["rot_cols"], 1)
            dve.wait_ge(k["zeroed"], 8)
            for hh in range(HG):
                p0 = BLK * hh
                dve.memset(vxt[p0:p0 + KT0, :, p0 + DH:p0 + DH + 1], 1.0).then_inc(k["casts"], 1)
            dve.wait_ge(k["casts"], 13)
            dve.tensor_copy(cols[:, COL_FBQR:COL_FBKR + 1], bank[1][:, 0:2]).then_inc(k["setup_done"], 1)
            dve.wait_ge(k["setup_done"], 1)

            def layer_norm(b, n, src, dst):
                for t in range(T):
                    own.inc(dve.bn_stats(stats[:, t, :], src[:, t, :]))
                own.wait()
                own.inc(dve.tensor_tensor(lnw[:, 0, :], stats[:, :, 1], stats[:, :, 4], ALU.add))
                own.inc(dve.tensor_tensor(lnw[:, 1, :], stats[:, :, 1], stats[:, :, 4], ALU.subtract))
                own.inc(dve.tensor_tensor(lnw[:, 2, :], stats[:, :, 2], stats[:, :, 5], ALU.add))
                own.wait()
                own.inc(dve.tensor_tensor(lnw[:, 3, :], lnw[:, 1, :], lnw[:, 1, :], ALU.mult))
                own.inc(dve.tensor_scalar(lnw[:, 4, :], lnw[:, 2, :], 1.0 / D, EPS, ALU.mult, ALU.add))
                own.inc(dve.tensor_scalar(mean[:], lnw[:, 0, :], 0.5, None, ALU.mult))
                own.wait()
                dve.scalar_tensor_tensor(ve[:], lnw[:, 3, :], 0.25, lnw[:, 4, :], ALU.mult, ALU.add).then_inc(k["ln_var"], 1)
                dve.wait_ge(k["ln_rstd"], b * LN + n + 1)
                for t in range(T):
                    dve.tensor_scalar(dst[:, t, :], src[:, t, :], mean[:, t:t + 1], rstd[:, t:t + 1],
                                      ALU.subtract, ALU.mult).then_inc(k["ln_hat"], 1)

            def bc(v):
                return vecs[:, v, :].unsqueeze(1).to_broadcast([P, T, D])

            def normalise_heads(b, n):
                for t in range(T):
                    dve.wait_ge(k["o_turned"], T * (2 * b + n) + t + 1)
                    heads = bank[4 + t][:].rearrange("p (h c) -> p h c", c=BLK)
                    own.inc(dve.reciprocal(rs[:, t, :].unsqueeze(2), heads[:, :, DH:DH + 1]))
                    own.wait()
                    dve.tensor_tensor(on[:, t, :].rearrange("p (h d) -> p h d", d=DH), heads[:, :, 0:DH],
                                      rs[:, t, :].unsqueeze(2).to_broadcast([P, H, DH]), ALU.mult).then_inc(k["on_ready"], 1)

            with dve.Fori(0, B) as b:
                own.start(b)
                dve.wait_ge(k["x_loaded"], 16 * b + 16)
                layer_norm(b, 0, xin, hat)
                dve.wait_ge(k["a_proj"], 3 * b + 2)
                dve.tensor_copy(qTa[:], bank[2][:]).then_inc(k["a_q"], 1)
                for t in range(T):
                    dve.wait_ge(k["a_scores"], T * b + t + 1)
                    own.inc(dve.tensor_reduce(nma[:, t:t + 1], bank[4 + t][:, 0:(t + 1) * P], AX.X, ALU.max, negate=True))
                    own.wait()
                    dve.tensor_scalar(nmas[:, t:t + 1], nma[:, t:t + 1], SCALE_A, None, ALU.mult).then_inc(k["a_max"], 1)
                dve.wait_ge(k["mask_loaded"], 16 * b + 16)
                dve.tensor_scalar(mb[:], msk[:], 0.0, NEG, ALU.is_equal, ALU.mult).then_inc(k["mb_ready"], 1)
                dve.wait_ge(k["a_probs"], T * b + T)
                own.inc(dve.reciprocal(ria[:], rsa[:]))
                own.wait()
                dve.wait_ge(k["a_out"], b + 1)
                for t in range(T):
                    ins = dve.scalar_tensor_tensor(xa[:, t, :], bank[4][:, t * D:(t + 1) * D], ria[:, t:t + 1],
                                                   xin[:, t, :], ALU.mult, ALU.add)
                ins.then_inc(k["a_done"], 1)
                dve.wait_ge(k["x_khi"], b + 1)
                dve.scalar_tensor_tensor(klo[:, 0:KC], bank[1][:, 0:KC], cols[:, ROW_XBK:ROW_XBK + 1],
                                         khi[:, 0:KC], ALU.add, ALU.subtract).then_inc(k["x_klo"], 1)
                dve.wait_ge(k["x_proj"], 3 * b + 3)
                dve.tensor_tensor(vx[:, :, 0:DH], bank[2][:, 0:D].rearrange("p (h d) -> p h d", d=DH),
                                  vecs[:, VEC_XBV, :].rearrange("p (h d) -> p h d", d=DH), ALU.add).then_inc(k["x_v"], 1)
                for hh in range(HG):
                    p0 = BLK * hh
                    dve.tensor_tensor(
                        vxt[p0:p0 + KT0, :, p0:p0 + DH],
                        bank[3][p0:p0 + KT0, 0:G * DH].rearrange("p (g d) -> p g d", d=DH),
                        vecs[p0:p0 + KT0, VEC_XBV, :].rearrange("p (g c) -> p g c", g=G)[:, :, hh * DH:(hh + 1) * DH],
                        ALU.add).then_inc(k["x_v"], 1)
                dve.wait_ge(k["x_kst"], 2 * b + 2)
                for hh in range(HG):
                    p0 = BLK * hh
                    dve.tensor_copy(ktail[p0:p0 + BLK, :, p0:p0 + KT0], kst[p0:p0 + BLK, :, P:KC]).then_inc(k["x_ktail"], 1)
                dve.wait_ge(k["a_done"], b + 1)
                layer_norm(b, 1, xa, hat)
                dve.wait_ge(k["x_qhi"], b + 1)
                dve.scalar_tensor_tensor(qlo[:], bank[4][:], cols[:, ROW_XBQ:ROW_XBQ + 1], qhi[:],
                                         ALU.add, ALU.subtract).then_inc(k["x_qlo"], 1)
                for g in (1, 3):
                    dve.wait_ge(k["x_qst_mm"], G * b + g + 1)
                    dve.tensor_copy(qst[:, g, :], bank[g if g < 3 else 7][:]).then_inc(k["x_qst"], 1)
                for t in range(T):
                    for hh in range(HG):
                        dve.wait_ge(k["x_s1"], H * b + HG * t + hh + 1)
                        for i in range(2):
                            ins = dve.tensor_reduce(
                                nm[:, t, 2 * i:2 * i + 2, BLK * hh],
                                bank[2 * hh + i][:, 0:2 * KC].rearrange("p (g k) -> p g k", g=2),
                                AX.X, ALU.max, negate=True)
                        ins.then_inc(k["x_max"], 1)
                for g in range(G):
                    dve.wait_ge(k["x_av"], G * b + g + 1)
                    dve.tensor_copy(ot[:, g, :], bank[1 + 2 * (g % 2)][:]).then_inc(k["ot_ready"], 1)
                normalise_heads(b, 0)
                dve.wait_ge(k["xab_ready"], b + 1)
                dve.wait_ge(k["o_proj"], 2 * b + 1)
                own.inc(dve.tensor_tensor(x2[:].rearrange("p t d -> p (t d)"), bank[1][:],
                                          xab[:].rearrange("p t d -> p (t d)"), ALU.add))
                own.wait()
                layer_norm(b, 2, x2, hat3)
                for i in range(2):
                    dve.wait_ge(k["f_proj"], 5 * b + 2 * i + 2)
                    dve.scalar_tensor_tensor(rope_t[:, 2 * i, :], bank[2 + 2 * i][:], cols[:, ROW_FBQ + i:ROW_FBQ + i + 1],
                                             cos[:], ALU.add, ALU.mult).then_inc(k["f_rope"], 1)
                    dve.scalar_tensor_tensor(rope_t[:, 2 * i + 1, :], bank[3 + 2 * i][:], cols[:, COL_FBQR + i:COL_FBQR + i + 1],
                                             sin[:], ALU.add, ALU.mult).then_inc(k["f_rope"], 1)
                    dve.wait_ge(k["f_rope"], 2 * (2 * b + i + 1))
                    dve.tensor_tensor(rope_f[:, i, :], rope_t[:, 2 * i, :], rope_t[:, 2 * i + 1, :], ALU.add).then_inc(k["f_full"], 1)
                    dve.wait_ge(k["f_full"], 2 * b + i + 1)
                for i, hi, lo in ((0, qhi, qlo), (1, khi, klo)):
                    dve.wait_ge(k["f_hi"], 2 * b + i + 1)
                    dve.tensor_tensor(lo[:], rope_f[:, i, :], hi[:], ALU.subtract).then_inc(k["f_lo"], 1)
                dve.wait_ge(k["f_st_mm"], 2 * G * b + 1)
                dve.tensor_copy(qst[:, 0, :], bank[ST_BANKS[0]][:]).then_inc(k["f_qst0"], 1)

                def row_maxima(g, t):
                    for hh in range(HG):
                        dve.wait_ge(k["f_s1"], H * T * b + (g * T + t) * HG + hh + 1)
                        dve.tensor_reduce(nm[:, t, g, BLK * hh:BLK * hh + 1], bank[s1_bank(g, t, hh)][:],
                                          AX.X, ALU.max, negate=True).then_inc(k["f_max"], 1)

                for t in range(T):
                    row_maxima(0, t)
                row_maxima(1, 0)
                row_maxima(1, 1)
                dve.wait_ge(k["f_proj"], 5 * b + 5)
                dve.tensor_tensor(vf[:].rearrange("p t h c -> p (t h) c")[:, :, 0:DH],
                                  bank[3][:].rearrange("p (n d) -> p n d", d=DH),
                                  vecs[:, VEC_FBV, :].unsqueeze(1).to_broadcast([P, T, D]).rearrange("p t (h d) -> p t h d", d=DH),
                                  ALU.add).then_inc(k["f_v"], 1)
                for g in range(1, G):
                    for t in range(2 if g == 1 else 1, T):
                        row_maxima(g, t)
                    if g + 1 < G:
                        row_maxima(g + 1, 0)
                normalise_heads(b, 1)
                dve.wait_ge(k["hat3b_ready"], b + 1)
                dve.wait_ge(k["o_proj"], 2 * b + 2)
                own.inc(dve.tensor_tensor(r1[:].rearrange("p t d -> p (t d)"), bank[1][:],
                                          hat3b[:].rearrange("p t d -> p (t d)"), ALU.add))
                own.wait()
                layer_norm(b, 3, r1, hat)
                dve.wait_ge(k["ln_T"], (LN - 1) * b + LN - 1)
                dve.tensor_tensor(x1lo[:], x1T[:], x1hi[:], ALU.subtract).then_inc(k["x1_split"], 1)

                def split_h(j):
                    dve.wait_ge(k["h_act"], NJ * b + j + 1)
                    if j >= 2:
                        dve.wait_ge(k["y_part"], NJ * b + j - 1)
                    dve.tensor_copy(hhi[:, j % 2, :], hT[:, j % 2, :]).then_inc(k["h_hi"], 1)
                    dve.wait_ge(k["h_hi"], NJ * b + j + 1)
                    dve.tensor_tensor(hlo[j % 2][:], hT[:, j % 2, :], hhi[:, j % 2, :], ALU.subtract).then_inc(k["h_lo"], 1)

                def scale_expert(e):
                    dve.wait_ge(k["y_part"], NJ * b + FC * (e + 1))
                    if e == 0:
                        dve.wait_ge(k["comb_loaded"], 16 * b + 16)
                    if e >= 2:
                        dve.wait_ge(k["rT_added"], NE * b + e - 1)
                    dve.tensor_tensor(ys[e % 2][:], bank[Y_BANKS[e % len(Y_BANKS)]][:], combB[:, e, :],
                                      ALU.mult).then_inc(k["y_scaled"], 1)

                flat = lambda i: gt[:, i]
                per_token = lambda i: gs[:, i, :].unsqueeze(2).to_broadcast([P, T, NE])
                dve.wait_ge(k["g_logits"], b + 1)
                own.inc(dve.tensor_tensor(flat(2), bank[1][:, 0:T * NE].rearrange("p (t e) -> p t e", e=NE),
                                          bg[:].unsqueeze(1).to_broadcast([P, T, NE]), ALU.add))
                own.wait()
                own.inc(dve.reduce_max(gs[:, 0, :], flat(2), AX.X))
                own.wait()
                dve.tensor_tensor(flat(0), flat(2), per_token(0), ALU.subtract).then_inc(k["g_shift"], 1)
                split_h(0)
                dve.wait_ge(k["g_exp"], b + 1)
                left = 1
                for i in range(2):
                    m, r, eq, hit = 1 + 2 * i, 2 + 2 * i, 3 + 3 * i, 4 + 3 * i
                    own.inc(dve.reduce_max(gs[:, m, :], flat(left), AX.X))
                    own.wait()
                    own.inc(dve.tensor_tensor(flat(eq), flat(left), per_token(m), ALU.is_equal))
                    split_h(3 * i + 1)
                    own.wait()
                    own.inc(dve.tensor_tensor(flat(5 + i * 4), flat(eq), rank, ALU.mult))
                    own.wait()
                    own.inc(dve.reduce_max(gs[:, r, :], flat(5 + i * 4), AX.X))
                    split_h(3 * i + 2)
                    own.wait()
                    own.inc(dve.tensor_tensor(flat(hit), flat(5 + i * 4), per_token(r), ALU.is_equal))
                    split_h(3 * i + 3)
                    own.wait()
                    if i == 0:
                        own.inc(dve.scalar_tensor_tensor(flat(8), flat(hit), -4.0, flat(1), ALU.mult, ALU.add))
                        own.wait()
                        left = 8
                own.inc(dve.tensor_tensor(flat(2), flat(4), flat(7), ALU.add))
                own.inc(dve.tensor_tensor(gs[:, 5, :], gs[:, 1, :], gs[:, 3, :], ALU.add))
                own.wait()
                own.inc(dve.tensor_tensor(flat(3), flat(2), flat(1), ALU.mult))
                own.inc(dve.reciprocal(gs[:, 6, :], gs[:, 5, :]))
                own.wait()
                dve.tensor_tensor(comb[:], flat(3), per_token(6), ALU.mult).then_inc(k["g_comb"], 1)
                for j in range(7, NJ):
                    split_h(j)
                    if j == COMB_AT + 4:
                        dve.wait_ge(k["b2_mm"], b + 1)
                        dve.tensor_tensor(rT[:], bank[1][:], x1T[:], ALU.add).then_inc(k["rT_begun"], 1)
                    if j in SCALE_AT:
                        scale_expert(SCALE_AT.index(j))
                scale_expert(NE - 1)
                dve.wait_ge(k["r_turned"], b + 1)
                layer_norm(b, 4, bank[7][:].rearrange("p (t d) -> p t d", t=T), r1)
                dve.wait_ge(k["ln_hat"], T * (b * LN + 5))
                own.inc(dve.tensor_tensor(hat[:], r1[:], bc(VEC_G2), ALU.mult))
                own.wait()
                dve.wait_ge(k["x2b_ready"], b + 1)
                dve.tensor_tensor(outb[:], hat[:], x2b[:], ALU.add).then_inc(k["out_ready"], 1)
                assert own.n == DVE_STEPS, own.n

        @block.tensor
        def _(pe):
            pe.wait_ge(k["loaded"], 16 * N_LOADS)
            pe.transpose(bank[0][:, 0:NROWS], rows[:], eye[0:NROWS, 0:NROWS]).then_inc(k["rows_turned"], 1)
            pe.wait_ge(k["bias_cols"], 1)
            for i in range(2):
                ins = pe.matmul(bank[1][:, i:i + 1], rot[:], cols[:, ROW_FBQ + i:ROW_FBQ + i + 1], start=True, stop=True)
            ins.then_inc(k["rot_cols"], 1)
            pe.wait_ge(k["setup_done"], 1)

            def turn_rows(b, n, src):
                for t in range(T):
                    pe.wait_ge(k["ln_hat"], T * (b * LN + n) + t + 1)
                    ins = pe.transpose(bank[0][:, t * P:(t + 1) * P], src[:, t, :], eye[:])
                ins.then_inc(k["ln_turned"], 1)
                pe.wait_ge(k["ln_T"], b * (LN - 1) + n + 1)

            def attention_out(b, n, wo):
                for t in range(T):
                    for g in range(G):
                        ins = pe.transpose(bank[4 + t][:, g * P:(g + 1) * P], ot[:, g, t * P:(t + 1) * P], eye[:])
                    ins.then_inc(k["o_turned"], 1)
                for t in range(T):
                    pe.wait_ge(k["on_ready"], T * (2 * b + n) + t + 1)
                    ins = pe.transpose(bank[0][:, t * P:(t + 1) * P], on[:, t, :], eye[:])
                ins.then_inc(k["on_turned"], 1)
                pe.wait_ge(k["onT_ready"], 2 * b + n + 1)
                for t in range(T):
                    ins = pe.matmul(bank[1][:, t * D:(t + 1) * D], onT[:, t * P:(t + 1) * P], wo, start=True, stop=True)
                ins.then_inc(k["o_proj"], 1)

            def blk(hh):
                return slice(BLK * hh, BLK * (hh + 1))

            with pe.Fori(0, B) as b:
                turn_rows(b, 0, hat)
                pe.matmul(bank[1][:], wa[:, 0, :], hatT[:], start=True, stop=True).then_inc(k["a_proj"], 1)
                pe.matmul(bank[2][:], wa[:, 1, :], hatT[:], start=True, stop=True).then_inc(k["a_proj"], 1)
                for t in range(T):
                    ins = pe.matmul(bank[3][:, t * D:(t + 1) * D], hatT[:, t * P:(t + 1) * P], wa[:, 2, :], start=True, stop=True)
                ins.then_inc(k["a_proj"], 1)
                pe.wait_ge(k["a_k"], b + 1)
                pe.wait_ge(k["a_q"], b + 1)
                for t in range(T):
                    n = (t + 1) * P
                    pe.matmul(bank[4 + t][:, 0:n], qTa[:, t * P:(t + 1) * P], kTa[:, 0:n], start=True, stop=True)
                    pe.matmul(bank[4 + t][:, t * P:n], eye_b[:], tri_b[:], start=False, stop=True,
                              skip_group_check=True).then_inc(k["a_scores"], 1)
                pe.wait_ge(k["a_v"], b + 1)
                for t in range(T):
                    pe.wait_ge(k["a_probs"], T * b + t + 1)
                    for c in range(t + 1):
                        ins = pe.transpose(bank[t][:, c * P:(c + 1) * P], pa[:, t, c * P:(c + 1) * P], eye[:])
                    ins.then_inc(k["a_turned"], 1)
                for t in range(T):
                    pe.wait_ge(k["a_probsT"], T * b + t + 1)
                    for c in range(t + 1):
                        ins = pe.matmul(bank[4][:, t * D:(t + 1) * D], pTa[:, t, c * P:(c + 1) * P], va[:, c, :],
                                        start=(c == 0), stop=(c == t))
                ins.then_inc(k["a_out"], 1)

                pe.wait_ge(k["ctx_loaded"], 32 * b + 32)
                pe.transpose(bank[5][:, 0:P], ctx[:, 0, :], eye[:])
                pe.transpose(bank[5][:, P:KC], ctx[0:KT0, 1, :], eye[0:KT0, 0:KT0]).then_inc(k["c_turned"], 1)
                pe.wait_ge(k["mb_ready"], b + 1)
                for t in range(T):
                    pe.transpose(bank[6][:].bitcast(BF16)[:, t * P:(t + 1) * P], mb[:, t, 0:P], eye_b[:])
                    ins = pe.transpose(bank[7][0:KT0, :].bitcast(BF16)[:, t * P:(t + 1) * P], mb[:, t, P:KC], eye_b[:])
                ins.then_inc(k["m_turned"], 1)
                pe.wait_ge(k["ctxT_ready"], b + 1)
                pe.matmul(bank[1][:, 0:KC], wx[:, 1, :], ctxT[:], start=True, stop=True).then_inc(k["x_proj"], 1)
                pe.matmul(bank[2][:, 0:D], ctxT[:, 0:P], wx[:, 2, :], start=True, stop=True).then_inc(k["x_proj"], 1)
                for hh in range(HG):
                    ins = pe.matmul(bank[3][BLK * hh:BLK * hh + KT0, 0:G * DH], ctxT[:, P:KC],
                                    wx[:, 2, :].rearrange("p (g c) -> p g c", g=G)[:, :, hh * DH:(hh + 1) * DH],
                                    start=True, stop=True)
                ins.then_inc(k["x_proj"], 1)
                pe.wait_ge(k["x_klo"], b + 1)
                pe.wait_ge(k["mT_ready"], b + 1)
                for g in range(G):
                    dst = bank[5 + g // 2][:, (g % 2) * KC:(g % 2 + 1) * KC]
                    pe.matmul(dst, sel_r[:, 2, g, :], khi[:, 0:KC], start=True, stop=False)
                    ins = pe.matmul(dst, sel_r[:, 3, g, :], klo[:, 0:KC], start=False, stop=True)
                    if g % 2:
                        ins.then_inc(k["x_kst_mm"], 1)
                turn_rows(b, 1, hat)
                pe.matmul(bank[4][:], wx[:, 0, :], hatT[:], start=True, stop=True).then_inc(k["x_qproj"], 1)
                pe.wait_ge(k["x_qlo"], b + 1)
                for g in range(G):
                    dst = bank[g if g < 3 else 7][:]
                    pe.matmul(dst, sel_r[:, 0, g, :], qhi[:], start=True, stop=False)
                    pe.matmul(dst, sel_r[:, 1, g, :], qlo[:], start=False, stop=True).then_inc(k["x_qst_mm"], 1)
                pe.wait_ge(k["x_qst"], G * b + G)
                pe.wait_ge(k["x_ktail"], HG * b + HG)
                for t in range(T):
                    for hh in range(HG):
                        if t:
                            pe.wait_ge(k["x_max"], H * b + HG * (t - 1) + hh + 1)
                        for i in range(2):
                            pe.matmul(bank[2 * hh + i][:, 0:2 * KC], eye_b[:],
                                      mb[:, t, :].unsqueeze(1).to_broadcast([P, 2, KC]), start=True, stop=True,
                                      skip_group_check=True)
                        for g in range(G):
                            ins = pe.matmul(bank[2 * hh + g // 2][:, (g % 2) * KC:(g % 2 + 1) * KC],
                                            qst[blk(hh), g, t * P:(t + 1) * P], kst[blk(hh), g, 0:KC],
                                            start=False, stop=True, skip_group_check=True)
                        ins.then_inc(k["x_s1"], 1)
                pe.wait_ge(k["x_max"], H * b + H)

                def x_q2(g):
                    pe.matmul(bank[g][:], sel_r[:, 0, g, :], qhi[:], start=True, stop=False, skip_group_check=True)
                    pe.matmul(bank[g][:], sel_r[:, 1, g, :], qlo[:], start=False, stop=False, skip_group_check=True)
                    for t in range(T):
                        ins = pe.matmul(bank[g][:, t * P:(t + 1) * P], nm[:, t, g, :], eye_r[:], start=False,
                                        stop=(t == T - 1), skip_group_check=True)
                    ins.then_inc(k["x_q2_mm"], 1)

                def x_sums(g):
                    acc = bank[1 + 2 * (g % 2)]
                    pe.wait_ge(k["x_exp"], H * b + HG * (g + 1))
                    pe.wait_ge(k["x_expt"], G * b + g + 1)
                    if g >= 2:
                        pe.wait_ge(k["ot_ready"], G * b + g - 1)
                    for hh in range(HG):
                        pe.matmul(acc[blk(hh), :], vx[:, HG * g + hh, :], px[:, g % 2, hh, :], start=True,
                                  stop=False, skip_group_check=True)
                    pe.matmul(acc[:], vxt[:, g, :], pxt[:, g % 2, :], start=False, stop=True,
                              skip_group_check=True).then_inc(k["x_av"], 1)

                x_q2(0)
                x_q2(1)
                for g in range(G):
                    pe.wait_ge(k["x_q2"], G * b + g + 1)
                    for hh in range(HG):
                        if g:
                            pe.wait_ge(k["x_exp"], H * b + HG * (g - 1) + hh + 1)
                        pe.matmul(bank[4 + hh][:], eye_b[:], mT[:], start=True, stop=False, skip_group_check=True)
                        pe.matmul(bank[4 + hh][:], kst[blk(hh), g, 0:P], q2st[blk(hh), g, :], start=False,
                                  stop=True, skip_group_check=True).then_inc(k["x_s2"], 1)
                    if g >= 2:
                        pe.wait_ge(k["x_expt"], G * b + g - 1)
                    if g == 1:
                        pe.wait_ge(k["x_q2"], G * b + 3)
                    tail = bank[2 * (g % 2)]
                    pe.matmul(tail[:], rep_b[0:BLK, :], mTt[:], start=True, stop=False, skip_group_check=True)
                    pe.matmul(tail[:], ktail[:, g, :], q2st[:, g, :], start=False, stop=True,
                              skip_group_check=True).then_inc(k["x_st"], 1)
                    if g + 2 < G:
                        x_q2(g + 2)
                    if g == 2:
                        pe.wait_ge(k["x_q2"], G * b + 4)
                    if g:
                        x_sums(g - 1)
                x_sums(G - 1)
                pe.wait_ge(k["ot_ready"], G * b + G)
                attention_out(b, 0, wx[:, 3, :])

                turn_rows(b, 2, hat3)
                for i in range(2):
                    pe.matmul(bank[2 + 2 * i][:], wf[:, i, :], hatT[:], start=True, stop=True).then_inc(k["f_proj"], 1)
                    pe.matmul(bank[3 + 2 * i][:], wfr[:, i, :], hatT[:], start=True, stop=True).then_inc(k["f_proj"], 1)

                def stacks(g):
                    if g == 3:
                        pe.wait_ge(k["f_st"], (2 * G - 1) * b + 3)
                    for lo, hi, first in ((qhi, qlo, 0), (khi, klo, 2)):
                        dst = bank[ST_BANKS[2 * g + first // 2]][:]
                        pe.matmul(dst, sel_r[:, first, g, :], lo[:], start=True, stop=False)
                        pe.matmul(dst, sel_r[:, first + 1, g, :], hi[:], start=False, stop=True).then_inc(k["f_st_mm"], 1)

                def wait_slot(c):
                    if c >= RING:
                        step = RING_ORDER[c - RING]
                        if len(step) == 1:
                            pe.wait_ge(k["f_q2"], G * b + step[0] + 1)
                        else:
                            g, t, hh = step
                            pe.wait_ge(k["f_max"], H * T * b + (g * T + t) * HG + hh + 1)

                def s1(g, t, hh):
                    wait_slot(RING_ORDER.index((g, t, hh)))
                    pe.matmul(bank[s1_bank(g, t, hh)][:], qst[blk(hh), g, t * P:(t + 1) * P], kst[blk(hh), g, :],
                              start=True, stop=True).then_inc(k["f_s1"], 1)

                def q2(g):
                    wait_slot(RING_ORDER.index((g,)))
                    pe.wait_ge(k["f_max"], H * T * b + (g + 1) * H)
                    dst = bank[q2_bank(g)]
                    pe.matmul(dst[:], sel_r[:, 0, g, :], qhi[:], start=True, stop=False, skip_group_check=True)
                    pe.matmul(dst[:], sel_r[:, 1, g, :], qlo[:], start=False, stop=False, skip_group_check=True)
                    for t in range(T):
                        ins = pe.matmul(dst[:, t * P:(t + 1) * P], nm[:, t, g, :], eye_r[:], start=False,
                                        stop=(t == T - 1), skip_group_check=True)
                    ins.then_inc(k["f_q2_mm"], 1)

                def s2(g, c, i):
                    n = (g * T + c) * 2 + i
                    if n >= 2:
                        pe.wait_ge(k["f_exp"], H * T * b + 2 * (n - 1))
                    for q in range(2):
                        hh = 2 * i + q
                        ins = pe.matmul(bank[4 + hh][:], kst[blk(hh), g, c * P:(c + 1) * P], q2st[blk(hh), g, :],
                                        start=True, stop=True)
                    ins.then_inc(k["f_s2"], 1)

                def sums_of(n):
                    g, c = divmod(n, T)
                    pe.wait_ge(k["f_exp"], H * T * b + (n + 1) * HG)
                    if c == 0 and g:
                        pe.wait_ge(k["f_ot"], G * b + g)
                    for hh in range(HG):
                        ins = pe.matmul(bank[3][blk(hh), :], vf[:, c, HG * g + hh, :], px[:, c % 2, hh, :],
                                        start=(c == 0), stop=(c == T - 1), skip_group_check=True)
                    ins.then_inc(k["f_av"], 1)

                pe.wait_ge(k["f_lo"], 2 * b + 2)
                stacks(0)
                pe.wait_ge(k["f_st"], (2 * G - 1) * b + 1)
                pe.wait_ge(k["f_qst0"], b + 1)
                for t in range(T):
                    for hh in range(HG):
                        s1(0, t, hh)
                stacks(1)
                stacks(2)
                pe.wait_ge(k["f_st"], (2 * G - 1) * b + 3)
                s1(1, 0, 0)
                s1(1, 0, 1)
                q2(0)
                s1(1, 0, 2)
                s1(1, 0, 3)
                stacks(3)
                pe.wait_ge(k["f_st"], (2 * G - 1) * b + 5)
                for g in range(G):
                    pe.wait_ge(k["f_q2"], G * b + g + 1)
                    for c in range(T):
                        ga, ta = divmod((g + 1) * T + c + 1, T)
                        for i in range(2):
                            if i and g * T + c == 0:
                                pe.wait_ge(k["f_st"], (2 * G - 1) * (b + 1))
                            s2(g, c, i)
                            if ga < G:
                                s1(ga, ta, 2 * i)
                                s1(ga, ta, 2 * i + 1)
                            if c == T - 1 and i == 0 and g + 1 < G:
                                q2(g + 1)
                            if g * T + c == 0:
                                for t in (2 * i, 2 * i + 1):
                                    ins = pe.matmul(bank[3][:, t * D:(t + 1) * D], hatT[:, t * P:(t + 1) * P],
                                                    wf[:, 2, :], start=True, stop=True)
                                if i:
                                    ins.then_inc(k["f_proj"], 1)
                        if g * T + c == 1:
                            pe.wait_ge(k["f_v"], b + 1)
                        if g * T + c:
                            sums_of(g * T + c - 1)
                sums_of(G * T - 1)
                pe.wait_ge(k["f_ot"], G * b + G)
                attention_out(b, 1, wf[:, 3, :])

                turn_rows(b, 3, hat)
                for t in range(T):
                    ins = pe.matmul(bank[1][:, t * NE:(t + 1) * NE], x1T[:, t * P:(t + 1) * P], wg[:], start=True, stop=True)
                ins.then_inc(k["g_logits"], 1)

                def up(j):
                    e, c = divmod(j, FC)
                    if j >= 2:
                        pe.wait_ge(k["h_act"], NJ * b + j - 1)
                    if c == 0:
                        pe.wait_ge(k["w_lo"], 2 * (NE * b + e) + 1)
                    hi, lo = (wsp[0][:, i, e % 2, c * P:(c + 1) * P] for i in range(2))
                    dst = bank[4 + j % 2][:]
                    pe.matmul(dst, hi, x1hi[:], start=True, stop=False)
                    pe.matmul(dst, lo, x1hi[:], start=False, stop=False)
                    pe.matmul(dst, hi, x1lo[:], start=False, stop=True).then_inc(k["h_ready"], 1)

                def down(j):
                    e, c = divmod(j, FC)
                    if c == 0:
                        pe.wait_ge(k["w_lo"], 2 * (NE * b + e) + 2)
                        if e == 4:
                            pe.wait_ge(k["rT_begun"], b + 1)
                        if e >= len(Y_BANKS):
                            pe.wait_ge(k["y_scaled"], NE * b + e - len(Y_BANKS) + 1)
                    pe.wait_ge(k["h_lo"], NJ * b + j + 1)
                    hi, lo = (wsp[1][:, i, e % 2, c * P:(c + 1) * P] for i in range(2))
                    dst = bank[Y_BANKS[e % len(Y_BANKS)]][:]
                    pe.matmul(dst, hi, hhi[:, j % 2, :], start=(c == 0), stop=False)
                    pe.matmul(dst, lo, hhi[:, j % 2, :], start=False, stop=False)
                    pe.matmul(dst, hi, hlo[j % 2][:], start=False, stop=(c == FC - 1)).then_inc(k["y_part"], 1)

                pe.wait_ge(k["x1_split"], b + 1)
                for j in range(NJ + 2):
                    if j < NJ:
                        up(j)
                    if j >= 2:
                        down(j - 2)
                    if j == COMB_AT:
                        pe.wait_ge(k["g_comb"], b + 1)
                        for t in range(T):
                            ins = pe.transpose(bank[0][0:NE, t * P:(t + 1) * P], comb[:, t, :], eye[:])
                        ins.then_inc(k["g_turned"], 1)
                    if j == COMB_AT + 3:
                        pe.wait_ge(k["combT_ready"], b + 1)
                        pe.matmul(bank[1][:], b2[:], combT[:], start=True, stop=True).then_inc(k["b2_mm"], 1)
                pe.wait_ge(k["rT_added"], NE * (b + 1))
                for t in range(T):
                    ins = pe.transpose(bank[7][:, t * P:(t + 1) * P], rT[:, t * P:(t + 1) * P], eye[:])
                ins.then_inc(k["r_turned"], 1)


COMB_AT = 9
SCALE_AT = (18, 19, 20, 21, 23, 26, 30)
RING = 3
N_LOADS = 22 + 6 + 7 + 2
ACT_STEPS = 1
DVE_STEPS = 83


RING_ORDER = [(0, t, hh) for t in range(T) for hh in range(HG)]
for _g in range(G):
    _next = [(_g + 1, t, hh) for t in range(T) for hh in range(HG) if _g + 1 < G]
    RING_ORDER += _next[:2] + [(_g,)] + _next[2:]
ST_BANKS = (4, 5, 6, 7, 4, 5, 6, 7)


def s1_bank(g, t, hh):
    return RING_ORDER.index((g, t, hh)) % RING


def q2_bank(g):
    return RING_ORDER.index((g,)) % RING


_WEIGHTS = [
    "L0_attn_Wk", "L0_attn_Wq", "L0_attn_Wv", "L0_xattn_wq", "L0_xattn_bq", "L0_xattn_wk", "L0_xattn_bk",
    "L0_xattn_wv", "L0_xattn_bv", "L0_xattn_wo", "L0_xattn_bo", "L0_ffn_Wq", "L0_ffn_bq", "L0_ffn_Wk",
    "L0_ffn_bk", "L0_ffn_Wv", "L0_ffn_bv", "L0_ffn_Wo", "L0_ffn_bo", "L0_ffn_Wg", "L0_ffn_bg", "L0_ffn_W1",
    "L0_ffn_b1", "L0_ffn_W2", "L0_ffn_b2", "L0_ffn_g1", "L0_ffn_be1", "L0_ffn_g2", "L0_ffn_be2",
]


def kernel(**inputs):
    import concourse.bacc as _bacc
    from concourse import mybir as _mybir
    from concourse.bass_utils import run_bass_kernel_spmd as _run

    nc = _bacc.Bacc("TRN2", target_bir_lowering=False, num_devices=1)
    arrays = {}

    def given(name, a):
        a = np.ascontiguousarray(a)
        arrays[f"in_{name}"] = a
        return nc.dram_tensor(f"in_{name}", a.shape, _mybir.dt.from_np(a.dtype), kind="ExternalInput").ap()

    x = given("x", inputs["x"])
    ctx = given("ctx_1024", inputs["ctx_1024"])
    mask = given("mask", inputs["mask_Bx1xSxS2_ik1"])
    w = {n: given(n, inputs[n]) for n in _WEIGHTS}
    consts = {n: given(f"const_{n}", a) for n, a in shape_constants().items()}
    comb = nc.dram_tensor("gate_weights", (NE, S), F32, kind="Internal").ap()
    out = nc.dram_tensor("out_0", (B, S, D), F32, kind="ExternalOutput").ap()
    build(nc, x, ctx, mask, w, consts, comb, out)
    r = _run(nc, [arrays], core_ids=[0])
    return r.results[0]["out_0"]
```

```python
from contextlib import ExitStack

import numpy as np

import concourse.bass as bass
from concourse import mybir

F32 = mybir.dt.float32
F32R = mybir.dt.float32r
BF16 = mybir.dt.bfloat16
I32 = mybir.dt.int32
ALU = mybir.AluOpType
ACT = mybir.ActivationFunctionType
AX = mybir.AxisListType

P = 128
B = 4
S = 512
T = S // P
D = 128
H = 16
DH = D // H
HG = 4
G = H // HG
BLK = P // HG
KC = 154
KT0 = KC - P
NE = 8
FF = 512
FC = FF // P
NJ = NE * FC
Y_BANKS = (6, 7, 2, 3, 1, 0)
EPS = 1e-5
NEG = -1e30
SCALE_A = float(1.0 / np.sqrt(np.float32(D)))
SCALE_H = float(1.0 / np.sqrt(np.float32(DH)))

ROW_B1 = 0
ROW_XBQ, ROW_XBK, ROW_FBQ, ROW_FBK, ROW_G1, ROW_BE1 = range(NJ, NJ + 6)
NROWS = NJ + 6
COL_FBQR, COL_FBKR = NROWS, NROWS + 1
VEC_XBV, VEC_XBO, VEC_FBV, VEC_FBO, VEC_G2, VEC_BE2 = range(6)


def shape_constants():
    eye = np.eye(P, dtype=np.float32)
    tri = np.where(np.arange(P)[None, :] > np.arange(P)[:, None], np.float32(NEG), np.float32(0))
    sel = np.zeros((4, P, G, P), np.float32)
    for which, slots in enumerate(((1, 2), (3,), (1, 3), (2,))):
        for g in range(G):
            for hh in range(HG):
                for j in slots:
                    for d in range(DH):
                        sel[which, (HG * g + hh) * DH + d, g, BLK * hh + DH * j + d] = 1
    rep = np.zeros((P, P), np.float32)
    for hh in range(HG):
        for k in range(KT0):
            rep[k, BLK * hh + k] = 1
    rot = np.zeros((P, P), np.float32)
    half = DH // 2
    for h in range(H):
        for d in range(half):
            rot[h * DH + half + d, h * DH + d] = -1
            rot[h * DH + d, h * DH + half + d] = 1
    inv = (1.0 / np.power(np.float32(10000.0), np.arange(0, DH, 2, dtype=np.float32) / np.float32(DH))).astype(np.float32)
    freqs = np.arange(S, dtype=np.float32)[:, None] * inv[None, :]
    emb = np.concatenate([freqs, freqs], axis=-1).astype(np.float32)
    cos = np.tile(np.cos(emb).T, (H, 1)).astype(np.float32)
    sin = np.tile(np.sin(emb).T, (H, 1)).astype(np.float32)
    misc = np.zeros((P, 64), np.float32)
    misc[:, 0:T] = -0.5
    misc[::BLK, 4] = 1.0
    misc[:, 8:8 + T * NE] = np.tile(NE - np.arange(NE), T)[None, :]
    return dict(eye=eye, tri=tri, sel=sel, rep=rep, rot=rot, cos=cos, sin=sin, misc=misc)


class Own:

    def __init__(self, eng, sem, per):
        self.eng, self.sem, self.per, self.base, self.n = eng, sem, per, 0, 0

    def start(self, b):
        assert self.n in (0, self.per), (self.n, self.per)
        self.base, self.n = b * self.per, 0

    def inc(self, ins):
        self.n += 1
        return ins.then_inc(self.sem, 1)

    def wait(self):
        if self.n:
            self.eng.wait_ge(self.sem, self.base + self.n)


def build(nc, x, ctx_in, mask, w, consts, comb_dram, out):
    stack = ExitStack()
    with stack:
        def sb(name, shape, dt=F32):
            return stack.enter_context(nc.sbuf_tensor(name, shape, dt))

        def sem(name):
            return stack.enter_context(nc.semaphore(name))

        eye = sb("eye", [P, P])
        eye_r = sb("eye_r", [P, P], F32R)
        eye_b = sb("eye_b", [P, P], BF16)
        tri = sb("tri", [P, P])
        tri_b = sb("tri_b", [P, P], BF16)
        sel_r = sb("sel_r", [P, 4, G, P], F32R)
        rep = sb("rep", [P, P])
        rep_b = sb("rep_b", [P, P], BF16)
        rot = sb("rot", [P, P])
        cos = sb("cos", [P, S])
        sin = sb("sin", [P, S])
        misc = sb("misc", [P, 64])
        exponent = misc[:, 0:T]
        ones_row = misc[:, 4:5]
        rank = misc[:, 8:8 + T * NE].rearrange("p (t e) -> p t e", t=T)
        wa = sb("wa", [P, 3, D])
        wx = sb("wx", [P, 4, D])
        wf = sb("wf", [P, 4, D])
        wfr = sb("wfr", [P, 2, D])
        wg = sb("wg", [P, NE])
        w1 = sb("w1", [P, NE, FF])
        w2 = sb("w2", [P, NJ, D])
        b2 = sb("b2", [NE, D])
        rows = sb("rows", [NROWS, P])
        cols = sb("cols", [P, NROWS + 2])
        vecs = sb("vecs", [P, 6, D])
        bg = sb("bg", [P, NE])

        xin = sb("xin", [P, T, D])
        ctx = sb("ctx", [P, 2, D])
        msk = sb("msk", [P, T, KC], I32)
        stats = sb("stats", [P, T, 6])
        lnw = sb("lnw", [P, 5, T])
        mean = sb("mean", [P, T])
        ve = sb("ve", [P, T])
        rstd = sb("rstd", [P, T])
        hat = sb("hat", [P, T, D])
        hat3 = sb("hat3", [P, T, D])
        hatT = sb("hatT", [P, S])
        kTa = sb("kTa", [P, S])
        qTa = sb("qTa", [P, S])
        va = sb("va", [P, T, D])
        nma = sb("nma", [P, T])
        nmas = sb("nmas", [P, T])
        rsa = sb("rsa", [P, T])
        ria = sb("ria", [P, T])
        xa = sb("xa", [P, T, D])
        xab = sb("xab", [P, T, D])
        ctxT = sb("ctxT", [P, KC])
        mb = sb("mb", [P, T, KC], BF16)
        mT = sb("mT", [P, S], BF16)
        mTt = sb("mTt", [BLK, S], BF16)
        khi = sb("khi", [P, S], F32R)
        klo = sb("klo", [P, S], F32R)
        qhi = sb("qhi", [P, S], F32R)
        qlo = sb("qlo", [P, S], F32R)
        kst = sb("kst", [P, G, S], F32R)
        ktail = sb("ktail", [P, G, P], F32R)
        qst = sb("qst", [P, G, S], F32R)
        q2st = sb("q2st", [P, G, S], F32R)
        nm = sb("nm", [P, T, G, P], F32R)
        vx = sb("vx", [P, H, BLK])
        vxt = sb("vxt", [P, G, P])
        px = sb("px", [P, 2, HG, S])
        pxt = sb("pxt", [P, 2, S])
        pa, pTa = px[:, 0], px[:, 1]
        rope_t, rope_f = px[:, 0], px[:, 1, 0:2]
        combB = px[:].rearrange("p a b s -> p (a b) s")
        ot = sb("ot", [P, G, S])
        sel = ot[:].rearrange("p w (g q) -> p w g q", g=G)
        rs = sb("rs", [P, T, H])
        on = sb("on", [P, T, D])
        onT = sb("onT", [P, S])
        x2 = sb("x2", [P, T, D])
        x2b = sb("x2b", [P, T, D])
        hat3b = sb("hat3b", [P, T, D])
        vf = sb("vf", [P, T, H, BLK])
        r1 = sb("r1", [P, T, D])
        x1T = sb("x1T", [P, S])
        gt = sb("gt", [P, 10, T, NE])
        gs = sb("gs", [P, 8, T])
        comb = sb("comb", [P, T, NE])
        combT = sb("combT", [NE, S])
        hT = sb("hT", [P, 2, S])
        hhi = sb("hhi", [P, 2, S], F32R)
        rT = sb("rT", [P, S])
        wsp = [t[:].rearrange("p (m r) s -> p m r s", r=2) for t in (qst, q2st)]
        x1hi, x1lo = qhi, qlo
        hlo = [khi, klo]
        ys = [onT[:], r1[:].rearrange("p t d -> p (t d)")]
        outb = sb("outb", [P, T, D])

        bank = [stack.enter_context(nc.psum_tensor(f"bank{i}", [P, 512], F32)) for i in range(8)]

        k = {name: sem(name) for name in (
            "front_loaded", "loaded", "casts", "zeroed", "rows_turned", "bias_cols", "rot_cols", "setup_done",
            "x_loaded", "ctx_loaded", "mask_loaded", 
            "ln_var", "ln_rstd", "ln_hat", "ln_turned", "ln_T", "end_var", "end_rstd", "end_hat",
            "a_proj", "a_k", "a_q", "a_v", "a_scores", "a_max", "a_probs", "a_turned", "a_probsT",
            "a_out", "a_done",
            "c_turned", "ctxT_ready", "mb_ready", "m_turned", "mT_ready", "x_proj", "x_khi", "x_klo",
            "x_v", "x_kst_mm", "x_kst", "x_ktail", "x_qproj", "x_qhi", "x_qlo", "x_qst_mm", "x_qst",
            "x_s1", "x_max", "x_q2_mm", "x_q2", "x_s2", "x_exp", "x_st", "x_expt", "x_av",
            "ot_ready", "o_turned", "on_ready", "on_turned", "onT_ready", "o_proj", "xab_ready",
            "b_done",
            "f_proj", "f_rope", "f_full", "f_hi", "f_lo", "f_v", "f_st_mm", "f_qst0", "f_st", "f_s1", "f_max",
            "f_q2_mm", "f_q2", "f_s2", "f_exp", "f_av", "f_ot", "hat3b_ready", "r1_ready",
            "g_logits", "g_shift", "g_exp", "g_comb", "g_turned", "combT_ready", "comb_stored", "comb_loaded",
            "x1_split", "w_hi", "w_lo", "h_ready", "h_act", "h_hi", "h_hi_act", "h_lo", "y_part", "y_scaled", "b2_mm",
            "rT_begun", "rT_added", "r_turned", "x2b_ready",
            "out_ready", "out_stored",
            "act_own", "dve_own", "dve_front", "experts_loaded",
        )}

        def w_of(e, i):
            return w2[:, FC * e:FC * (e + 1), :].rearrange("p c d -> p (c d)") if i else w1[:, e, :]

        block = stack.enter_context(nc.Block())

        LN = 4

        @block.sync
        def _(sp):
            front_loads = [
                (eye[:], consts["eye"]), (tri[:], consts["tri"]), (misc[:], consts["misc"]),
                (wa[:, 0, :], w["L0_attn_Wk"]), (wa[:, 1, :], w["L0_attn_Wq"]), (wa[:, 2, :], w["L0_attn_Wv"]),
            ]
            loads = [
                (sel, consts["sel"].rearrange("w p g q -> p w g q")),
                (rep[:], consts["rep"]), (rot[:], consts["rot"]),
                (cos[:], consts["cos"]), (sin[:], consts["sin"]),
                (wx[:, 0, :], w["L0_xattn_wq"]), (wx[:, 1, :], w["L0_xattn_wk"]),
                (wx[:, 2, :], w["L0_xattn_wv"]), (wx[:, 3, :], w["L0_xattn_wo"]),
                (wf[:, 0, :], w["L0_ffn_Wq"]), (wf[:, 1, :], w["L0_ffn_Wk"]),
                (wf[:, 2, :], w["L0_ffn_Wv"]), (wf[:, 3, :], w["L0_ffn_Wo"]),
                (wg[:], w["L0_ffn_Wg"]), (b2[:], w["L0_ffn_b2"]),
                (rows[ROW_B1:NJ, :], w["L0_ffn_b1"].rearrange("e (c p) -> (e c) p", p=P)),
            ]
            for r, n in ((ROW_XBQ, "L0_xattn_bq"), (ROW_XBK, "L0_xattn_bk"), (ROW_FBQ, "L0_ffn_bq"),
                         (ROW_FBK, "L0_ffn_bk"), (ROW_G1, "L0_ffn_g1"), (ROW_BE1, "L0_ffn_be1")):
                loads.append((rows[r:r + 1, :], w[n].rearrange("(a d) -> a d", a=1)))
            for v, n in ((VEC_XBV, "L0_xattn_bv"), (VEC_XBO, "L0_xattn_bo"), (VEC_FBV, "L0_ffn_bv"),
                         (VEC_FBO, "L0_ffn_bo"), (VEC_G2, "L0_ffn_g2"), (VEC_BE2, "L0_ffn_be2")):
                loads.append((vecs[:, v, :], w[n].partition_broadcast(P)))
            loads.append((bg[:], w["L0_ffn_bg"].partition_broadcast(P)))
            expert_loads = [
                (w1[:], w["L0_ffn_W1"].rearrange("e d f -> d e f")),
                (w2[:], w["L0_ffn_W2"].rearrange("e (c p) d -> p (e c) d", p=P)),
            ]
            assert len(loads) == N_LOADS

            def load_x(b):
                sp.dma_start(xin[:], x[bass.ds(b, 1)].rearrange("b (t p) d -> p (b t) d", p=P)).then_inc(k["x_loaded"], 16)

            def load_ctx(b):
                sp.dma_start(ctx[:, 0, :], ctx_in[bass.ds(b, 1), 0:P, :].rearrange("b k d -> (b k) d")).then_inc(k["ctx_loaded"], 16)
                sp.dma_start(ctx[0:KT0, 1, :], ctx_in[bass.ds(b, 1), P:KC, :].rearrange("b k d -> (b k) d")).then_inc(k["ctx_loaded"], 16)

            def load_mask(b):
                sp.dma_start(msk[:], mask[bass.ds(b, 1)].rearrange("b o (t p) k -> p (b o t) k", p=P)).then_inc(k["mask_loaded"], 16)

            load_x(0)
            for dst, src in front_loads:
                sp.dma_start(dst, src).then_inc(k["front_loaded"], 16)
            for dst, src in loads:
                sp.dma_start(dst, src).then_inc(k["loaded"], 16)
            load_ctx(0)
            load_mask(0)
            for dst, src in expert_loads:
                sp.dma_start(dst, src).then_inc(k["experts_loaded"], 16)

            def results(b):
                sp.wait_ge(k["combT_ready"], b + 1)
                sp.dma_start(comb_dram, combT[:]).then_inc(k["comb_stored"], 16)
                sp.wait_ge(k["comb_stored"], b * 16 + 16)
                sp.dma_start(combB.rearrange("p e s -> p (e s)"),
                             comb_dram.rearrange("e s -> (e s)").partition_broadcast(P)).then_inc(k["comb_loaded"], 16)
                sp.wait_ge(k["out_ready"], b + 1)
                sp.dma_start(out[bass.ds(b, 1)].rearrange("b (t p) d -> p (b t) d", p=P), outb[:]).then_inc(k["out_stored"], 16)

            with sp.Fori(0, B - 1) as b:
                sp.wait_ge(k["a_done"], b + 1)
                load_x(b + 1)
                sp.wait_ge(k["c_turned"], b + 1)
                load_ctx(b + 1)
                sp.wait_ge(k["mb_ready"], b + 1)
                load_mask(b + 1)
                results(b)
            results(B - 1)
            sp.wait_ge(k["out_stored"], 16 * B)

        @block.gpsimd
        def _(pool):
            for tile in (ktail, nm):
                pool.memset(tile[:].bitcast(F32), 0.0).then_inc(k["zeroed"], 1)
            for tile in (vx, vxt, vf):
                pool.memset(tile[:], 0.0).then_inc(k["zeroed"], 1)
            pool.memset(mTt[:], 0.0).then_inc(k["zeroed"], 1)
            pool.wait_ge(k["zeroed"], 6)
            pool.memset(vx[:, :, DH:DH + 1], 1.0).then_inc(k["zeroed"], 1)
            pool.memset(vf[:, :, :, DH:DH + 1], 1.0).then_inc(k["zeroed"], 1)
            pool.wait_ge(k["front_loaded"], 16 * N_FRONT_LOADS)

            def rstd_of(b, n):
                pool.wait_ge(k["ln_var"], b * LN + n + 1)
                pool.tensor_tensor(rstd[:], ve[:], exponent, ALU.pow).then_inc(k["ln_rstd"], 1)

            def batch(b, last):
                pool.wait_ge(k["a_done"], b + 1)
                pool.tensor_tensor(xab[:], xa[:], vecs[:, VEC_XBO, :].unsqueeze(1).to_broadcast([P, T, D]), ALU.add).then_inc(k["xab_ready"], 1)
                rstd_of(b, 1)
                rstd_of(b, 2)
                pool.tensor_tensor(x2b[:], x2[:], vecs[:, VEC_BE2, :].unsqueeze(1).to_broadcast([P, T, D]), ALU.add).then_inc(k["x2b_ready"], 1)
                pool.wait_ge(k["ln_hat"], T * (b * LN + 3))
                pool.tensor_tensor(hat3b[:], hat3[:], vecs[:, VEC_FBO, :].unsqueeze(1).to_broadcast([P, T, D]), ALU.add).then_inc(k["hat3b_ready"], 1)
                def w_low(e):
                    for i in range(2):
                        pool.wait_ge(k["w_hi"], 2 * (NE * b + e) + i + 1)
                        pool.tensor_tensor(wsp[i][:, 1, e % 2, :], w_of(e, i), wsp[i][:, 0, e % 2, :],
                                           ALU.subtract).then_inc(k["w_lo"], 1)

                def add_expert(e):
                    pool.wait_ge(k["y_scaled"], NE * b + e + 1)
                    if e:
                        pool.wait_ge(k["rT_added"], (NE - 1) * b + e)
                    else:
                        pool.wait_ge(k["rT_begun"], b + 1)
                    pool.tensor_tensor(rT[:], rT[:], ys[e % 2], ALU.add).then_inc(k["rT_added"], 1)

                pool.wait_ge(k["experts_loaded"], 32)
                w_low(0)
                w_low(1)
                rstd_of(b, 3)
                w_low(2)
                w_low(3)
                w_low(4)
                if not last:
                    rstd_of(b + 1, 0)
                w_low(5)
                add_expert(0)
                add_expert(1)
                w_low(6)
                add_expert(2)
                add_expert(3)
                add_expert(4)
                w_low(7)
                add_expert(5)
                add_expert(6)
                pool.wait_ge(k["end_var"], b + 1)
                pool.tensor_tensor(rstd[:], ve[:], exponent, ALU.pow).then_inc(k["end_rstd"], 1)

            rstd_of(0, 0)
            pool.wait_ge(k["loaded"], 16 * N_LOADS)
            with pool.Fori(0, B - 1) as b:
                batch(b, False)
            batch(B - 1, True)

        @block.scalar
        def _(act):
            own = Own(act, k["act_own"], ACT_STEPS)

            def ln_evac(b, n):
                act.wait_ge(k["ln_turned"], b * LN + n + 1)
                if n == 3:
                    for dst in (x1hi, x1T):
                        ins = act.activation(dst[:], bank[0][:], ACT.Identity, bias=cols[:, ROW_BE1:ROW_BE1 + 1],
                                             scale=cols[:, ROW_G1:ROW_G1 + 1])
                    ins.then_inc(k["ln_T"], 1)
                else:
                    act.activation(hatT[:], bank[0][:], ACT.Copy).then_inc(k["ln_T"], 1)

            def attention_out(b, n):
                act.wait_ge(k["on_turned"], 2 * b + n + 1)
                act.activation(onT[:], bank[0][:], ACT.Copy).then_inc(k["onT_ready"], 1)

            def front(b):
                ln_evac(b, 0)
                act.wait_ge(k["a_proj"], 3 * b + 1)
                act.activation(kTa[:], bank[1][:], ACT.Copy).then_inc(k["a_k"], 1)
                act.wait_ge(k["a_proj"], 3 * b + 3)
                act.activation(va[:].rearrange("p t d -> p (t d)"), bank[0][:], ACT.Copy).then_inc(k["a_v"], 1)

            def batch(b, last):
                own.start(b)
                for t in range(T):
                    act.wait_ge(k["a_max"], T * b + t + 1)
                    n = (t + 1) * P
                    act.activation(pa[:, t, 0:n], bank[4 + t][:, 0:n], ACT.Exp, bias=nmas[:, t:t + 1],
                                   scale=SCALE_A, accum_out=rsa[:, t:t + 1]).then_inc(k["a_probs"], 1)
                for t in range(T):
                    act.wait_ge(k["a_turned"], T * b + t + 1)
                    n = (t + 1) * P
                    act.activation(pTa[:, t, 0:n], bank[t][:, 0:n], ACT.Copy).then_inc(k["a_probsT"], 1)
                act.wait_ge(k["c_turned"], b + 1)
                act.activation(ctxT[:], bank[5][:, 0:KC], ACT.Copy).then_inc(k["ctxT_ready"], 1)
                act.wait_ge(k["m_turned"], b + 1)
                own.inc(act.activation(mT[:], bank[6][:].bitcast(BF16)[:, 0:S], ACT.Copy))
                act.activation(mTt[0:KT0, :], bank[7][0:KT0, :].bitcast(BF16)[:, 0:S], ACT.Copy).then_inc(k["mT_ready"], 1)
                act.wait_ge(k["x_proj"], 3 * b + 1)
                act.activation(khi[:, 0:KC], bank[1][:, 0:KC], ACT.Identity,
                               bias=cols[:, ROW_XBK:ROW_XBK + 1]).then_inc(k["x_khi"], 1)
                for i in range(2):
                    act.wait_ge(k["x_kst_mm"], 2 * b + i + 1)
                    act.activation(kst[:, 2 * i:2 * i + 2, 0:KC],
                                   bank[5 + i][:, 0:2 * KC].rearrange("p (g k) -> p g k", g=2),
                                   ACT.Identity, bias=ones_row).then_inc(k["x_kst"], 1)
                ln_evac(b, 1)
                act.wait_ge(k["x_qproj"], b + 1)
                act.activation(qhi[:], bank[4][:], ACT.Identity, bias=cols[:, ROW_XBQ:ROW_XBQ + 1]).then_inc(k["x_qhi"], 1)
                for i, g in enumerate((0, 2)):
                    act.wait_ge(k["x_qst_mm"], G * b + g + 1)
                    act.activation(qst[:, g, :], bank[g][:], ACT.Copy).then_inc(k["x_qst"], 1)
                def copy_xq2(g):
                    act.wait_ge(k["x_q2_mm"], G * b + g + 1)
                    act.activation(q2st[:, g, :], bank[g][:], ACT.Copy).then_inc(k["x_q2"], 1)

                copy_xq2(0)
                copy_xq2(1)
                for g in range(G):
                    if g >= 2:
                        act.wait_ge(k["x_av"], G * b + g - 1)
                    for i in range(HG):
                        act.wait_ge(k["x_s2"], H * b + HG * g + i + 1)
                        act.activation(px[:, g % 2, i, :], bank[4 + i][:], ACT.Exp, scale=SCALE_H).then_inc(k["x_exp"], 1)
                    act.wait_ge(k["x_st"], G * b + g + 1)
                    act.activation(pxt[:, g % 2, :], bank[2 * (g % 2)][:], ACT.Exp, scale=SCALE_H).then_inc(k["x_expt"], 1)
                    if g + 2 < G:
                        copy_xq2(g + 2)
                attention_out(b, 0)
                ln_evac(b, 2)
                for i, hi in ((0, qhi), (1, khi)):
                    act.wait_ge(k["f_full"], 2 * b + i + 1)
                    act.activation(hi[:], rope_f[:, i, :], ACT.Copy).then_inc(k["f_hi"], 1)
                act.wait_ge(k["f_st_mm"], 2 * G * b + 2)
                act.activation(kst[:, 0, :], bank[ST_BANKS[1]][:], ACT.Identity, bias=ones_row).then_inc(k["f_st"], 1)

                def copy_stacks(g):
                    act.wait_ge(k["f_st_mm"], 2 * (G * b + g) + 1)
                    act.activation(qst[:, g, :], bank[ST_BANKS[2 * g]][:], ACT.Copy).then_inc(k["f_st"], 1)
                    act.wait_ge(k["f_st_mm"], 2 * (G * b + g) + 2)
                    act.activation(kst[:, g, :], bank[ST_BANKS[2 * g + 1]][:], ACT.Identity, bias=ones_row).then_inc(k["f_st"], 1)

                def copy_q2(g):
                    act.wait_ge(k["f_q2_mm"], G * b + g + 1)
                    act.activation(q2st[:, g, :], bank[q2_bank(g)][:], ACT.Copy).then_inc(k["f_q2"], 1)

                copy_stacks(1)
                copy_stacks(2)
                copy_q2(0)
                copy_stacks(3)
                for g in range(G):
                    for c in range(T):
                        for i in range(2):
                            n = (g * T + c) * 2 + i
                            act.wait_ge(k["f_s2"], 2 * T * G * b + n + 1)
                            if g * T + c >= 2:
                                act.wait_ge(k["f_av"], T * G * b + g * T + c - 1)
                            for q in range(2):
                                act.activation(px[:, c % 2, 2 * i + q, :], bank[4 + 2 * i + q][:],
                                               ACT.Exp, scale=SCALE_H).then_inc(k["f_exp"], 1)
                            if c == T - 1 and i == 0 and g + 1 < G:
                                copy_q2(g + 1)
                        if g and c == 0:
                            act.wait_ge(k["f_av"], T * G * b + g * T)
                            act.activation(ot[:, g - 1, :], bank[3][:], ACT.Copy).then_inc(k["f_ot"], 1)
                act.wait_ge(k["f_av"], T * G * (b + 1))
                act.activation(ot[:, G - 1, :], bank[3][:], ACT.Copy).then_inc(k["f_ot"], 1)

                def w_high(e, i):
                    if e >= 2 and i:
                        act.wait_ge(k["y_part"], NJ * b + FC * (e - 1))
                    act.activation(wsp[i][:, 0, e % 2, :], w_of(e, i), ACT.Copy).then_inc(k["w_hi"], 1)

                act.wait_ge(k["experts_loaded"], 32)
                for e in range(2):
                    w_high(e, 0)
                    w_high(e, 1)
                attention_out(b, 1)
                ln_evac(b, 3)
                act.wait_ge(k["g_shift"], b + 1)
                act.activation(gt[:, 1].rearrange("p t e -> p (t e)"), gt[:, 0].rearrange("p t e -> p (t e)"),
                               ACT.Exp).then_inc(k["g_exp"], 1)
                for j in range(NJ):
                    act.wait_ge(k["h_ready"], NJ * b + j + 1)
                    if j >= 2:
                        act.wait_ge(k["h_lo"], NJ * b + j - 1)
                    act.activation(hT[:, j % 2, :], bank[4 + j % 2][:], ACT.Gelu,
                                   bias=cols[:, ROW_B1 + j:ROW_B1 + j + 1]).then_inc(k["h_act"], 1)
                    if j in HI_ON_ACT:
                        act.wait_ge(k["y_part"], NJ * b + j - 1)
                        act.activation(hhi[:, j % 2, :], bank[4 + j % 2][:], ACT.Gelu,
                                       bias=cols[:, ROW_B1 + j:ROW_B1 + j + 1]).then_inc(k["h_hi_act"], 1)
                    if j == COMB_AT:
                        act.wait_ge(k["g_turned"], b + 1)
                        act.activation(combT[:], bank[0][0:NE, :], ACT.Copy).then_inc(k["combT_ready"], 1)
                    e, c = divmod(j - 1 - FC, FC)
                    if e >= 0 and e + 2 < NE and c < 2:
                        w_high(e + 2, c)
                if not last:
                    front(b + 1)
                assert own.n == ACT_STEPS

            front(0)
            act.wait_ge(k["setup_done"], 1)
            with act.Fori(0, B - 1) as b:
                batch(b, False)
            batch(B - 1, True)

        @block.vector
        def _(dve):
            own = Own(dve, k["dve_own"], DVE_STEPS)
            dve.wait_ge(k["front_loaded"], 16 * N_FRONT_LOADS)
            for dst, src in ((eye_r, eye[:]), (eye_b, eye[:]), (tri_b, tri[:])):
                dve.tensor_copy(dst[:], src).then_inc(k["casts"], 1)
            dve.memset(outb[:, 0, 0:1], 0.0).then_inc(k["end_hat"], 1)

            def ln_stats(own, ready, src):
                for t in range(T):
                    own.inc(dve.bn_stats(stats[:, t, :], src[:, t, :]))
                ln_moments(own, ready)

            def ln_moments(own, ready):
                own.wait()
                own.inc(dve.tensor_tensor(lnw[:, 0, :], stats[:, :, 1], stats[:, :, 4], ALU.add))
                own.inc(dve.tensor_tensor(lnw[:, 1, :], stats[:, :, 1], stats[:, :, 4], ALU.subtract))
                own.inc(dve.tensor_tensor(lnw[:, 2, :], stats[:, :, 2], stats[:, :, 5], ALU.add))
                own.wait()
                own.inc(dve.tensor_tensor(lnw[:, 3, :], lnw[:, 1, :], lnw[:, 1, :], ALU.mult))
                own.inc(dve.tensor_scalar(lnw[:, 4, :], lnw[:, 2, :], 1.0 / D, EPS, ALU.mult, ALU.add))
                own.inc(dve.tensor_scalar(mean[:], lnw[:, 0, :], 0.5, None, ALU.mult))
                own.wait()
                dve.scalar_tensor_tensor(ve[:], lnw[:, 3, :], 0.25, lnw[:, 4, :], ALU.mult, ALU.add).then_inc(ready, 1)

            def ln_rows(src, dst, ready):
                for t in range(T):
                    dve.tensor_scalar(dst[:, t, :], src[:, t, :], mean[:, t:t + 1], rstd[:, t:t + 1],
                                      ALU.subtract, ALU.mult).then_inc(ready, 1)

            def layer_norm(b, n, src, dst):
                ln_stats(own, k["ln_var"], src)
                dve.wait_ge(k["ln_rstd"], b * LN + n + 1)
                ln_rows(src, dst, k["ln_hat"])

            def bc(v):
                return vecs[:, v, :].unsqueeze(1).to_broadcast([P, T, D])

            def normalise_heads(b, n):
                for t in range(T):
                    dve.wait_ge(k["o_turned"], T * (2 * b + n) + t + 1)
                    heads = bank[4 + t][:].rearrange("p (h c) -> p h c", c=BLK)
                    own.inc(dve.reciprocal(rs[:, t, :].unsqueeze(2), heads[:, :, DH:DH + 1]))
                    own.wait()
                    dve.tensor_tensor(on[:, t, :].rearrange("p (h d) -> p h d", d=DH), heads[:, :, 0:DH],
                                      rs[:, t, :].unsqueeze(2).to_broadcast([P, H, DH]), ALU.mult).then_inc(k["on_ready"], 1)

            front = Own(dve, k["dve_front"], FRONT_STEPS)

            def front_stats(b, t):
                if t == 0:
                    front.start(b)
                    dve.wait_ge(k["x_loaded"], 16 * b + 16)
                front.inc(dve.bn_stats(stats[:, t, :], xin[:, t, :]))

            def front_moments(b):
                ln_moments(front, k["ln_var"])

            def front_rows(b):
                dve.wait_ge(k["ln_rstd"], b * LN + 1)
                ln_rows(xin, hat, k["ln_hat"])

            def front_queries(b):
                dve.wait_ge(k["a_proj"], 3 * b + 2)
                dve.tensor_copy(qTa[:], bank[2][:]).then_inc(k["a_q"], 1)

            def front_maxima(b):
                for t in range(T):
                    dve.wait_ge(k["a_scores"], T * b + t + 1)
                    front.inc(dve.tensor_reduce(nma[:, t:t + 1], bank[4 + t][:, 0:(t + 1) * P], AX.X, ALU.max, negate=True))
                    front.wait()
                    dve.tensor_scalar(nmas[:, t:t + 1], nma[:, t:t + 1], SCALE_A, None, ALU.mult).then_inc(k["a_max"], 1)
                assert front.n == FRONT_STEPS, front.n

            def batch(b, last):
                own.start(b)
                dve.wait_ge(k["mask_loaded"], 16 * b + 16)
                dve.tensor_scalar(mb[:], msk[:], 0.0, NEG, ALU.is_equal, ALU.mult).then_inc(k["mb_ready"], 1)
                dve.wait_ge(k["a_probs"], T * b + T)
                own.inc(dve.reciprocal(ria[:], rsa[:]))
                own.wait()
                dve.wait_ge(k["a_out"], b + 1)
                for t in range(T):
                    ins = dve.scalar_tensor_tensor(xa[:, t, :], bank[4][:, t * D:(t + 1) * D], ria[:, t:t + 1],
                                                   xin[:, t, :], ALU.mult, ALU.add)
                ins.then_inc(k["a_done"], 1)
                dve.wait_ge(k["a_done"], b + 1)
                ln_stats(own, k["ln_var"], xa)
                dve.wait_ge(k["x_khi"], b + 1)
                dve.scalar_tensor_tensor(klo[:, 0:KC], bank[1][:, 0:KC], cols[:, ROW_XBK:ROW_XBK + 1],
                                         khi[:, 0:KC], ALU.add, ALU.subtract).then_inc(k["x_klo"], 1)
                dve.wait_ge(k["x_proj"], 3 * b + 3)
                dve.tensor_tensor(vx[:, :, 0:DH], bank[2][:, 0:D].rearrange("p (h d) -> p h d", d=DH),
                                  vecs[:, VEC_XBV, :].rearrange("p (h d) -> p h d", d=DH), ALU.add).then_inc(k["x_v"], 1)
                for hh in range(HG):
                    p0 = BLK * hh
                    dve.tensor_tensor(
                        vxt[p0:p0 + KT0, :, p0:p0 + DH],
                        bank[3][p0:p0 + KT0, 0:G * DH].rearrange("p (g d) -> p g d", d=DH),
                        vecs[p0:p0 + KT0, VEC_XBV, :].rearrange("p (g c) -> p g c", g=G)[:, :, hh * DH:(hh + 1) * DH],
                        ALU.add).then_inc(k["x_v"], 1)
                dve.wait_ge(k["ln_rstd"], b * LN + 2)
                ln_rows(xa, hat, k["ln_hat"])
                dve.wait_ge(k["x_kst"], 2 * b + 2)
                for hh in range(HG):
                    p0 = BLK * hh
                    dve.tensor_copy(ktail[p0:p0 + BLK, :, p0:p0 + KT0], kst[p0:p0 + BLK, :, P:KC]).then_inc(k["x_ktail"], 1)
                dve.wait_ge(k["x_qhi"], b + 1)
                dve.scalar_tensor_tensor(qlo[:], bank[4][:], cols[:, ROW_XBQ:ROW_XBQ + 1], qhi[:],
                                         ALU.add, ALU.subtract).then_inc(k["x_qlo"], 1)
                for g in (1, 3):
                    dve.wait_ge(k["x_qst_mm"], G * b + g + 1)
                    dve.tensor_copy(qst[:, g, :], bank[g if g < 3 else 7][:]).then_inc(k["x_qst"], 1)
                for t in range(T):
                    for hh in range(HG):
                        dve.wait_ge(k["x_s1"], H * b + HG * t + hh + 1)
                        for i in range(2):
                            ins = dve.tensor_reduce(
                                nm[:, t, 2 * i:2 * i + 2, BLK * hh],
                                bank[2 * hh + i][:, 0:2 * KC].rearrange("p (g k) -> p g k", g=2),
                                AX.X, ALU.max, negate=True)
                        ins.then_inc(k["x_max"], 1)
                for g in range(G):
                    dve.wait_ge(k["x_av"], G * b + g + 1)
                    dve.tensor_copy(ot[:, g, :], bank[1 + 2 * (g % 2)][:]).then_inc(k["ot_ready"], 1)
                normalise_heads(b, 0)
                dve.wait_ge(k["xab_ready"], b + 1)
                dve.wait_ge(k["o_proj"], 2 * b + 1)
                own.inc(dve.tensor_tensor(x2[:].rearrange("p t d -> p (t d)"), bank[1][:],
                                          xab[:].rearrange("p t d -> p (t d)"), ALU.add))
                own.wait()
                layer_norm(b, 2, x2, hat3)
                for i in range(2):
                    dve.wait_ge(k["f_proj"], 5 * b + 2 * i + 2)
                    dve.scalar_tensor_tensor(rope_t[:, 2 * i, :], bank[2 + 2 * i][:], cols[:, ROW_FBQ + i:ROW_FBQ + i + 1],
                                             cos[:], ALU.add, ALU.mult).then_inc(k["f_rope"], 1)
                    dve.scalar_tensor_tensor(rope_t[:, 2 * i + 1, :], bank[3 + 2 * i][:], cols[:, COL_FBQR + i:COL_FBQR + i + 1],
                                             sin[:], ALU.add, ALU.mult).then_inc(k["f_rope"], 1)
                    dve.wait_ge(k["f_rope"], 2 * (2 * b + i + 1))
                    dve.tensor_tensor(rope_f[:, i, :], rope_t[:, 2 * i, :], rope_t[:, 2 * i + 1, :], ALU.add).then_inc(k["f_full"], 1)
                    dve.wait_ge(k["f_full"], 2 * b + i + 1)
                for i, hi, lo in ((0, qhi, qlo), (1, khi, klo)):
                    dve.wait_ge(k["f_hi"], 2 * b + i + 1)
                    dve.tensor_tensor(lo[:], rope_f[:, i, :], hi[:], ALU.subtract).then_inc(k["f_lo"], 1)
                dve.wait_ge(k["f_st_mm"], 2 * G * b + 1)
                dve.tensor_copy(qst[:, 0, :], bank[ST_BANKS[0]][:]).then_inc(k["f_qst0"], 1)

                def row_maxima(g, t):
                    for hh in range(HG):
                        dve.wait_ge(k["f_s1"], H * T * b + (g * T + t) * HG + hh + 1)
                        dve.tensor_reduce(nm[:, t, g, BLK * hh:BLK * hh + 1], bank[s1_bank(g, t, hh)][:],
                                          AX.X, ALU.max, negate=True).then_inc(k["f_max"], 1)

                for t in range(T):
                    row_maxima(0, t)
                row_maxima(1, 0)
                row_maxima(1, 1)
                dve.wait_ge(k["f_proj"], 5 * b + 5)
                dve.tensor_tensor(vf[:].rearrange("p t h c -> p (t h) c")[:, :, 0:DH],
                                  bank[3][:].rearrange("p (n d) -> p n d", d=DH),
                                  vecs[:, VEC_FBV, :].unsqueeze(1).to_broadcast([P, T, D]).rearrange("p t (h d) -> p t h d", d=DH),
                                  ALU.add).then_inc(k["f_v"], 1)
                for g in range(1, G):
                    for t in range(2 if g == 1 else 1, T):
                        row_maxima(g, t)
                    if g + 1 < G:
                        row_maxima(g + 1, 0)
                normalise_heads(b, 1)
                dve.wait_ge(k["hat3b_ready"], b + 1)
                dve.wait_ge(k["o_proj"], 2 * b + 2)
                own.inc(dve.tensor_tensor(r1[:].rearrange("p t d -> p (t d)"), bank[1][:],
                                          hat3b[:].rearrange("p t d -> p (t d)"), ALU.add))
                own.wait()
                layer_norm(b, 3, r1, hat)
                dve.wait_ge(k["ln_T"], LN * b + LN)
                dve.tensor_tensor(x1lo[:], x1T[:], x1hi[:], ALU.subtract).then_inc(k["x1_split"], 1)

                def split_h(j):
                    dve.wait_ge(k["h_act"], NJ * b + j + 1)
                    if j >= 2:
                        dve.wait_ge(k["y_part"], NJ * b + j - 1)
                    on_act = len([i for i in HI_ON_ACT if i <= j])
                    if j in HI_ON_ACT:
                        dve.wait_ge(k["h_hi_act"], len(HI_ON_ACT) * b + on_act)
                    else:
                        dve.tensor_copy(hhi[:, j % 2, :], hT[:, j % 2, :]).then_inc(k["h_hi"], 1)
                        dve.wait_ge(k["h_hi"], (NJ - len(HI_ON_ACT)) * b + j + 1 - on_act)
                    dve.tensor_tensor(hlo[j % 2][:], hT[:, j % 2, :], hhi[:, j % 2, :], ALU.subtract).then_inc(k["h_lo"], 1)

                def scale_expert(e):
                    dve.wait_ge(k["y_part"], NJ * b + FC * (e + 1))
                    if e == 0:
                        dve.wait_ge(k["comb_loaded"], 16 * b + 16)
                    if e >= 2:
                        dve.wait_ge(k["rT_added"], (NE - 1) * b + e - 1)
                    dve.tensor_tensor(ys[e % 2], bank[Y_BANKS[e % len(Y_BANKS)]][:], combB[:, e, :],
                                      ALU.mult).then_inc(k["y_scaled"], 1)

                flat = lambda i: gt[:, i]
                per_token = lambda i: gs[:, i, :].unsqueeze(2).to_broadcast([P, T, NE])
                dve.wait_ge(k["g_logits"], b + 1)
                own.inc(dve.tensor_tensor(flat(2), bank[1][:, 0:T * NE].rearrange("p (t e) -> p t e", e=NE),
                                          bg[:].unsqueeze(1).to_broadcast([P, T, NE]), ALU.add))
                own.wait()
                own.inc(dve.reduce_max(gs[:, 0, :], flat(2), AX.X))
                own.wait()
                dve.tensor_tensor(flat(0), flat(2), per_token(0), ALU.subtract).then_inc(k["g_shift"], 1)
                split_h(0)
                dve.wait_ge(k["g_exp"], b + 1)
                left = 1
                for i in range(2):
                    m, r, eq, hit = 1 + 2 * i, 2 + 2 * i, 3 + 3 * i, 4 + 3 * i
                    own.inc(dve.reduce_max(gs[:, m, :], flat(left), AX.X))
                    own.wait()
                    own.inc(dve.tensor_tensor(flat(eq), flat(left), per_token(m), ALU.is_equal))
                    split_h(3 * i + 1)
                    own.wait()
                    own.inc(dve.tensor_tensor(flat(5 + i * 4), flat(eq), rank, ALU.mult))
                    own.wait()
                    own.inc(dve.reduce_max(gs[:, r, :], flat(5 + i * 4), AX.X))
                    split_h(3 * i + 2)
                    own.wait()
                    own.inc(dve.tensor_tensor(flat(hit), flat(5 + i * 4), per_token(r), ALU.is_equal))
                    split_h(3 * i + 3)
                    own.wait()
                    if i == 0:
                        own.inc(dve.scalar_tensor_tensor(flat(8), flat(hit), -4.0, flat(1), ALU.mult, ALU.add))
                        own.wait()
                        left = 8
                own.inc(dve.tensor_tensor(flat(2), flat(4), flat(7), ALU.add))
                own.inc(dve.tensor_tensor(gs[:, 5, :], gs[:, 1, :], gs[:, 3, :], ALU.add))
                own.wait()
                own.inc(dve.tensor_tensor(flat(3), flat(2), flat(1), ALU.mult))
                own.inc(dve.reciprocal(gs[:, 6, :], gs[:, 5, :]))
                own.wait()
                dve.tensor_tensor(comb[:], flat(3), per_token(6), ALU.mult).then_inc(k["g_comb"], 1)
                for j in range(7, NJ):
                    split_h(j)
                    if j == COMB_AT + 4:
                        dve.wait_ge(k["b2_mm"], b + 1)
                        dve.tensor_tensor(rT[:], bank[1][:], x1T[:], ALU.add).then_inc(k["rT_begun"], 1)
                    if j in SCALE_AT:
                        scale_expert(SCALE_AT.index(j))
                    if j in FRONT_STATS_AT and not last:
                        front_stats(b + 1, FRONT_STATS_AT.index(j))
                    if j == FRONT_MOMENTS_AT and not last:
                        front_moments(b + 1)
                    if j == FRONT_ROWS_AT and not last:
                        front_rows(b + 1)
                scale_expert(NE - 1)
                if not last:
                    front_queries(b + 1)
                dve.wait_ge(k["r_turned"], b + 1)
                end_rows = bank[3][:].rearrange("p (t d) -> p t d", t=T)
                ln_stats(own, k["end_var"], end_rows)
                if not last:
                    front_maxima(b + 1)
                dve.wait_ge(k["end_rstd"], b + 1)
                ln_rows(end_rows, r1, k["end_hat"])
                dve.wait_ge(k["end_hat"], T * (b + 1) + 1)
                own.inc(dve.tensor_tensor(outb[:], r1[:], bc(VEC_G2), ALU.mult))
                own.wait()
                dve.wait_ge(k["x2b_ready"], b + 1)
                dve.tensor_tensor(outb[:], outb[:], x2b[:], ALU.add).then_inc(k["out_ready"], 1)
                assert own.n == DVE_STEPS, own.n

            for t in range(T):
                front_stats(0, t)
            front_moments(0)
            front_rows(0)
            front_queries(0)
            front_maxima(0)
            dve.wait_ge(k["loaded"], 16 * N_LOADS)
            for dst, src in ((sel_r, sel), (rep_b, rep[:])):
                dve.tensor_copy(dst[:], src).then_inc(k["casts"], 1)
            half = DH // 2
            for i in range(2):
                src = wf[:, i, :].rearrange("p (h d) -> p h d", d=DH)
                dst = wfr[:, i, :].rearrange("p (h d) -> p h d", d=DH)
                dve.tensor_scalar(dst[:, :, 0:half], src[:, :, half:DH], -1.0, None, ALU.mult).then_inc(k["casts"], 1)
                dve.tensor_copy(dst[:, :, half:DH], src[:, :, 0:half]).then_inc(k["casts"], 1)
            dve.wait_ge(k["rows_turned"], 1)
            dve.tensor_copy(cols[:, 0:NROWS], bank[1][:, 0:NROWS]).then_inc(k["bias_cols"], 1)
            dve.wait_ge(k["rot_cols"], 1)
            dve.wait_ge(k["zeroed"], 8)
            for hh in range(HG):
                p0 = BLK * hh
                dve.memset(vxt[p0:p0 + KT0, :, p0 + DH:p0 + DH + 1], 1.0).then_inc(k["casts"], 1)
            dve.wait_ge(k["casts"], 13)
            dve.tensor_copy(cols[:, COL_FBQR:COL_FBKR + 1], bank[2][:, 0:2]).then_inc(k["setup_done"], 1)
            dve.wait_ge(k["setup_done"], 1)

            with dve.Fori(0, B - 1) as b:
                batch(b, False)
            batch(B - 1, True)

        @block.tensor
        def _(pe):
            pe.wait_ge(k["front_loaded"], 16 * N_FRONT_LOADS)

            def keep_warm(n, i):
                for _ in range(n):
                    pe.matmul(bank[i][:], eye_r[:], sel_r[:, 0].rearrange("p g q -> p (g q)"), start=True, stop=True)

            def turn_rows(b, n, src, wait=True):
                for t in range(T):
                    pe.wait_ge(k["ln_hat"], T * (b * LN + n) + t + 1)
                    ins = pe.transpose(bank[0][:, t * P:(t + 1) * P], src[:, t, :], eye[:])
                ins.then_inc(k["ln_turned"], 1)
                if wait:
                    pe.wait_ge(k["ln_T"], b * LN + n + 1)

            def attention_out(b, n, wo):
                for t in range(T):
                    for g in range(G):
                        ins = pe.transpose(bank[4 + t][:, g * P:(g + 1) * P], ot[:, g, t * P:(t + 1) * P], eye[:])
                    ins.then_inc(k["o_turned"], 1)
                for t in range(T):
                    pe.wait_ge(k["on_ready"], T * (2 * b + n) + t + 1)
                    ins = pe.transpose(bank[0][:, t * P:(t + 1) * P], on[:, t, :], eye[:])
                ins.then_inc(k["on_turned"], 1)
                pe.wait_ge(k["onT_ready"], 2 * b + n + 1)
                for t in range(T):
                    ins = pe.matmul(bank[1][:, t * D:(t + 1) * D], onT[:, t * P:(t + 1) * P], wo, start=True, stop=True)
                ins.then_inc(k["o_proj"], 1)

            def blk(hh):
                return slice(BLK * hh, BLK * (hh + 1))

            def front_turn(b):
                turn_rows(b, 0, hat, wait=False)

            def front_keys_queries(b):
                pe.wait_ge(k["ln_T"], b * LN + 1)
                pe.matmul(bank[1][:], wa[:, 0, :], hatT[:], start=True, stop=True).then_inc(k["a_proj"], 1)
                pe.matmul(bank[2][:], wa[:, 1, :], hatT[:], start=True, stop=True).then_inc(k["a_proj"], 1)

            def front_values(b):
                for t in range(T):
                    ins = pe.matmul(bank[0][:, t * D:(t + 1) * D], hatT[:, t * P:(t + 1) * P], wa[:, 2, :], start=True, stop=True)
                ins.then_inc(k["a_proj"], 1)

            def front_scores(b):
                pe.wait_ge(k["a_k"], b + 1)
                pe.wait_ge(k["a_q"], b + 1)
                for t in range(T):
                    n = (t + 1) * P
                    pe.matmul(bank[4 + t][:, 0:n], qTa[:, t * P:(t + 1) * P], kTa[:, 0:n], start=True, stop=True)
                    pe.matmul(bank[4 + t][:, t * P:n], eye_b[:], tri_b[:], start=False, stop=True,
                              skip_group_check=True).then_inc(k["a_scores"], 1)

            def batch(b, last):
                pe.wait_ge(k["a_v"], b + 1)
                for t in range(T):
                    pe.wait_ge(k["a_probs"], T * b + t + 1)
                    if t == 3:
                        pe.wait_ge(k["end_hat"], T * b + 1)
                    for c in range(t + 1):
                        ins = pe.transpose(bank[t][:, c * P:(c + 1) * P], pa[:, t, c * P:(c + 1) * P], eye[:])
                    ins.then_inc(k["a_turned"], 1)
                for t in range(T):
                    pe.wait_ge(k["a_probsT"], T * b + t + 1)
                    for c in range(t + 1):
                        ins = pe.matmul(bank[4][:, t * D:(t + 1) * D], pTa[:, t, c * P:(c + 1) * P], va[:, c, :],
                                        start=(c == 0), stop=(c == t))
                ins.then_inc(k["a_out"], 1)

                pe.wait_ge(k["ctx_loaded"], 32 * b + 32)
                pe.transpose(bank[5][:, 0:P], ctx[:, 0, :], eye[:])
                pe.transpose(bank[5][:, P:KC], ctx[0:KT0, 1, :], eye[0:KT0, 0:KT0]).then_inc(k["c_turned"], 1)
                pe.wait_ge(k["mb_ready"], b + 1)
                for t in range(T):
                    pe.transpose(bank[6][:].bitcast(BF16)[:, t * P:(t + 1) * P], mb[:, t, 0:P], eye_b[:])
                    ins = pe.transpose(bank[7][0:KT0, :].bitcast(BF16)[:, t * P:(t + 1) * P], mb[:, t, P:KC], eye_b[:])
                ins.then_inc(k["m_turned"], 1)
                pe.wait_ge(k["ctxT_ready"], b + 1)
                pe.matmul(bank[1][:, 0:KC], wx[:, 1, :], ctxT[:], start=True, stop=True).then_inc(k["x_proj"], 1)
                pe.matmul(bank[2][:, 0:D], ctxT[:, 0:P], wx[:, 2, :], start=True, stop=True).then_inc(k["x_proj"], 1)
                for hh in range(HG):
                    ins = pe.matmul(bank[3][BLK * hh:BLK * hh + KT0, 0:G * DH], ctxT[:, P:KC],
                                    wx[:, 2, :].rearrange("p (g c) -> p g c", g=G)[:, :, hh * DH:(hh + 1) * DH],
                                    start=True, stop=True)
                ins.then_inc(k["x_proj"], 1)
                pe.wait_ge(k["x_klo"], b + 1)
                pe.wait_ge(k["mT_ready"], b + 1)
                for g in range(G):
                    dst = bank[5 + g // 2][:, (g % 2) * KC:(g % 2 + 1) * KC]
                    pe.matmul(dst, sel_r[:, 2, g, :], khi[:, 0:KC], start=True, stop=False)
                    ins = pe.matmul(dst, sel_r[:, 3, g, :], klo[:, 0:KC], start=False, stop=True)
                    if g % 2:
                        ins.then_inc(k["x_kst_mm"], 1)
                keep_warm(WARM_LN1, 7)
                turn_rows(b, 1, hat)
                pe.matmul(bank[4][:], wx[:, 0, :], hatT[:], start=True, stop=True).then_inc(k["x_qproj"], 1)

                def x_mask(t, i):
                    pe.matmul(bank[i][:, 0:2 * KC], eye_b[:], mb[:, t, :].unsqueeze(1).to_broadcast([P, 2, KC]),
                              start=True, stop=True, skip_group_check=True)

                pe.wait_ge(k["x_kst"], 2 * b + 2)
                for i in (3, 5, 6):
                    x_mask(0, i)
                keep_warm(3, 7)
                pe.wait_ge(k["x_qlo"], b + 1)
                for g in range(G):
                    dst = bank[g if g < 3 else 7][:]
                    pe.matmul(dst, sel_r[:, 0, g, :], qhi[:], start=True, stop=False)
                    pe.matmul(dst, sel_r[:, 1, g, :], qlo[:], start=False, stop=True).then_inc(k["x_qst_mm"], 1)
                keep_warm(2, 4)
                x_mask(0, 4)
                pe.wait_ge(k["x_qst"], G * b + G)
                for i in (0, 1, 2, 7):
                    x_mask(0, i)
                pe.wait_ge(k["x_ktail"], HG * b + HG)
                for t in range(T):
                    for hh in range(HG):
                        if t:
                            pe.wait_ge(k["x_max"], H * b + HG * (t - 1) + hh + 1)
                            x_mask(t, 2 * hh)
                            x_mask(t, 2 * hh + 1)
                        for g in range(G):
                            ins = pe.matmul(bank[2 * hh + g // 2][:, (g % 2) * KC:(g % 2 + 1) * KC],
                                            qst[blk(hh), g, t * P:(t + 1) * P], kst[blk(hh), g, 0:KC],
                                            start=False, stop=True, skip_group_check=True)
                        ins.then_inc(k["x_s1"], 1)
                for g in range(G):
                    if g % 2 == 0:
                        pe.wait_ge(k["x_max"], H * b + H - HG + g // 2 + 1)
                    pe.matmul(bank[g][:], sel_r[:, 0, g, :], qhi[:], start=True, stop=False, skip_group_check=True)
                    pe.matmul(bank[g][:], sel_r[:, 1, g, :], qlo[:], start=False, stop=False, skip_group_check=True)
                pe.wait_ge(k["x_max"], H * b + H)
                for g in range(G):
                    for t in range(T):
                        ins = pe.matmul(bank[g][:, t * P:(t + 1) * P], nm[:, t, g, :], eye_r[:], start=False,
                                        stop=(t == T - 1), skip_group_check=True)
                    ins.then_inc(k["x_q2_mm"], 1)

                def x_sums(g):
                    acc = bank[1 + 2 * (g % 2)]
                    pe.wait_ge(k["x_exp"], H * b + HG * (g + 1))
                    pe.wait_ge(k["x_expt"], G * b + g + 1)
                    if g >= 2:
                        pe.wait_ge(k["ot_ready"], G * b + g - 1)
                    for hh in range(HG):
                        pe.matmul(acc[blk(hh), :], vx[:, HG * g + hh, :], px[:, g % 2, hh, :], start=True,
                                  stop=False, skip_group_check=True)
                    pe.matmul(acc[:], vxt[:, g, :], pxt[:, g % 2, :], start=False, stop=True,
                              skip_group_check=True).then_inc(k["x_av"], 1)

                for g in range(G):
                    pe.wait_ge(k["x_q2"], G * b + g + 1)
                    for hh in range(HG):
                        if g:
                            pe.wait_ge(k["x_exp"], H * b + HG * (g - 1) + hh + 1)
                        pe.matmul(bank[4 + hh][:], eye_b[:], mT[:], start=True, stop=False, skip_group_check=True)
                        pe.matmul(bank[4 + hh][:], kst[blk(hh), g, 0:P], q2st[blk(hh), g, :], start=False,
                                  stop=True, skip_group_check=True).then_inc(k["x_s2"], 1)
                    if g >= 2:
                        pe.wait_ge(k["x_expt"], G * b + g - 1)
                    if g == 1:
                        pe.wait_ge(k["x_q2"], G * b + 3)
                    tail = bank[2 * (g % 2)]
                    pe.matmul(tail[:], rep_b[0:BLK, :], mTt[:], start=True, stop=False, skip_group_check=True)
                    pe.matmul(tail[:], ktail[:, g, :], q2st[:, g, :], start=False, stop=True,
                              skip_group_check=True).then_inc(k["x_st"], 1)
                    if g == 2:
                        pe.wait_ge(k["x_q2"], G * b + 4)
                    if g:
                        x_sums(g - 1)
                x_sums(G - 1)
                pe.wait_ge(k["ot_ready"], G * b + G)
                attention_out(b, 0, wx[:, 3, :])

                keep_warm(WARM_LN2, 3)
                turn_rows(b, 2, hat3)
                for i in range(2):
                    pe.matmul(bank[2 + 2 * i][:], wf[:, i, :], hatT[:], start=True, stop=True).then_inc(k["f_proj"], 1)
                    pe.matmul(bank[3 + 2 * i][:], wfr[:, i, :], hatT[:], start=True, stop=True).then_inc(k["f_proj"], 1)

                def stack_part(g, i):
                    if g == 3 and i == 0:
                        pe.wait_ge(k["f_st"], (2 * G - 1) * b + 3)
                    ins = pe.matmul(bank[ST_BANKS[2 * g + i // 2]][:], sel_r[:, i, g, :], (qhi, qlo, khi, klo)[i][:],
                                    start=(i % 2 == 0), stop=(i % 2 == 1))
                    if i % 2:
                        ins.then_inc(k["f_st_mm"], 1)

                def wait_slot(c):
                    if c >= RING:
                        step = RING_ORDER[c - RING]
                        if len(step) == 1:
                            pe.wait_ge(k["f_q2"], G * b + step[0] + 1)
                        else:
                            g, t, hh = step
                            pe.wait_ge(k["f_max"], H * T * b + (g * T + t) * HG + hh + 1)

                def s1(g, t, hh):
                    wait_slot(RING_ORDER.index((g, t, hh)))
                    if g and hh == 0:
                        keep_warm(1, s1_bank(g, t, hh))
                    pe.matmul(bank[s1_bank(g, t, hh)][:], qst[blk(hh), g, t * P:(t + 1) * P], kst[blk(hh), g, :],
                              start=True, stop=True).then_inc(k["f_s1"], 1)

                def q2(g):
                    wait_slot(RING_ORDER.index((g,)))
                    pe.wait_ge(k["f_max"], H * T * b + (g + 1) * H)
                    dst = bank[q2_bank(g)]
                    pe.matmul(dst[:], sel_r[:, 0, g, :], qhi[:], start=True, stop=False, skip_group_check=True)
                    pe.matmul(dst[:], sel_r[:, 1, g, :], qlo[:], start=False, stop=False, skip_group_check=True)
                    for t in range(T):
                        ins = pe.matmul(dst[:, t * P:(t + 1) * P], nm[:, t, g, :], eye_r[:], start=False,
                                        stop=(t == T - 1), skip_group_check=True)
                    ins.then_inc(k["f_q2_mm"], 1)

                def s2(g, c, i):
                    n = (g * T + c) * 2 + i
                    if n >= 2:
                        pe.wait_ge(k["f_exp"], H * T * b + 2 * (n - 1))
                    for q in range(2):
                        hh = 2 * i + q
                        ins = pe.matmul(bank[4 + hh][:], kst[blk(hh), g, c * P:(c + 1) * P], q2st[blk(hh), g, :],
                                        start=True, stop=True)
                    ins.then_inc(k["f_s2"], 1)

                def sums_of(n):
                    g, c = divmod(n, T)
                    pe.wait_ge(k["f_exp"], H * T * b + (n + 1) * HG)
                    if c == 0 and g:
                        pe.wait_ge(k["f_ot"], G * b + g)
                    for hh in range(HG):
                        ins = pe.matmul(bank[3][blk(hh), :], vf[:, c, HG * g + hh, :], px[:, c % 2, hh, :],
                                        start=(c == 0), stop=(c == T - 1), skip_group_check=True)
                    ins.then_inc(k["f_av"], 1)

                keep_warm(WARM_ROPE, 6)
                pe.wait_ge(k["f_lo"], 2 * b + 2)
                for i in range(4):
                    stack_part(0, i)
                keep_warm(2, 3)
                pe.wait_ge(k["f_st"], (2 * G - 1) * b + 1)
                pe.wait_ge(k["f_qst0"], b + 1)
                for t in range(T):
                    for hh in range(HG):
                        s1(0, t, hh)
                        if t in (1, 2):
                            stack_part(t, hh)
                        else:
                            keep_warm(1, 3)
                pe.wait_ge(k["f_st"], (2 * G - 1) * b + 3)
                s1(1, 0, 0)
                s1(1, 0, 1)
                q2(0)
                s1(1, 0, 2)
                s1(1, 0, 3)
                for i in range(4):
                    stack_part(3, i)
                pe.wait_ge(k["f_st"], (2 * G - 1) * b + 5)
                for g in range(G):
                    pe.wait_ge(k["f_q2"], G * b + g + 1)
                    for c in range(T):
                        ga, ta = divmod((g + 1) * T + c + 1, T)
                        for i in range(2):
                            if i and g * T + c == 0:
                                pe.wait_ge(k["f_st"], (2 * G - 1) * (b + 1))
                            s2(g, c, i)
                            if ga < G:
                                s1(ga, ta, 2 * i)
                            if i:
                                if g * T + c == 1:
                                    pe.wait_ge(k["f_v"], b + 1)
                                if g * T + c:
                                    sums_of(g * T + c - 1)
                            if ga < G:
                                s1(ga, ta, 2 * i + 1)
                            if c == T - 1 and i == 0 and g + 1 < G:
                                q2(g + 1)
                            if g * T + c == 0:
                                for t in (2 * i, 2 * i + 1):
                                    ins = pe.matmul(bank[3][:, t * D:(t + 1) * D], hatT[:, t * P:(t + 1) * P],
                                                    wf[:, 2, :], start=True, stop=True)
                                if i:
                                    ins.then_inc(k["f_proj"], 1)
                sums_of(G * T - 1)
                pe.wait_ge(k["f_ot"], G * b + G)
                attention_out(b, 1, wf[:, 3, :])

                keep_warm(WARM_LN3, 3)
                turn_rows(b, 3, hat, wait=False)
                keep_warm(4, 3)
                pe.wait_ge(k["ln_T"], (b + 1) * LN)

                def up(j):
                    e, c = divmod(j, FC)
                    if j >= 2:
                        pe.wait_ge(k["h_act"], NJ * b + j - 1)
                    if j - 2 in HI_ON_ACT:
                        pe.wait_ge(k["h_hi_act"], len(HI_ON_ACT) * b + HI_ON_ACT.index(j - 2) + 1)
                    if c == 0:
                        pe.wait_ge(k["w_lo"], 2 * (NE * b + e) + 1)
                    hi, lo = (wsp[0][:, i, e % 2, c * P:(c + 1) * P] for i in range(2))
                    dst = bank[4 + j % 2][:]
                    pe.matmul(dst, hi, x1hi[:], start=True, stop=False)
                    pe.matmul(dst, lo, x1hi[:], start=False, stop=False)
                    if j == 0:
                        pe.wait_ge(k["x1_split"], b + 1)
                    pe.matmul(dst, hi, x1lo[:], start=False, stop=True).then_inc(k["h_ready"], 1)

                def down(j):
                    e, c = divmod(j, FC)
                    if c == 0:
                        pe.wait_ge(k["w_lo"], 2 * (NE * b + e) + 2)
                        if e == 4:
                            pe.wait_ge(k["rT_begun"], b + 1)
                        if e >= len(Y_BANKS):
                            pe.wait_ge(k["y_scaled"], NE * b + e - len(Y_BANKS) + 1)
                    pe.wait_ge(k["h_lo"], NJ * b + j + 1)
                    hi, lo = (wsp[1][:, i, e % 2, c * P:(c + 1) * P] for i in range(2))
                    dst = bank[Y_BANKS[e % len(Y_BANKS)]][:]
                    pe.matmul(dst, hi, hhi[:, j % 2, :], start=(c == 0), stop=False)
                    pe.matmul(dst, lo, hhi[:, j % 2, :], start=False, stop=False)
                    pe.matmul(dst, hi, hlo[j % 2][:], start=False, stop=(c == FC - 1)).then_inc(k["y_part"], 1)

                for t in range(T):
                    ins = pe.matmul(bank[1][:, t * NE:(t + 1) * NE], x1T[:, t * P:(t + 1) * P], wg[:], start=True, stop=True)
                ins.then_inc(k["g_logits"], 1)
                for j in range(NJ + 2):
                    if j < NJ:
                        up(j)
                    if j == 1:
                        keep_warm(WARM_GELU, 3)
                    if j == NJ and not last:
                        front_turn(b + 1)
                    if j == NJ + 1 and not last:
                        front_keys_queries(b + 1)
                    if j >= 2:
                        down(j - 2)
                    if j == COMB_AT:
                        pe.wait_ge(k["g_comb"], b + 1)
                        for t in range(T):
                            ins = pe.transpose(bank[0][0:NE, t * P:(t + 1) * P], comb[:, t, :], eye[:])
                        ins.then_inc(k["g_turned"], 1)
                    if j == COMB_AT + 3:
                        pe.wait_ge(k["combT_ready"], b + 1)
                        pe.matmul(bank[1][:], b2[:], combT[:], start=True, stop=True).then_inc(k["b2_mm"], 1)
                if not last:
                    front_values(b + 1)
                pe.wait_ge(k["rT_added"], (NE - 1) * (b + 1))
                for t in range(T):
                    pe.matmul(bank[3][:, t * P:(t + 1) * P], rT[:, t * P:(t + 1) * P], eye[:], start=(t == 0),
                              stop=False, skip_group_check=True)
                pe.wait_ge(k["y_scaled"], NE * (b + 1))
                for t in range(T):
                    ins = pe.matmul(bank[3][:, t * P:(t + 1) * P], ys[(NE - 1) % 2][:, t * P:(t + 1) * P], eye[:],
                                    start=False, stop=True, skip_group_check=True)
                ins.then_inc(k["r_turned"], 1)
                if not last:
                    front_scores(b + 1)

            front_turn(0)
            front_keys_queries(0)
            front_values(0)
            pe.wait_ge(k["casts"], 3)
            front_scores(0)
            pe.wait_ge(k["loaded"], 16 * N_LOADS)
            pe.transpose(bank[1][:, 0:NROWS], rows[:], eye[0:NROWS, 0:NROWS]).then_inc(k["rows_turned"], 1)
            pe.wait_ge(k["bias_cols"], 1)
            for i in range(2):
                ins = pe.matmul(bank[2][:, i:i + 1], rot[:], cols[:, ROW_FBQ + i:ROW_FBQ + i + 1], start=True, stop=True)
            ins.then_inc(k["rot_cols"], 1)
            pe.wait_ge(k["setup_done"], 1)

            with pe.Fori(0, B - 1) as b:
                batch(b, False)
            batch(B - 1, True)


HI_ON_ACT = (7, 8, 19, 20, 23, 24, 27, 28, 30, 31)
WARM_LN1, WARM_LN2, WARM_LN3 = 14, 14, 14
WARM_GELU = 5
WARM_ROPE = 16
FRONT_STATS_AT, FRONT_MOMENTS_AT, FRONT_ROWS_AT = (10, 11, 12, 14), 15, 17
COMB_AT = 9
SCALE_AT = (18, 19, 20, 21, 23, 26, 30)
RING = 3
N_FRONT_LOADS = 6
N_LOADS = 16 + 6 + 7
ACT_STEPS = 1
DVE_STEPS = 69
FRONT_STEPS = 14


RING_ORDER = [(0, t, hh) for t in range(T) for hh in range(HG)]
for _g in range(G):
    _next = [(_g + 1, t, hh) for t in range(T) for hh in range(HG) if _g + 1 < G]
    RING_ORDER += _next[:2] + [(_g,)] + _next[2:]
ST_BANKS = (4, 5, 6, 7, 4, 5, 6, 7)


def s1_bank(g, t, hh):
    return RING_ORDER.index((g, t, hh)) % RING


def q2_bank(g):
    return RING_ORDER.index((g,)) % RING


_WEIGHTS = [
    "L0_attn_Wk", "L0_attn_Wq", "L0_attn_Wv", "L0_xattn_wq", "L0_xattn_bq", "L0_xattn_wk", "L0_xattn_bk",
    "L0_xattn_wv", "L0_xattn_bv", "L0_xattn_wo", "L0_xattn_bo", "L0_ffn_Wq", "L0_ffn_bq", "L0_ffn_Wk",
    "L0_ffn_bk", "L0_ffn_Wv", "L0_ffn_bv", "L0_ffn_Wo", "L0_ffn_bo", "L0_ffn_Wg", "L0_ffn_bg", "L0_ffn_W1",
    "L0_ffn_b1", "L0_ffn_W2", "L0_ffn_b2", "L0_ffn_g1", "L0_ffn_be1", "L0_ffn_g2", "L0_ffn_be2",
]


def kernel(**inputs):
    import concourse.bacc as _bacc
    from concourse import mybir as _mybir
    from concourse.bass_utils import run_bass_kernel_spmd as _run

    nc = _bacc.Bacc("TRN2", target_bir_lowering=False, num_devices=1)
    arrays = {}

    def given(name, a):
        a = np.ascontiguousarray(a)
        arrays[f"in_{name}"] = a
        return nc.dram_tensor(f"in_{name}", a.shape, _mybir.dt.from_np(a.dtype), kind="ExternalInput").ap()

    x = given("x", inputs["x"])
    ctx = given("ctx_1024", inputs["ctx_1024"])
    mask = given("mask", inputs["mask_Bx1xSxS2_ik1"])
    w = {n: given(n, inputs[n]) for n in _WEIGHTS}
    consts = {n: given(f"const_{n}", a) for n, a in shape_constants().items()}
    comb = nc.dram_tensor("gate_weights", (NE, S), F32, kind="Internal").ap()
    out = nc.dram_tensor("out_0", (B, S, D), F32, kind="ExternalOutput").ap()
    build(nc, x, ctx, mask, w, consts, comb, out)
    r = _run(nc, [arrays], core_ids=[0])
    return r.results[0]["out_0"]
```
